# Optimizing a Trainium2 kernel written in Bass

```python
import numpy as np
import jax
import jax.numpy as jnp

def _softmax(x, axis=-1):
    return jax.nn.softmax(x, axis=axis)

def _gelu(x):
    return jax.nn.gelu(x, approximate=True)

def _silu(x):
    return jax.nn.silu(x)

def _sigmoid(x):
    return jax.nn.sigmoid(x)

def _layernorm(x, axis=-1, eps=1e-05):
    m = jnp.mean(x, axis=axis, keepdims=True)
    v = jnp.var(x, axis=axis, keepdims=True)
    return (x - m) / jnp.sqrt(v + eps)

def _scatter_add(tgt, idx, src, axis=0):
    return tgt.at[idx].add(src)

def _segment_sum(src, seg, n):
    return jax.ops.segment_sum(src, seg, n)
kernel_name = 'mk_adaln_d1_jaxref_r4_2aa36d'

def setup_inputs(seed: int=0):
    np.random.seed(seed)
    _w = jnp.asarray

    def _L0_attn_setup():
        import jax, jax.numpy as jnp
        import numpy as np
        D_MODEL = 256
        N_HEADS = 16
        HEAD_D = D_MODEL // N_HEADS
        B, T = (4, 1024)
        ROPE_BASE = 10000.0

        def _rope(x):
            Bx, Tx, Dx = x.shape
            half = Dx // 2
            inv_freq = 1.0 / ROPE_BASE ** (jnp.arange(half, dtype=jnp.float32) / half)
            ang = jnp.arange(Tx, dtype=jnp.float32)[:, None] * inv_freq[None, :]
            cos, sin = (jnp.cos(ang), jnp.sin(ang))
            x1 = x[..., 0::2]
            x2 = x[..., 1::2]
            r1 = x1 * cos - x2 * sin
            r2 = x1 * sin + x2 * cos
            out = jnp.stack([r1, r2], axis=-1).reshape(Bx, Tx, Dx)
            return out
        key = jax.random.key(seed)
        k_x, k_q, k_k, k_v = jax.random.split(key, 4)
        x = jax.random.normal(k_x, (B, T, D_MODEL), dtype=jnp.float32)
        bound = np.sqrt(6.0 / (HEAD_D * N_HEADS))
        shp = (HEAD_D, HEAD_D, N_HEADS)
        w_q = jax.random.uniform(k_q, shp, jnp.float32, -bound, bound)
        w_k = jax.random.uniform(k_k, shp, jnp.float32, -bound, bound)
        w_v = jax.random.uniform(k_v, shp, jnp.float32, -bound, bound)
        return {'x': x, 'w_q': w_q, 'w_k': w_k, 'w_v': w_v}
    _L0_attn_in = _L0_attn_setup()

    def _L0_ffn_setup():
        import jax, jax.numpy as jnp
        import numpy as np
        DIM = 256
        DEPTH = 2
        HEADS = 8
        DIM_HEAD = 64
        WINDOW = 128
        INNER = HEADS * DIM_HEAD
        HID = int(DIM * 4 * 2 / 3)
        B, N = (2, 2048)
        QK_SCALE = 8.0

        def shift_token(t):
            t1, t2 = jnp.split(t, 2, axis=-1)
            t2 = jnp.pad(t2, ((0, 0), (1, 0), (0, 0)))[:, :-1]
            return jnp.concatenate([t1, t2], axis=-1)

        def l2norm(t):
            return t / jnp.clip(jnp.linalg.norm(t, axis=-1, keepdims=True), 1e-12)

        def rotate_half(x):
            x1, x2 = jnp.split(x, 2, axis=-1)
            return jnp.concatenate([-x2, x1], axis=-1)

        def rotary_xpos(q, k):
            n = q.shape[-2]
            half_idx = jnp.arange(0, DIM_HEAD, 2, dtype=jnp.float32)
            inv_freq = 1.0 / 10000.0 ** (half_idx / DIM_HEAD)
            t = jnp.arange(n, dtype=jnp.float32)
            freqs = t[:, None] * inv_freq[None, :]
            freqs = jnp.concatenate([freqs, freqs], axis=-1)
            base = (half_idx + 0.4 * DIM_HEAD) / (1.4 * DIM_HEAD)
            power = (t - n // 2) / float(WINDOW // 2)
            scale = base[None, :] ** power[:, None]
            scale = jnp.concatenate([scale, scale], axis=-1)
            cos, sin = (jnp.cos(freqs), jnp.sin(freqs))
            q = q * cos * scale + rotate_half(q) * sin * scale
            k = k * cos / scale + rotate_half(k) * sin / scale
            return (q, k)

        def local_attention(q, k, v):
            b, h, n, d = q.shape
            w = n // WINDOW
            bq = q.reshape(b, h, w, WINDOW, d) * QK_SCALE
            bk = k.reshape(b, h, w, WINDOW, d)
            bv = v.reshape(b, h, w, WINDOW, d)

            def look_around(t):
                p = jnp.pad(t, ((0, 0), (0, 0), (1, 0), (0, 0), (0, 0)))
                return jnp.concatenate([p[:, :, :w], p[:, :, 1:]], axis=3)
            bk, bv = (look_around(bk), look_around(bv))
            bt = jnp.arange(n).reshape(w, WINDOW)
            btp = jnp.pad(bt, ((1, 0), (0, 0)), constant_values=-1)
            btk = jnp.concatenate([btp[:w], btp[1:]], axis=1)
            sim = jnp.einsum('bhwid,bhwjd->bhwij', bq, bk)
            i = bt[:, :, None]
            j = btk[:, None, :]
            mask = (i < j) | (i > j + WINDOW) | (j == -1)
            sim = jnp.where(mask, -jnp.finfo(sim.dtype).max, sim)
            attn = jax.nn.softmax(sim, axis=-1)
            out = jnp.einsum('bhwij,bhwjd->bhwid', attn, bv)
            return out.reshape(b, h, n, d)

        def _layer(x, wqkv, qs, ksc, wo, lg, lb, w1, b1, w2, b2):
            b, n, _ = x.shape
            h = shift_token(x)
            qkv = h @ wqkv
            q, k, v = jnp.split(qkv, 3, axis=-1)
            to_heads = lambda t: t.reshape(b, n, HEADS, DIM_HEAD).transpose(0, 2, 1, 3)
            q, k, v = (to_heads(q), to_heads(k), to_heads(v))
            q = l2norm(q) * qs
            k = l2norm(k) * ksc
            q, k = rotary_xpos(q, k)
            o = local_attention(q, k, v)
            o = o.transpose(0, 2, 1, 3).reshape(b, n, INNER)
            x = x + o @ wo
            h = shift_token(x)
            mu = h.mean(-1, keepdims=True)
            var = h.var(-1, keepdims=True)
            h = (h - mu) / jnp.sqrt(var + 1e-05) * lg + lb
            h = h @ w1 + b1
            a, g = jnp.split(h, 2, axis=-1)
            h = a * jax.nn.gelu(g, approximate=False)
            x = x + h @ w2 + b2
            return x
        key = jax.random.key(seed)
        ks = jax.random.split(key, 6)
        return {'x': jax.random.normal(ks[0], (B, N, DIM), jnp.float32), 'wqkv': jax.random.normal(ks[1], (DEPTH, DIM, 3 * INNER), jnp.float32) * 0.02, 'q_scale': jnp.ones((DEPTH, DIM_HEAD), jnp.float32), 'k_scale': jnp.ones((DEPTH, DIM_HEAD), jnp.float32), 'wo': jax.random.normal(ks[2], (DEPTH, INNER, DIM), jnp.float32) * 0.02, 'ln_g': jnp.ones((DEPTH, DIM), jnp.float32), 'ln_b': jnp.zeros((DEPTH, DIM), jnp.float32), 'w1': jax.random.normal(ks[3], (DEPTH, DIM, 2 * HID), jnp.float32) * 0.02, 'b1': jnp.zeros((DEPTH, 2 * HID), jnp.float32), 'w2': jax.random.normal(ks[4], (DEPTH, HID, DIM), jnp.float32) * 0.02, 'b2': jnp.zeros((DEPTH, DIM), jnp.float32)}
    _L0_ffn_in = _L0_ffn_setup()
    _L0_c = _w((lambda *s: np.random.randn(*s).astype(np.float32) * 0.05)(8, 256))
    _L0_wmod = _w((lambda *s: np.random.randn(*s).astype(np.float32) * 0.05)(256, 6 * 256) * 256 ** (-0.5))
    _d = {'L0_attn_x': _L0_attn_in['x'], 'L0_attn_w_q': _L0_attn_in['w_q'], 'L0_attn_w_k': _L0_attn_in['w_k'], 'L0_attn_w_v': _L0_attn_in['w_v'], 'L0_ffn_wqkv': _L0_ffn_in['wqkv'], 'L0_ffn_q_scale': _L0_ffn_in['q_scale'], 'L0_ffn_k_scale': _L0_ffn_in['k_scale'], 'L0_ffn_wo': _L0_ffn_in['wo'], 'L0_ffn_ln_g': _L0_ffn_in['ln_g'], 'L0_ffn_ln_b': _L0_ffn_in['ln_b'], 'L0_ffn_w1': _L0_ffn_in['w1'], 'L0_ffn_b1': _L0_ffn_in['b1'], 'L0_ffn_w2': _L0_ffn_in['w2'], 'L0_ffn_b2': _L0_ffn_in['b2'], 'L0_c': _L0_c, 'L0_wmod': _L0_wmod}
    _x0 = _d['L0_attn_x']
    _d['L0_attn_x'] = jax.random.normal(jax.random.fold_in(jax.random.key(seed), 1), (8, 1024, 256), dtype=_x0.dtype)
    del _x0
    return _d

def reference(L0_attn_x, L0_attn_w_q, L0_attn_w_k, L0_attn_w_v, L0_ffn_wqkv, L0_ffn_q_scale, L0_ffn_k_scale, L0_ffn_wo, L0_ffn_ln_g, L0_ffn_ln_b, L0_ffn_w1, L0_ffn_b1, L0_ffn_w2, L0_ffn_b2, L0_c, L0_wmod):

    def _L0_attn_ref(x, w_q, w_k, w_v):
        import jax, jax.numpy as jnp
        import numpy as np
        D_MODEL = 256
        N_HEADS = 16
        HEAD_D = D_MODEL // N_HEADS
        B, T = (4, 1024)
        ROPE_BASE = 10000.0

        def _rope(x):
            Bx, Tx, Dx = x.shape
            half = Dx // 2
            inv_freq = 1.0 / ROPE_BASE ** (jnp.arange(half, dtype=jnp.float32) / half)
            ang = jnp.arange(Tx, dtype=jnp.float32)[:, None] * inv_freq[None, :]
            cos, sin = (jnp.cos(ang), jnp.sin(ang))
            x1 = x[..., 0::2]
            x2 = x[..., 1::2]
            r1 = x1 * cos - x2 * sin
            r2 = x1 * sin + x2 * cos
            out = jnp.stack([r1, r2], axis=-1).reshape(Bx, Tx, Dx)
            return out
        Bx, Tx, Dx = x.shape
        d = Dx // N_HEADS
        xh = x.reshape(Bx, Tx, d, N_HEADS)
        q = jnp.einsum('btqh,qdh->btdh', xh, w_q).reshape(Bx, Tx, Dx)
        k = jnp.einsum('btkh,kdh->btdh', xh, w_k).reshape(Bx, Tx, Dx)
        v = jnp.einsum('btvh,vdh->btdh', xh, w_v).reshape(Bx, Tx, Dx)
        q = _rope(q)
        k = _rope(k)
        gamma = 1.0 / jnp.sqrt(jnp.float32(Dx))
        scores = jnp.einsum('bqd,bkd->bqk', q, k) * gamma
        causal = jnp.tril(jnp.ones((Tx, Tx), dtype=bool))
        scores = jnp.where(causal[None], scores, -jnp.inf)
        attn = jax.nn.softmax(scores, axis=-1)
        y = jnp.einsum('bqt,btd->bqd', attn, v)
        return y

    def _L0_ffn_ref(x, wqkv, q_scale, k_scale, wo, ln_g, ln_b, w1, b1, w2, b2):
        import jax, jax.numpy as jnp
        import numpy as np
        DIM = 256
        DEPTH = 2
        HEADS = 8
        DIM_HEAD = 64
        WINDOW = 128
        INNER = HEADS * DIM_HEAD
        HID = int(DIM * 4 * 2 / 3)
        B, N = (2, 2048)
        QK_SCALE = 8.0

        def shift_token(t):
            t1, t2 = jnp.split(t, 2, axis=-1)
            t2 = jnp.pad(t2, ((0, 0), (1, 0), (0, 0)))[:, :-1]
            return jnp.concatenate([t1, t2], axis=-1)

        def l2norm(t):
            return t / jnp.clip(jnp.linalg.norm(t, axis=-1, keepdims=True), 1e-12)

        def rotate_half(x):
            x1, x2 = jnp.split(x, 2, axis=-1)
            return jnp.concatenate([-x2, x1], axis=-1)

        def rotary_xpos(q, k):
            n = q.shape[-2]
            half_idx = jnp.arange(0, DIM_HEAD, 2, dtype=jnp.float32)
            inv_freq = 1.0 / 10000.0 ** (half_idx / DIM_HEAD)
            t = jnp.arange(n, dtype=jnp.float32)
            freqs = t[:, None] * inv_freq[None, :]
            freqs = jnp.concatenate([freqs, freqs], axis=-1)
            base = (half_idx + 0.4 * DIM_HEAD) / (1.4 * DIM_HEAD)
            power = (t - n // 2) / float(WINDOW // 2)
            scale = base[None, :] ** power[:, None]
            scale = jnp.concatenate([scale, scale], axis=-1)
            cos, sin = (jnp.cos(freqs), jnp.sin(freqs))
            q = q * cos * scale + rotate_half(q) * sin * scale
            k = k * cos / scale + rotate_half(k) * sin / scale
            return (q, k)

        def local_attention(q, k, v):
            b, h, n, d = q.shape
            w = n // WINDOW
            bq = q.reshape(b, h, w, WINDOW, d) * QK_SCALE
            bk = k.reshape(b, h, w, WINDOW, d)
            bv = v.reshape(b, h, w, WINDOW, d)

            def look_around(t):
                p = jnp.pad(t, ((0, 0), (0, 0), (1, 0), (0, 0), (0, 0)))
                return jnp.concatenate([p[:, :, :w], p[:, :, 1:]], axis=3)
            bk, bv = (look_around(bk), look_around(bv))
            bt = jnp.arange(n).reshape(w, WINDOW)
            btp = jnp.pad(bt, ((1, 0), (0, 0)), constant_values=-1)
            btk = jnp.concatenate([btp[:w], btp[1:]], axis=1)
            sim = jnp.einsum('bhwid,bhwjd->bhwij', bq, bk)
            i = bt[:, :, None]
            j = btk[:, None, :]
            mask = (i < j) | (i > j + WINDOW) | (j == -1)
            sim = jnp.where(mask, -jnp.finfo(sim.dtype).max, sim)
            attn = jax.nn.softmax(sim, axis=-1)
            out = jnp.einsum('bhwij,bhwjd->bhwid', attn, bv)
            return out.reshape(b, h, n, d)

        def _layer(x, wqkv, qs, ksc, wo, lg, lb, w1, b1, w2, b2):
            b, n, _ = x.shape
            h = shift_token(x)
            qkv = h @ wqkv
            q, k, v = jnp.split(qkv, 3, axis=-1)
            to_heads = lambda t: t.reshape(b, n, HEADS, DIM_HEAD).transpose(0, 2, 1, 3)
            q, k, v = (to_heads(q), to_heads(k), to_heads(v))
            q = l2norm(q) * qs
            k = l2norm(k) * ksc
            q, k = rotary_xpos(q, k)
            o = local_attention(q, k, v)
            o = o.transpose(0, 2, 1, 3).reshape(b, n, INNER)
            x = x + o @ wo
            h = shift_token(x)
            mu = h.mean(-1, keepdims=True)
            var = h.var(-1, keepdims=True)
            h = (h - mu) / jnp.sqrt(var + 1e-05) * lg + lb
            h = h @ w1 + b1
            a, g = jnp.split(h, 2, axis=-1)
            h = a * jax.nn.gelu(g, approximate=False)
            x = x + h @ w2 + b2
            return x
        for l in range(DEPTH):
            x = _layer(x, wqkv[l], q_scale[l], k_scale[l], wo[l], ln_g[l], ln_b[l], w1[l], b1[l], w2[l], b2[l])
        return x
    x = L0_attn_x
    mod = (_silu(L0_c) @ L0_wmod).reshape(L0_c.shape[0], 6, 1, -1)
    sa, ca, ga, sb, cb, gb = (mod[:, 0], mod[:, 1], mod[:, 2], mod[:, 3], mod[:, 4], mod[:, 5])
    ga = (2 * (ga >= 0) - 1) * jnp.maximum(jnp.abs(ga), 0.25)
    gb = (2 * (gb >= 0) - 1) * jnp.maximum(jnp.abs(gb), 0.25)
    h = _layernorm(x, axis=-1) * (1 + ca) + sa
    x = x + ga * _L0_attn_ref(h, L0_attn_w_q, L0_attn_w_k, L0_attn_w_v)
    h = _layernorm(x, axis=-1) * (1 + cb) + sb
    x = x + gb * _L0_ffn_ref(h, L0_ffn_wqkv, L0_ffn_q_scale, L0_ffn_k_scale, L0_ffn_wo, L0_ffn_ln_g, L0_ffn_ln_b, L0_ffn_w1, L0_ffn_b1, L0_ffn_w2, L0_ffn_b2)
    return x

_drawn_inputs = setup_inputs


def setup_inputs(seed=0):
    import zlib

    import numpy as np

    out = dict(_drawn_inputs(seed))
    spreads = {'L0_ffn_q_scale': (1.0, 0.6),
     'L0_ffn_k_scale': (1.0, 0.6),
     'L0_ffn_ln_g': (1.0, 0.6),
     'L0_ffn_ln_b': (0.0, 0.8),
     'L0_ffn_b1': (0.0, 0.8),
     'L0_ffn_b2': (0.0, 0.454)}
    factors = {'L0_attn_w_q': 8.0,
     'L0_attn_w_k': 8.0,
     'L0_attn_w_v': 7.274,
     'L0_ffn_wqkv': 6.933,
     'L0_ffn_wo': 6.818,
     'L0_ffn_w1': 4.768,
     'L0_ffn_w2': 4.749}
    for name, (base, spread) in spreads.items():
        noise = np.random.default_rng([zlib.crc32(name.encode()), seed]).standard_normal(out[name].shape)
        drawn = base * np.exp(spread * noise) if base else spread * noise
        out[name] = jnp.asarray(drawn.astype(out[name].dtype))
    for name, factor in factors.items():
        out[name] = (out[name] * factor).astype(out[name].dtype)
    return out
```

```python
from contextlib import ExitStack

import concourse.bass as bass
from concourse import mybir

F32 = mybir.dt.float32
F16 = mybir.dt.float16
BF16 = mybir.dt.bfloat16
ALU = mybir.AluOpType
ACT = mybir.ActivationFunctionType
AX = mybir.AxisListType.X

P = 128
EPS = 1e-5
NEG = -1.0e30
BATCH, SEQ, DIM = 8, 1024, 256
NT = SEQ // P
NC = DIM // P
AH = 16
AD = DIM // AH
HPC = AH // NC
DEPTH = 2
HEADS, DH = 8, 64
INNER = HEADS * DH
HID = DIM * 4 * 2 // 3
NJ = HID // P
TAIL = HID - NJ * P
NB1 = 2 * NJ + 1
GT = 64
NG = 2
GW = NT // NG
GAMMA = 1.0 / DIM ** 0.5


def adaln_kernel(nc, x, w_q, w_k, w_v, wqkv, q_scale, k_scale, wo, ln_g, ln_b, w1, b1, w2, b2,
                 cond, wmod, rope_cos, rope_sin, xpos, out):
    mod_rows = nc.dram_tensor("mod_rows", [BATCH, 6 * DIM], F32, kind="Internal").ap()

    with ExitStack() as ctx:
        ctx.enter_context(nc.allow_non_contiguous_dma(reason="small vectors and shifted rows"))
        def sb(name, shape, dt=F32):
            return ctx.enter_context(nc.sbuf_tensor(name, shape, dt))

        names = []

        def sem(name):
            s = ctx.enter_context(nc.semaphore(name))
            names.append(s)
            return s

        ps = ctx.enter_context(nc.psum_tensor("ps", [P, 8, 512], F32))

        wqkv_p = [sb(f"wqkv_{s}", [P, DEPTH, NC, 3 * INNER], F16) for s in ("hi", "lo")]
        wo_p = [sb(f"wo_{s}", [P, DEPTH, INNER // P, DIM], F16) for s in ("hi", "lo")]
        w1_p = [sb(f"w1_{s}", [P, DEPTH, NC, NB1, P], F16) for s in ("hi", "lo")]
        w2_p = [sb(f"w2_{s}", [P, DEPTH, NJ + 1, DIM], F16) for s in ("hi", "lo")]
        bd_p = [sb(f"bd_{s}", [P, NC, 3, P], F16) for s in ("hi", "lo")]
        cos_t = sb("cos_t", [P, NT, NC, P // 2])
        sin_t = sb("sin_t", [P, NT, NC, P // 2])
        xp_t = sb("xp_t", [P, DEPTH, NT, 4, DH])
        mask_t = sb("mask_t", [P, 2, 512], BF16)
        id_b = sb("id_b", [P, P], BF16)
        id_f = sb("id_f", [P, P])
        bias1 = sb("bias1", [P, DEPTH, NB1])
        u_tail = [sb(f"u_tail_{s}", [GT, 512], F16) for s in ("hi", "lo")]
        neg_half = sb("neg_half", [P, 16])

        xu = sb("xu", [P, 2, NT, DIM])
        X, U = xu[:, 0], xu[:, 1]
        modb = sb("modb", [P, 4, DIM])
        modc = sb("modc", [P, 2, NC])
        ht = [sb(f"ht_{s}", [P, NC, SEQ + 1], F16) for s in ("hi", "lo")]
        st = sb("st", [P, 8, 2, 6])
        mv = sb("mv", [P, NT, 2])
        rstd = sb("rstd", [P, NT])
        veps = sb("veps", [P, NT])

        ar_a = sb("ar_a", [P, 26 * 256])
        QK1 = ar_a[:, 0:4096].rearrange("p (c s n) -> p c s n", c=NC, s=2)
        V1 = ar_a[:, 4096:6144].rearrange("p (t n) -> p t n", t=NT)
        KT = ar_a[:, 0:1536].rearrange("p (r h n) -> p r h n", r=3, h=4)
        QT = ar_a[:, 1536:2560].rearrange("p (r h n) -> p r h n", r=2, h=4)
        V = ar_a[:, 2560:4096].rearrange("p (r n) -> p r n", r=3)
        RAW = ar_a[:, 4096:6144].rearrange("p (r s n) -> p r s n", r=2, s=2)
        ar_b = sb("ar_b", [P, 20 * 256])
        P1 = ar_b[:, 0:2048].rearrange("p (r n) -> p r n", r=2)
        PT1 = ar_b[:, 2048:4096].rearrange("p (r k n) -> p r k n", r=2, k=NT)
        PW = ar_b[:, 0:2048].rearrange("p (f x k n) -> p f x k n", f=2, x=2, k=2)
        PTW = ar_b[:, 2048:4096].rearrange("p (f x k n) -> p f x k n", f=2, x=2, k=4)
        GB = ar_b[:, 0:1024].rearrange("p (r n) -> p r n", r=2)
        UB = ar_b[:, 1024:2048].rearrange("p (r n) -> p r n", r=2)
        uh = ar_b[:, 2048:3328].bitcast(F16).rearrange("p (j n) -> p j n", j=NJ)
        ul = ar_b[:, 3328:4608].bitcast(F16).rearrange("p (j n) -> p j n", j=NJ)
        ar_c = sb("ar_c", [P, 16 * 256])
        M1 = ar_c[:, 0:2048].rearrange("p (r n) -> p r n", r=2)
        M2 = ar_c[:, 2048:3072]
        SQ = ar_c[:, 3072:4096]
        xn1 = ar_c[:, 0:1024].rearrange("p (r t c n) -> p r t c n", r=2, t=2, c=NC)
        hf1 = ar_c[:, 1024:2048].rearrange("p (r c n) -> p r c n", r=2, c=NC)
        ra = ar_c[:, 2048:3072].rearrange("p (r c s n) -> p r c s n", r=2, c=NC, s=2)
        rb = ar_c[:, 3072:4096].rearrange("p (r c s n) -> p r c s n", r=2, c=NC, s=2)
        XN = sb("XN", [P, 2, 2, DIM])
        XS = sb("XS", [P, NT, P])
        ot = [sb(f"ot_{s}", [P, 4, P], F16) for s in ("hi", "lo")]
        small = sb("small", [P, 160])
        mx1, nm1, sm1, rs1 = (small[:, 8 * i:8 * i + 8] for i in range(4))
        ss = small[:, 32:64].rearrange("p (r n) -> p r n", r=2)
        ssm = small[:, 64:80]
        rinv = small[:, 80:112].rearrange("p (r n) -> p r n", r=2)
        mxw = small[:, 112:120]
        nbw = small[:, 120:136].rearrange("p (r n) -> p r n", r=2)
        smw = small[:, 136:152].rearrange("p (r n) -> p r n", r=2)
        rsw = small[:, 152:156]
        yt = sb("yt", [P, 2, DIM])

        def mm3(pe, o, a, b, start, stop):
            pe.matmul(o, a[0], b[0], start=start, stop=False)
            pe.matmul(o, a[0], b[1], start=False, stop=False)
            return pe.matmul(o, a[1], b[0], start=False, stop=stop)

        setup(nc, ctx, locals())

        ctx2 = ctx.enter_context(ExitStack())
        names.clear()
        s_x = [sem(f"x_loaded{g}") for g in range(2)]
        s_mod = sem("mod_loaded")
        s_bst, s_mv, s_rstd = sem("bn_done"), sem("meanvar_ready"), sem("rstd_ready")
        s_xn, s_xnT, s_hh, s_hl = sem("xn_ready"), sem("xn_transposed"), sem("h_hi_ready"), sem("h_lo_ready")
        s_proj, s_m1a, s_v1, s_rot = sem("proj_done"), sem("rope_products"), sem("v_copied"), sem("rope_done")
        s_qkt, s_qk = sem("qk_transposed"), sem("qk_copied")
        s_s, s_mx, s_nm, s_e1 = sem("scores_done"), sem("rowmax_done"), sem("negmax_ready"), sem("probs_ready")
        s_ptr, s_pte, s_y, s_rs, s_yo, s_x2 = (sem("probsT_done"), sem("probsT_copied"), sem("attn_out_done"),
                                               sem("rowsum_inverse"), sem("attn_out_scaled"), sem("x_updated"))
        s_u0a, s_u0b, s_u0 = sem("ln2_ready"), sem("ln2_scaled"), sem("ffn_input_ready")
        s_t = sem("transposes_done")
        s_tf = [sem(f"transpose_bank{i}_read") for i in range(2)]
        s_dh = sem("hT_hi_ready")
        s_qkv, s_ev = sem("qkv_bank_done"), sem("qkv_bank_copied")
        s_sq, s_ss, s_rm, s_rinv = sem("squares_ready"), sem("sumsq_ready"), sem("sumsq_clipped"), sem("inverse_norms")
        s_m, s_add, s_rope = sem("xpos_products"), sem("xpos_sum"), sem("xpos_ready")
        s_sim, s_mxw, s_nb, s_exp = sem("sim_bank_done"), sem("sim_max"), sem("sim_negmax"), sem("sim_bank_exp")
        s_rsw, s_pn, s_pv = sem("prob_inverse_sums"), sem("probs_normalised"), sem("pv_half_done")
        s_oh, s_ol, s_wo, s_res = sem("o_hi_ready"), sem("o_lo_ready"), sem("wo_done"), sem("attn_residual_done")
        s_xs = [sem(f"shifted_rows{g}") for g in range(DEPTH * NG)]
        s_bn, s_lnmv, s_lnv, s_lnr, s_xnw = (sem("ln_stats"), sem("ln_meanvar"), sem("ln_var_eps"),
                                             sem("ln_rstd"), sem("ln_rows_ready"))
        s_nh = sem("ln_hi_ready")
        s_w1g, s_w1, s_g, s_ust, s_uh, s_ul = (sem("w1_gate_done"), sem("w1_done"), sem("gelu_ready"),
                                               sem("hidden_ready"), sem("hidden_hi"), sem("hidden_lo"))
        s_w2, s_u2 = sem("w2_done"), sem("mlp_residual_done")
        s_fa, s_fin, s_out = sem("final_scaled"), sem("final_ready"), sem("out_stored")
        s_v2, s_r2 = sem("var_eps_ready"), sem("pool_small")

        tuse = {}

        def plan_transposes():
            order = []
            for l in range(DEPTH):
                if l == 0:
                    order += [("D", 0, 0), ("D", 0, 1)]
                for s in range(NT + 2):
                    for piece in window_step(l, s):
                        if piece[0] == "F":
                            order += [("F", piece[1], 0), ("F", piece[1], 1)]
                        elif piece[0] == "H":
                            order += [("H", piece[1], piece[2], 0), ("H", piece[1], piece[2], 1)]
                        elif piece[0] in "DN":
                            order.append(piece)
                for piece in mlp_steps(l):
                    if piece[0] in "DN":
                        order.append(piece)
            for u, key in enumerate(order):
                tuse[key] = u

        def window_step(l, s):
            a, b, c = s, s - 1, s - 2
            n = l * NT
            f = []
            hb, hc, ha = 0 <= b < NT, 0 <= c < NT, a < NT
            if hb:
                f.append(("F", n + b))
            if ha:
                f.append(("E", n + a, 0))
            if hc:
                f.append(("H", n + c, 1))
            if hb:
                f.append(("G", n + b, 0))
            if ha:
                f.append(("E", n + a, 1))
            if hc:
                f.append(("I", n + c, 1))
            if hb:
                f.append(("G", n + b, 1))
            if ha:
                f.append(("E", n + a, 2))
            if hb:
                f.append(("G", n + b, 2))
            if hc:
                f.append(("J", n + c))
            if s in (1, 3):
                f.append(("D", l, (s + 3) // 2))
            if hb:
                f += [("H", n + b, 0), ("G", n + b, 3), ("I", n + b, 0)]
            if s == 6:
                f.append(("L", l, 0))
            if s in (7, 8):
                f.append(("N", l, s - 7))
            return f

        def mlp_steps(l):
            f = [("L", l, 1)]
            f += [("W", l, 0, j) for j in range(3)]
            f += [("N", l, 2), ("N", l, 3)]
            f += [("W", l, 0, j) for j in range(3, NJ + 1)]
            f += [("W", l, 1, 0), ("W", l, 1, 1)]
            f += [("Y", l * NT + w) for w in range(GW)]
            f += [("W", l, 1, j) for j in range(2, NJ + 1)]
            if l + 1 < DEPTH:
                f += [("D", l + 1, 0), ("D", l + 1, 1)]
            f += [("Y", l * NT + w) for w in range(GW, NT)]
            return f

        def schedule():
            f = [("D", 0, 0), ("D", 0, 1)]
            for l in range(DEPTH):
                for s in range(NT + 2):
                    f += window_step(l, s)
                f += mlp_steps(l)
            return f

        plan_transposes()
        PIECES = schedule()

        def tbank(key):
            return 5 + tuse[key] % 2

        def t_read(key):
            return s_tf[tuse[key] % 2], tuse[key] // 2 + 1

        with nc.Fori(0, BATCH) as b:
            block = nc.Block()
            with block:

                @block.sync
                def _(sp):
                    for g in range(2):
                        sp.dma_start(X[:, g * 4:g * 4 + 4, :],
                                     x[b, g * 512:(g + 1) * 512, :].rearrange("(t p) d -> p t d", p=P)
                                     ).then_inc(s_x[g], 16)
                    for k in range(2):
                        for c in range(NC):
                            for h in range(HPC):
                                src = mod_rows[b, k * DIM:(k + 1) * DIM].rearrange("(q h) -> h q", h=AH)
                                sp.dma_start(modc[h * AD:(h + 1) * AD, k, c:c + 1],
                                             src[c * HPC + h, :].unsqueeze(1)).then_inc(s_mod, 16)
                    sp.dma_start(modb[:, :, :],
                                 mod_rows[b, 2 * DIM:6 * DIM].rearrange("(k d) -> k d", k=4).partition_broadcast(P)
                                 ).then_inc(s_mod, 16)
                    for l in range(DEPTH):
                        for w in range(NT):
                            sp.wait_ge(s_res, l * NT + w + 1)
                            sp.dma_start(XS[1:P, w, :], U[0:P - 1, w, P:DIM]).then_inc(s_xs[l * NG + w // GW], 16)
                            if w:
                                sp.dma_start(XS[0:1, w, :], U[P - 1:P, w - 1, P:DIM]
                                             ).then_inc(s_xs[l * NG + w // GW], 16)
                    for w in range(NT):
                        sp.wait_ge(s_fin, w + 1)
                        sp.dma_start(out[b, w * P:(w + 1) * P, :], U[:, w, :]).then_inc(s_out, 16)
                    sp.wait_ge(s_out, 16 * NT)

                @block.tensor
                def _(pe):
                    def t_xn(p):
                        pe.wait_ge(s_xn, p + 1)
                        if p >= 2:
                            pe.wait_ge(s_hh, p - 1)
                        for t in range(2):
                            for c in range(NC):
                                last = pe.transpose(ps[:, 5 + p % 2, c * 256 + t * P:c * 256 + (t + 1) * P],
                                                    xn1[:, p % 2, t, c, :], id_f[:])
                        last.then_inc(s_xnT, 1)

                    def proj(t):
                        pe.wait_ge(s_hl, t // 2 + 1)
                        if t >= 2:
                            pe.wait_ge(s_v1, t - 1)
                        for c in range(NC):
                            h = [q[:, c, 1 + t * P:1 + (t + 1) * P] for q in ht]
                            w = [q[:, c, :, :].rearrange("p s n -> p (s n)") for q in bd_p]
                            last = mm3(pe, ps[:, 2 * (t % 2) + c, 0:3 * P], h, w, True, True)
                        last.then_inc(s_proj, 1)

                    def t_qk(t):
                        pe.wait_ge(s_rot, t + 1)
                        if t >= 2:
                            pe.wait_ge(s_qk, t - 1)
                        for c in range(NC):
                            for s in range(2):
                                k = (c * 2 + s) * P
                                last = pe.transpose(ps[:, (4, 7)[t % 2], k:k + P], ra[:, t % 2, c, s, :], id_f[:])
                        last.then_inc(s_qkt, 1)

                    t_xn(0)
                    for t in range(NT + 2):
                        if t % 2 == 0 and t // 2 + 1 < NT // 2:
                            t_xn(t // 2 + 1)
                        if t < NT:
                            proj(t)
                        if t >= 2:
                            t_qk(t - 2)

                    def scores(i):
                        if i >= 2:
                            pe.wait_ge(s_e1, i - 1)
                        n = (i + 1) * P
                        for kb in range((n + 511) // 512):
                            w = min(512, n - kb * 512)
                            bank = 2 * (i % 2) + kb
                            for c in range(NC):
                                pe.matmul(ps[:, bank, 0:w], QK1[:, c, 0, i * P:(i + 1) * P],
                                          QK1[:, c, 1, kb * 512:kb * 512 + w], start=(c == 0),
                                          stop=(c == 1))
                        last = pe.matmul(ps[:, 2 * (i % 2) + i // 4, (i % 4) * P:(i % 4 + 1) * P], id_b[:],
                                         mask_t[:, 0, P:2 * P], start=False, stop=True, skip_group_check=True)
                        last.then_inc(s_s, 1)

                    def probs_t(i):
                        pe.wait_ge(s_e1, i + 1)
                        for k4 in range(i // 4 + 1):
                            g = ptg[i] + k4
                            if g >= 2:
                                pe.wait_ge(s_pte, g - 1)
                            for kb in range(4 * k4, min(i + 1, 4 * k4 + 4)):
                                last = pe.transpose(ps[:, (4, 7)[g % 2], (kb % 4) * P:(kb % 4 + 1) * P],
                                                    P1[:, i % 2, kb * P:(kb + 1) * P], id_f[:])
                            last.then_inc(s_ptr, 1)

                    def attn_out(i):
                        pe.wait_ge(s_pte, ptg[i] + i // 4 + 1)
                        if i >= 2:
                            pe.wait_ge(s_yo, i - 1)
                        for kb in range(i + 1):
                            last = pe.matmul(ps[:, 5 + i % 2, 0:DIM], PT1[:, i % 2, kb, :], V1[:, kb, :],
                                             start=(kb == 0), stop=(kb == i))
                        last.then_inc(s_y, 1)

                    pe.wait_ge(s_qk, NT)
                    for i in range(NT + 2):
                        if i < NT:
                            scores(i)
                        if 1 <= i <= NT:
                            probs_t(i - 1)
                        if i >= 2:
                            attn_out(i - 2)

                    def claim(key):
                        u = tuse[key]
                        if u >= 2:
                            pe.wait_ge(s_tf[u % 2], u // 2)
                        return 5 + u % 2

                    def rows_t(key, rows):
                        bank = claim(key)
                        for t in range(2):
                            for c in range(NC):
                                last = pe.transpose(ps[:, bank, c * 256 + t * P:c * 256 + (t + 1) * P],
                                                    rows(t)[:, c * P:(c + 1) * P], id_f[:])
                        last.then_inc(s_t, 1)

                    pe.wait_ge(s_yo, NT)
                    for piece in PIECES:
                        kind, n = piece[0], piece[1]
                        l, w = n // NT, n % NT
                        if kind == "D":
                            l, p = piece[1:]
                            pe.wait_ge(s_u2 if l else s_u0, 2 * p + 2)
                            rows_t(piece, lambda t: U[:, 2 * p + t, :])
                        elif kind == "N":
                            l, p = piece[1:]
                            pe.wait_ge(s_xnw, l * 4 + p + 1)
                            rows_t(piece, lambda t: XN[:, p % 2, t, :])
                        elif kind == "E":
                            k = piece[2]
                            e = 3 * n + k
                            if k == 0 and w % 2 == 0:
                                pe.wait_ge(*t_read(("D", l, w // 2)))
                            if e >= 2:
                                pe.wait_ge(s_ev, e - 1)
                            for c in range(NC):
                                a = w * P + (1 - c)
                                last = mm3(pe, ps[:, e % 2, :], [q[:, c, a:a + P] for q in ht],
                                           [q[:, l, c, k * INNER:(k + 1) * INNER] for q in wqkv_p], c == 0, c == 1)
                            last.then_inc(s_qkv, 1)
                        elif kind == "F":
                            pe.wait_ge(s_rope, n + 1)
                            for s in range(2):
                                bank = claim(("F", n, s))
                                for h in range(4):
                                    k = s * INNER + h * P
                                    last = pe.transpose(ps[:, bank, h * P:(h + 1) * P], M1[:, n % 2, k:k + P], id_f[:])
                                last.then_inc(s_t, 1)
                        elif kind == "G":
                            k, m = piece[2], 4 * n + piece[2]
                            if k == 0:
                                pe.wait_ge(*t_read(("F", n, 0)))
                                pe.wait_ge(*t_read(("F", n, 1)))
                            if m >= 3:
                                pe.wait_ge(s_exp, m - 2)
                            bank, r = 2 + m % 3, 64 * (k % 2)
                            pe.matmul(ps[:, bank, :], id_b[:], mask_t[:, 0 if w else 1, :], start=True, stop=True)
                            for i in range(2):
                                hp = 2 * (k // 2) + i
                                for kb in range(0 if w else 1, 2):
                                    o = i * 256 + kb * P
                                    last = pe.matmul(ps[:, bank, o:o + P], QT[r:r + 64, n % 2, hp, :],
                                                     KT[r:r + 64, (n - 1 + kb) % 3, hp, :], start=False,
                                                     stop=True, skip_group_check=True)
                            last.then_inc(s_sim, 1)
                        elif kind == "H":
                            f = piece[2]
                            pe.wait_ge(s_pn, 2 * n + f + 1)
                            for q in range(2):
                                bank = claim(("H", n, f, q))
                                for k in range(4):
                                    last = pe.transpose(ps[:, bank, k * P:(k + 1) * P],
                                                        PW[:, f, q, k // 2, (k % 2) * P:(k % 2 + 1) * P], id_f[:])
                                last.then_inc(s_t, 1)
                        elif kind == "I":
                            f = piece[2]
                            pe.wait_ge(*t_read(("H", n, f, 0)))
                            pe.wait_ge(*t_read(("H", n, f, 1)))
                            pe.wait_ge(s_ev, 3 * n + 3)
                            if f == 0 and n >= 1:
                                pe.wait_ge(s_res, n)
                            for k in range(2):
                                for kb in range(0 if w else 1, 2):
                                    for q in range(2):
                                        h = 4 * f + q + 2 * k
                                        last = pe.matmul(ps[64 * q:64 * q + 64, 7, (h // 2) * P:(h // 2 + 1) * P],
                                                         V[:, (n - 1 + kb) % 3, h * DH:(h + 1) * DH],
                                                         PTW[:, f, q, 2 * k + kb, :], start=(kb == (0 if w else 1)),
                                                         stop=(kb == 1), skip_group_check=True)
                            last.then_inc(s_pv, 1)
                        elif kind == "J":
                            pe.wait_ge(s_ol, n + 1)
                            for c in range(4):
                                last = mm3(pe, ps[:, 7, 0:DIM], [q[:, c, :] for q in ot],
                                           [q[:, l, c, :] for q in wo_p], c == 0, c == 3)
                            last.then_inc(s_wo, 1)
                        elif kind == "W":
                            l, g, j = piece[1:]
                            v = (l * NG + g) * (NJ + 1) + j
                            if j == 0:
                                pe.wait_ge(*t_read(("N", l, 2 * g)))
                                pe.wait_ge(*t_read(("N", l, 2 * g + 1)))
                            if v >= 2:
                                pe.wait_ge(s_ust, v - 1)
                            for i in range(2 if j < NJ else 1):
                                m = P if j < NJ else GT + TAIL
                                for c in range(NC):
                                    a = g * 512 + 1
                                    last = mm3(pe, ps[0:m, 2 * (v % 2) + i, :],
                                               [q[:, l, c, 2 * j + i, 0:m] for q in w1_p],
                                               [q[:, c, a:a + 512] for q in ht], c == 0, c == 1)
                                last.then_inc(s_w1g if i == 0 else s_w1, 1)
                        elif kind == "Y":
                            if w % GW == 0:
                                pe.wait_ge(s_ul, (n // GW + 1) * (NJ + 1))
                            if w % NT >= 2:
                                pe.wait_ge(s_u2, n - 1)
                            a = (w % GW) * P
                            bank = (4, 7)[w % 2]
                            for j in range(NJ + 1):
                                if j < NJ:
                                    hid = [q[:, j, a:a + P] for q in (uh, ul)]
                                    wt = [q[:, l, j, :] for q in w2_p]
                                else:
                                    hid = [q[0:GT, a:a + P] for q in u_tail]
                                    wt = [q[0:GT, l, j, :] for q in w2_p]
                                last = mm3(pe, ps[:, bank, 0:DIM], hid, wt, j == 0, j == NJ)
                            last.then_inc(s_w2, 1)

                @block.scalar
                def _(act):
                    def h_parts(p):
                        act.wait_ge(s_xnT, p + 1)
                        if p == 0:
                            act.wait_ge(s_mod, 16 * (2 * NC * HPC + 1))
                        if p >= 2:
                            act.wait_ge(s_hl, p - 1)
                        for hi in range(2):
                            for c in range(NC):
                                dst = ht[0][:, c, 1 + p * 256:1 + (p + 1) * 256] if hi else hf1[:, p % 2, c, :]
                                last = act.activation(dst, ps[:, 5 + p % 2, c * 256:(c + 1) * 256], ACT.Identity,
                                                      scale=modc[:, 1, c:c + 1], bias=modc[:, 0, c:c + 1])
                        last.then_inc(s_hh, 1)

                    def v_copy(t):
                        act.wait_ge(s_m1a, t + 1)
                        src = ps[:, 2 * (t % 2):2 * (t % 2) + 2, 2 * P:3 * P].rearrange("p c (d h) -> p c d h", h=HPC)
                        act.activation(V1[:, t, :].rearrange("p (d c h) -> p c d h", c=NC, h=HPC), src,
                                       ACT.Copy).then_inc(s_v1, 1)

                    def qk_copy(t):
                        act.wait_ge(s_qkt, t + 1)
                        act.activation(QK1[:, :, :, t * P:(t + 1) * P],
                                       ps[:, (4, 7)[t % 2], :].rearrange("p (c s n) -> p c s n", c=NC, s=2),
                                       ACT.Copy).then_inc(s_qk, 1)

                    h_parts(0)
                    for t in range(NT + 2):
                        if t % 2 == 0 and t // 2 + 1 < NT // 2:
                            h_parts(t // 2 + 1)
                        if t < NT:
                            v_copy(t)
                        if t >= 2:
                            qk_copy(t - 2)
                    for i in range(NT):
                        act.wait_ge(s_nm, i + 1)
                        n = (i + 1) * P
                        if i >= 2:
                            act.wait_ge(s_ptr, ptg[i - 1])
                        src = ps[:, 2 * (i % 2):2 * (i % 2) + 2, :].rearrange("p a n -> p (a n)")
                        act.activation(P1[:, i % 2, 0:n], src[:, 0:n], ACT.Exp, bias=nm1[:, i:i + 1], scale=GAMMA,
                                       accum_out=sm1[:, i:i + 1]).then_inc(s_e1, 1)

                    for piece in PIECES:
                        kind, n = piece[0], piece[1]
                        if kind in "DN":
                            l, p = piece[1:]
                            act.wait_ge(s_t, tuse[piece] + 1)
                            act.activation(ht[0][:, :, 1 + p * 256:1 + (p + 1) * 256],
                                           ps[:, tbank(piece), :].rearrange("p (c n) -> p c n", c=NC),
                                           ACT.Copy).then_inc(s_dh if kind == "D" else s_nh, 1)
                        elif kind == "E":
                            k = piece[2]
                            act.wait_ge(s_qkv, 3 * n + k + 1)
                            if k == 0 and n >= 2:
                                act.wait_ge(s_m, n - 1)
                            if k == 2 and n >= 3:
                                act.wait_ge(s_pv, 2 * (n - 1))
                            dst = RAW[:, n % 2, k, :] if k < 2 else V[:, n % 3, :]
                            act.activation(dst, ps[:, (3 * n + k) % 2, :], ACT.Copy).then_inc(s_ev, 1)
                            if k == 1:
                                act.wait_ge(s_ev, 3 * n + 2)
                                if n >= 1:
                                    act.wait_ge(s_ss, n)
                                act.activation(SQ, RAW[:, n % 2, :, :].rearrange("p s n -> p (s n)"),
                                               ACT.Square).then_inc(s_sq, 1)
                        elif kind == "F":
                            for s in range(2):
                                key = ("F", n, s)
                                act.wait_ge(s_t, tuse[key] + 1)
                                act.activation(KT[:, n % 3] if s else QT[:, n % 2],
                                               ps[:, tbank(key), :].rearrange("p (h n) -> p h n", h=4),
                                               ACT.Copy).then_inc(t_read(key)[0], 1)
                        elif kind == "G":
                            k, m = piece[2], 4 * n + piece[2]
                            act.wait_ge(s_nb, m + 1)
                            for i in range(2):
                                h = 4 * (k // 2) + k % 2 + 2 * i
                                last = act.activation(PW[:, k // 2, k % 2, i, :],
                                                      ps[:, 2 + m % 3, i * 256:(i + 1) * 256], ACT.Exp,
                                                      bias=nbw[:, n % 2, h:h + 1], scale=rinv[:, n % 2, h:h + 1],
                                                      accum_out=smw[:, n % 2, h:h + 1])
                            last.then_inc(s_exp, 1)
                        elif kind == "H":
                            key = ("H", n, piece[2], 1)
                            act.wait_ge(s_t, tuse[key] + 1)
                            if 2 * n + piece[2] >= 2:
                                act.wait_ge(s_pv, 2 * n + piece[2] - 1)
                            act.activation(PTW[:, piece[2], 1],
                                           ps[:, tbank(key), :].rearrange("p (k n) -> p k n", k=4),
                                           ACT.Copy).then_inc(t_read(key)[0], 1)
                        elif kind == "I" and piece[2] == 1:
                            act.wait_ge(s_pv, 2 * n + 2)
                            act.activation(ot[0][:, :, :], ps[:, 7, :].rearrange("p (h n) -> p h n", h=4),
                                           ACT.Copy).then_inc(s_oh, 1)
                        elif kind == "W":
                            l, g, j = piece[1:]
                            v = (l * NG + g) * (NJ + 1) + j
                            act.wait_ge(s_w1g, v + 1)
                            if v >= 2:
                                act.wait_ge(s_ust, v - 1)
                            if j < NJ:
                                dst, src = GB[:, v % 2, :], ps[:, 2 * (v % 2), :]
                                bias = bias1[:, l, 2 * j:2 * j + 1]
                            else:
                                dst, src = GB[0:TAIL, v % 2, :], ps[GT:GT + TAIL, 2 * (v % 2), :]
                                bias = bias1[GT:GT + TAIL, l, 2 * j:2 * j + 1]
                            act.activation(dst, src, ACT.Gelu, bias=bias).then_inc(s_g, 1)
                            todo = [v - 1] if j > 0 else []
                            if j == NJ:
                                todo.append(v)
                            for q in todo:
                                jj = q % (NJ + 1)
                                act.wait_ge(s_ust, q + 1)
                                if jj == 0 and q > 0:
                                    act.wait_ge(s_w2, (q // (NJ + 1)) * GW)
                                rows = P if jj < NJ else TAIL
                                dst = uh[:, jj, :] if jj < NJ else u_tail[0][0:TAIL, :]
                                act.activation(dst, UB[0:rows, q % 2, :], ACT.Copy).then_inc(s_uh, 1)

                @block.vector
                def _(dve):
                    for g in range(2):
                        dve.wait_ge(s_x[g], 16)
                        for t in range(4):
                            last = dve.bn_stats(st[:, t + 4 * g, 0, :], X[:, t + 4 * g, :])
                        last.then_inc(s_bst, 1)
                    for g in range(2):
                        dve.wait_ge(s_bst, g + 1)
                        for t in range(4 * g, 4 * g + 4):
                            last = dve.bn_aggr(mv[:, t, :], st[:, t, 0, :])
                        last.then_inc(s_mv, 1)
                    for p in range(NT // 2):
                        if p % 2 == 0:
                            dve.wait_ge(s_rstd, p // 2 + 1)
                        if p >= 2:
                            dve.wait_ge(s_xnT, p - 1)
                        for i in range(2):
                            t = 2 * p + i
                            last = dve.tensor_scalar(
                                xn1[:, p % 2, i, :, :].rearrange("p c (h q) -> p (c h) q", q=AD),
                                X[:, t, :].rearrange("p (q h) -> p h q", h=AH),
                                mv[:, t, 0:1], rstd[:, t:t + 1], ALU.subtract, ALU.mult)
                        last.then_inc(s_xn, 1)

                    def rope1(t):
                        dve.wait_ge(s_proj, t + 1)
                        if t >= 2:
                            dve.wait_ge(s_qkt, t - 1)
                        for c in range(NC):
                            src = ps[:, 2 * (t % 2) + c, 0:2 * P].rearrange("p (s i e) -> p s i e", s=2, e=2)
                            a = ra[:, t % 2, c].rearrange("p s (i e) -> p s i e", e=2)
                            bb = rb[:, t % 2, c].rearrange("p s (i e) -> p s i e", e=2)
                            cs = cos_t[:, t, c, :].unsqueeze(1).broadcast_to((P, 2, 64))
                            sn = sin_t[:, t, c, :].unsqueeze(1).broadcast_to((P, 2, 64))
                            for e in range(2):
                                dve.tensor_tensor(a[:, :, :, e], src[:, :, :, e], cs, ALU.mult)
                            dve.scalar_tensor_tensor(out=bb[:, :, :, 0], in0=src[:, :, :, 1], scalar=-1.0, in1=sn,
                                                     op0=ALU.mult, op1=ALU.mult)
                            last = dve.tensor_tensor(bb[:, :, :, 1], src[:, :, :, 0], sn, ALU.mult)
                        last.then_inc(s_m1a, 1)

                    for t in range(NT):
                        rope1(t)

                    def row_max(i):
                        dve.wait_ge(s_s, i + 1)
                        src = ps[:, 2 * (i % 2):2 * (i % 2) + 2, :].rearrange("p a n -> p (a n)")
                        dve.tensor_reduce(mx1[:, i:i + 1], src[:, 0:(i + 1) * P], AX, ALU.max).then_inc(s_mx, 1)
                        dve.wait_ge(s_mx, i + 1)
                        dve.tensor_scalar(nm1[:, i:i + 1], mx1[:, i:i + 1], -GAMMA, None, ALU.mult).then_inc(s_nm, 1)

                    def probs_copy(i):
                        for k4 in range(i // 4 + 1):
                            g = ptg[i] + k4
                            dve.wait_ge(s_ptr, g + 1)
                            if i >= 2 and k4 == 0:
                                dve.wait_ge(s_y, i - 1)
                            m = min(4, i + 1 - 4 * k4)
                            dve.tensor_copy(PT1[:, i % 2, 4 * k4:4 * k4 + m, :],
                                            ps[:, (4, 7)[g % 2], 0:m * P].rearrange("p (k n) -> p k n", n=P)
                                            ).then_inc(s_pte, 1)

                    def y_scale(i):
                        dve.wait_ge(s_e1, i + 1)
                        dve.reciprocal(rs1[:, i:i + 1], sm1[:, i:i + 1]).then_inc(s_rs, 1)
                        dve.wait_ge(s_rs, i + 1)
                        dve.wait_ge(s_y, i + 1)
                        if i >= 2:
                            dve.wait_ge(s_x2, i - 1)
                        dve.scalar_tensor_tensor(out=yt[:, i % 2, :], in0=ps[:, 5 + i % 2, 0:DIM],
                                                 scalar=rs1[:, i:i + 1], in1=modb[:, 0, :], op0=ALU.mult,
                                                 op1=ALU.mult).then_inc(s_yo, 1)

                    dve.wait_ge(s_mod, 16 * (2 * NC * HPC + 1))
                    for i in range(NT + 2):
                        if i < NT:
                            row_max(i)
                        if 1 <= i <= NT:
                            probs_copy(i - 1)
                        if i >= 2:
                            y_scale(i - 2)
                        if i in (6, NT + 1):
                            g = 0 if i == 6 else 1
                            dve.wait_ge(s_x2, 4 * g + 4)
                            for t in range(4 * g, 4 * g + 4):
                                last = dve.bn_stats(st[:, t, 0, :], X[:, t, :])
                            last.then_inc(s_bst, 1)
                            dve.wait_ge(s_bst, 3 + g)
                            for t in range(4 * g, 4 * g + 4):
                                last = dve.bn_aggr(mv[:, t, :], st[:, t, 0, :])
                            last.then_inc(s_mv, 1)
                            dve.wait_ge(s_rstd, 3 + g)
                            for t in range(4 * g, 4 * g + 4):
                                dve.tensor_scalar(U[:, t, :], X[:, t, :], mv[:, t, 0:1], rstd[:, t:t + 1],
                                                  ALU.subtract, ALU.mult).then_inc(s_u0a, 1)

                    def norm(n, f):
                        dve.wait_ge(s_exp, 4 * n + 2 * f + 2)
                        dve.reciprocal(rsw, smw[:, n % 2, 4 * f:4 * f + 4]).then_inc(s_rsw, 1)
                        dve.wait_ge(s_rsw, 2 * n + f + 1)
                        for q in range(2):
                            for i in range(2):
                                k = q + 2 * i
                                pw = PW[:, f, q, i, :]
                                last = dve.tensor_scalar(pw, pw, rsw[:, k:k + 1], None, ALU.mult)
                        last.then_inc(s_pn, 1)

                    for piece in PIECES:
                        kind, n = piece[0], piece[1]
                        l, w = n // NT, n % NT
                        if kind in "DN":
                            l, p = piece[1:]
                            dve.wait_ge(s_dh if kind == "D" else s_nh, l * 4 + p + 1)
                            cols = slice(1 + p * 256, 1 + (p + 1) * 256)
                            dve.tensor_tensor(ht[1][:, :, cols],
                                              ps[:, tbank(piece), :].rearrange("p (c n) -> p c n", c=NC),
                                              ht[0][:, :, cols], ALU.subtract).then_inc(t_read(piece)[0], 1)
                        elif kind == "E" and piece[2] == 1:
                            dve.wait_ge(s_sq, n + 1)
                            dve.tensor_reduce(ss[:, n % 2, :], SQ.rearrange("p (h d) -> p h d", d=DH), AX,
                                              ALU.add).then_inc(s_ss, 1)
                            if n >= 2:
                                dve.wait_ge(s_t, tuse[("F", n - 2, 1)] + 1)
                            raw = RAW[:, n % 2].rearrange("p s (h d) -> p s h d", d=DH)
                            m1 = M1[:, n % 2, :].rearrange("p (s h d) -> p s h d", s=2, d=DH)
                            m2 = M2.rearrange("p (s h d) -> p s h d", s=2, d=DH)
                            cs = xp_t[:, l, w, 0:2, :].unsqueeze(2).broadcast_to((P, 2, HEADS, DH))
                            sn = xp_t[:, l, w, 2:4, :].unsqueeze(2).broadcast_to((P, 2, HEADS, DH))
                            dve.tensor_tensor(m1, raw, cs, ALU.mult)
                            if n >= 1:
                                dve.wait_ge(s_add, n)
                            for e in range(2):
                                lo, hi = slice(32 * e, 32 * e + 32), slice(32 - 32 * e, 64 - 32 * e)
                                last = dve.tensor_tensor(m2[:, :, :, lo], raw[:, :, :, hi], sn[:, :, :, lo], ALU.mult)
                            last.then_inc(s_m, 1)
                        elif kind == "G":
                            k, m = piece[2], 4 * n + piece[2]
                            h = 4 * (k // 2) + k % 2
                            dve.wait_ge(s_sim, m + 1)
                            dve.tensor_reduce(mxw[:, h:h + 3:2], ps[:, 2 + m % 3, :].rearrange("p (i n) -> p i n", i=2),
                                              AX, ALU.max).then_inc(s_mxw, 1)
                            dve.wait_ge(s_mxw, m + 1)
                            dve.wait_ge(s_rinv, n + 1)
                            dve.scalar_tensor_tensor(out=nbw[:, n % 2, h:h + 3:2], in0=mxw[:, h:h + 3:2], scalar=-1.0,
                                                     in1=rinv[:, n % 2, h:h + 3:2], op0=ALU.mult,
                                                     op1=ALU.mult).then_inc(s_nb, 1)
                            if k == 2:
                                norm(n, 0)
                            elif k == 3:
                                norm(n, 1)
                        elif kind == "H":
                            key = ("H", n, piece[2], 0)
                            dve.wait_ge(s_t, tuse[key] + 1)
                            if 2 * n + piece[2] >= 2:
                                dve.wait_ge(s_pv, 2 * n + piece[2] - 1)
                            dve.tensor_copy(PTW[:, piece[2], 0],
                                            ps[:, tbank(key), :].rearrange("p (k n) -> p k n", k=4)
                                            ).then_inc(t_read(key)[0], 1)
                        elif kind == "I" and piece[2] == 1:
                            dve.wait_ge(s_oh, n + 1)
                            dve.tensor_tensor(ot[1][:, :, :], ps[:, 7, :].rearrange("p (h n) -> p h n", h=4),
                                              ot[0][:, :, :], ALU.subtract).then_inc(s_ol, 1)
                        elif kind == "J":
                            dve.wait_ge(s_wo, n + 1)
                            dve.tensor_tensor(U[:, w, :], ps[:, 7, 0:DIM], U[:, w, :], ALU.add).then_inc(s_res, 1)
                        elif kind == "L":
                            l, g = piece[1:]
                            q = l * NG + g
                            dve.wait_ge(s_xs[q], 16 * (2 * GW - (g == 0)))
                            dve.wait_ge(s_res, l * NT + GW * (g + 1))
                            for w in range(g * GW, (g + 1) * GW):
                                dve.bn_stats(st[:, w, 0, :], U[:, w, 0:P])
                                last = dve.bn_stats(st[:, w, 1, :], XS[:, w, :])
                            last.then_inc(s_bn, 1)
                            dve.wait_ge(s_bn, q + 1)
                            for w in range(g * GW, (g + 1) * GW):
                                last = dve.bn_aggr(mv[:, w, :], st[:, w, :, :].rearrange("p a b -> p (a b)"))
                            last.then_inc(s_lnmv, 1)
                            dve.wait_ge(s_lnr, q + 1)
                            for p in range(2 * g, 2 * g + 2):
                                if l * 4 + p >= 2:
                                    pl, pp = divmod(l * 4 + p - 2, 4)
                                    dve.wait_ge(s_t, tuse[("N", pl, pp)] + 1)
                                for i in range(2):
                                    w = 2 * p + i
                                    dve.tensor_scalar(XN[:, p % 2, i, 0:P], U[:, w, 0:P], mv[:, w, 0:1],
                                                      rstd[:, w:w + 1], ALU.subtract, ALU.mult)
                                    last = dve.tensor_scalar(XN[:, p % 2, i, P:DIM], XS[:, w, :], mv[:, w, 0:1],
                                                             rstd[:, w:w + 1], ALU.subtract, ALU.mult)
                                last.then_inc(s_xnw, 1)
                        elif kind == "W":
                            l, g, j = piece[1:]
                            v = (l * NG + g) * (NJ + 1) + j
                            dve.wait_ge(s_g, v + 1)
                            if j < NJ:
                                dve.wait_ge(s_w1, (l * NG + g) * NJ + j + 1)
                            if v >= 2:
                                dve.wait_ge(s_ul, v - 1)
                            rows = P if j < NJ else TAIL
                            src = ps[0:rows, 2 * (v % 2) + (1 if j < NJ else 0), :]
                            dve.scalar_tensor_tensor(out=UB[0:rows, v % 2, :], in0=src,
                                                     scalar=bias1[0:rows, l, min(2 * j + 1, 2 * NJ):min(2 * j + 1, 2 * NJ) + 1],
                                                     in1=GB[0:rows, v % 2, :], op0=ALU.add,
                                                     op1=ALU.mult).then_inc(s_ust, 1)
                        elif kind == "Y":
                            dve.wait_ge(s_w2, n + 1)
                            dve.tensor_tensor(U[:, w, :], ps[:, (4, 7)[w % 2], 0:DIM], U[:, w, :],
                                              ALU.add).then_inc(s_u2, 1)

                @block.gpsimd
                def _(pool):
                    def root(count, lo, hi):
                        pool.tensor_scalar(veps[:, lo:hi], mv[:, lo:hi, 1], EPS, None, ALU.add).then_inc(s_v2, 1)
                        pool.wait_ge(s_v2, count)
                        return pool.tensor_tensor(rstd[:, lo:hi], veps[:, lo:hi], neg_half[:, 0:hi - lo], ALU.pow)

                    for g in range(2):
                        pool.wait_ge(s_mv, g + 1)
                        root(g + 1, 4 * g, 4 * g + 4).then_inc(s_rstd, 1)
                    for t in range(NT + 2):
                        if t % 2 == 0 and t // 2 < NT // 2:
                            p = t // 2
                            pool.wait_ge(s_hh, p + 1)
                            pool.tensor_tensor(ht[1][:, :, 1 + p * 256:1 + (p + 1) * 256], hf1[:, p % 2],
                                               ht[0][:, :, 1 + p * 256:1 + (p + 1) * 256],
                                               ALU.subtract).then_inc(s_hl, 1)
                        if t >= 2:
                            i = t - 2
                            pool.wait_ge(s_m1a, i + 1)
                            a = ra[:, i % 2].rearrange("p c s n -> p (c s n)")
                            pool.tensor_tensor(a, a, rb[:, i % 2].rearrange("p c s n -> p (c s n)"),
                                               ALU.add).then_inc(s_rot, 1)
                    pool.wait_ge(s_mod, 16 * (2 * NC * HPC + 1))
                    for i in range(NT):
                        pool.wait_ge(s_yo, i + 1)
                        pool.tensor_tensor(X[:, i, :], X[:, i, :], yt[:, i % 2, :], ALU.add).then_inc(s_x2, 1)
                        if i in (4, NT - 1):
                            g = 0 if i == 4 else 1
                            pool.wait_ge(s_mv, 3 + g)
                            root(3 + g, 4 * g, 4 * g + 4).then_inc(s_rstd, 1)
                            for t in range(4 * g, 4 * g + 4):
                                pool.wait_ge(s_u0a, t + 1)
                                pool.tensor_tensor(U[:, t, :], U[:, t, :], modb[:, 2, :], ALU.mult).then_inc(s_u0b, 1)
                            for t in range(4 * g, 4 * g + 4):
                                pool.wait_ge(s_u0b, t + 1)
                                pool.tensor_tensor(U[:, t, :], U[:, t, :], modb[:, 1, :], ALU.add).then_inc(s_u0, 1)

                    roots = 4
                    for piece in PIECES:
                        kind, n = piece[0], piece[1]
                        l, w = n // NT, n % NT
                        if kind == "E" and piece[2] == 1:
                            pool.wait_ge(s_ss, n + 1)
                            pool.tensor_scalar(ssm, ss[:, n % 2, :], 1e-24, None, ALU.max).then_inc(s_rm, 1)
                            pool.wait_ge(s_rm, n + 1)
                            pool.tensor_tensor(rinv[:, n % 2, :], ssm, neg_half[:, 0:16], ALU.pow).then_inc(s_rinv, 1)
                            pool.wait_ge(s_m, n + 1)
                            pool.tensor_tensor(M1[:, n % 2, :], M1[:, n % 2, :], M2, ALU.add).then_inc(s_add, 1)
                            pool.wait_ge(s_add, n + 1)
                            pool.wait_ge(s_rinv, n + 1)
                            kk = M1[:, n % 2, INNER:2 * INNER].rearrange("p (h d) -> p h d", d=DH)
                            pool.tensor_tensor(kk, kk, rinv[:, n % 2, 8:16].unsqueeze(2).broadcast_to((P, HEADS, DH)),
                                               ALU.mult).then_inc(s_rope, 1)
                        elif kind == "L":
                            l, g = piece[1:]
                            pool.wait_ge(s_lnmv, l * NG + g + 1)
                            roots += 1
                            root(roots, 4 * g, 4 * g + 4).then_inc(s_lnr, 1)
                        elif kind == "W":
                            l, g, j = piece[1:]
                            v = (l * NG + g) * (NJ + 1) + j
                            pool.wait_ge(s_uh, v + 1)
                            rows = P if j < NJ else TAIL
                            hi = uh[:, j, :] if j < NJ else u_tail[0][0:TAIL, :]
                            lo = ul[:, j, :] if j < NJ else u_tail[1][0:TAIL, :]
                            pool.tensor_tensor(lo, UB[0:rows, v % 2, :], hi, ALU.subtract).then_inc(s_ul, 1)
                        elif kind == "Y" and l == DEPTH - 1:
                            pool.wait_ge(s_u2, n + 1)
                            pool.tensor_tensor(U[:, w, :], U[:, w, :], modb[:, 3, :], ALU.mult).then_inc(s_fa, 1)
                            pool.wait_ge(s_fa, w + 1)
                            pool.tensor_tensor(U[:, w, :], U[:, w, :], X[:, w, :], ALU.add).then_inc(s_fin, 1)

            for s in names:
                nc.gpsimd.sem_clear(s)
            nc.all_engine_barrier()


ptg = [sum(k // 4 + 1 for k in range(i)) for i in range(NT + 1)]


def setup(nc, ctx, v):
    ps, ar_a, ar_b, ar_c, xu = v["ps"], v["ar_a"], v["ar_b"], v["ar_c"], v["xu"]
    wqkv_p, wo_p, w1_p, w2_p, bd_p = v["wqkv_p"], v["wo_p"], v["w1_p"], v["w2_p"], v["bd_p"]
    id_f, id_b, mask_t, xp_t, bias1 = v["id_f"], v["id_b"], v["mask_t"], v["xp_t"], v["bias1"]
    u_tail, ht, XS = v["u_tail"], v["ht"], v["XS"]
    sem = v["sem"]

    xu_f = xu[:, :, :, :].rearrange("p a t d -> p (a t d)")
    st_qkv = ar_a[:, 0:6144].rearrange("p (l c n) -> p l c n", l=DEPTH, c=NC)
    st_w2 = ar_b[:, 0:2560].rearrange("p (l j n) -> p l j n", l=DEPTH, j=NJ)
    st_w2t = ar_b[0:GT, 2560:3072].rearrange("p (l n) -> p l n", l=DEPTH)
    st_wo = ar_b[:, 3072:5120].rearrange("p (l c n) -> p l c n", l=DEPTH, c=4)
    st_w1 = [xu_f[:, 0:4 * HID].rearrange("p (c n) -> p c n", c=NC),
             ar_c[:, 0:4 * HID].rearrange("p (c n) -> p c n", c=NC)]
    o = 4 * HID
    w_rep = xu_f[:, o:o + 768].rearrange("p (s n) -> p s n", s=3)
    cT = xu_f[:, o + 768:o + 784].rearrange("p (c n) -> p c n", c=NC)
    c_e = xu_f[:, o + 784:o + 800].rearrange("p (c n) -> p c n", c=NC)
    silu = xu_f[:, o + 800:o + 816].rearrange("p (c n) -> p c n", c=NC)
    lgb = xu_f[:, o + 816:o + 824].rearrange("p (k l c) -> p k l c", k=2, l=DEPTH)
    qks = xu_f[:, o + 824:o + 824 + 512].rearrange("p (l k d) -> p l k d", l=DEPTH, k=4)
    w_mod = ar_a[:, 0:3072].rearrange("p (c n) -> p c n", c=NC)
    mrow = ar_a[0:BATCH, 3072:4608]
    mtmp = ar_a[0:BATCH, 4608:5120]
    xp_base = ar_a[:, 3072:3072 + 2048].rearrange("p (t k d) -> p t k d", t=NT, k=4)
    bd_f = ar_a[:, 5120:5120 + 768].rearrange("p (c s n) -> p c s n", c=NC, s=3)
    m_f = ar_b[:, 0:1024].rearrange("p (a n) -> p a n", a=2)

    l_qkv, l_wo, l_w1, l_w2, l_rep, l_small, l_tab = (sem(f"load_{n}") for n in
                                                      ("qkv", "wo", "w1", "w2", "rep", "small", "tables"))
    z_id, z_id2, z_w2, z_mask, z_mask2, z_rest = (sem(n) for n in ("id_zero", "id_ready", "w2_tail_zero", "mask_zero",
                                                                   "mask_ready", "rest_filled"))
    z_bias, z_tail = sem("bias_zero"), sem("w1_tail_zero")
    hi_done, lo_done = sem("setup_hi"), sem("setup_lo")
    lbw, w1s, bias_done = sem("lb_w1_done"), sem("w1_scaled"), sem("bias_done")
    bd_a, bd_b = sem("bd_first"), sem("bd_ready")
    e_done, e1_done, e2_done, e3_done = sem("silu_exp"), sem("silu_plus1"), sem("silu_recip"), sem("silu_ready")
    l_mod, l_xp, mm_done, row_done, row_t, mod_done, mod_out, xp_done = (sem(n) for n in (
        "load_wmod", "load_xpos", "mod_product", "mod_row", "mod_tmp", "mod_changed", "mod_stored", "xpos_scaled"))
    mask_used = sem("masks_cast")

    block = nc.Block()
    with block:
        @block.sync
        def _(sp):
            for l in range(DEPTH):
                sp.dma_start(st_w1[l], v["w1"][l].rearrange("(c p) n -> p c n", p=P)).then_inc(l_w1, 16)
            for k, src in enumerate((v["ln_g"], v["ln_b"])):
                for l in range(DEPTH):
                    sp.dma_start(lgb[:, k, l, :], src[l].rearrange("(c p) -> p c", p=P)).then_inc(l_small, 16)
            for c in range(NC):
                sp.dma_start(cT[:, c, :], v["cond"][:, c * P:(c + 1) * P].rearrange("b p -> p b")).then_inc(l_small, 16)
            sp.wait_ge(z_bias, 1)
            for l in range(DEPTH):
                for i, base in enumerate((HID, 0)):
                    sp.dma_start(bias1[:, l, i:2 * NJ:2],
                                 v["b1"][l, base:base + NJ * P].rearrange("(j p) -> p j", p=P)).then_inc(l_small, 16)
                    r = (GT, 0)[i]
                    sp.dma_start(bias1[r:r + TAIL, l, 2 * NJ:2 * NJ + 1],
                                 v["b1"][l, base + NJ * P:base + HID].unsqueeze(1)).then_inc(l_small, 16)
            for l in range(DEPTH):
                for k, src in enumerate((v["q_scale"], v["k_scale"])):
                    sp.dma_start(qks[:, l, k, :], src[l].partition_broadcast(P)).then_inc(l_small, 16)
                    for e in range(2):
                        sp.dma_start(qks[:, l, 2 + k, 32 * e:32 * e + 32],
                                     src[l, 32 - 32 * e:64 - 32 * e].partition_broadcast(P)).then_inc(l_small, 16)
            sp.wait_ge(hi_done, 2)
            sp.wait_ge(lo_done, 2)
            sp.dma_start(w_mod, v["wmod"].rearrange("(c p) n -> p c n", p=P)).then_inc(l_mod, 16)
            sp.wait_ge(mod_done, 1)
            sp.dma_start(v["mod_rows"], mrow).then_inc(mod_out, 16)
            sp.wait_ge(mod_out, 16)
            sp.dma_start(xp_base, v["xpos"]).then_inc(l_xp, 16)
            sp.wait_ge(l_tab, 32)

        @block.scalar
        def _(act):
            act.dma_start(st_qkv, v["wqkv"].rearrange("l (c p) n -> p l c n", p=P)).then_inc(l_qkv, 16)
            act.dma_start(st_wo, v["wo"].rearrange("l (c p) n -> p l c n", p=P)).then_inc(l_wo, 16)
            act.wait_ge(z_w2, 1)
            for l in range(DEPTH):
                act.dma_start(st_w2[:, l], v["w2"][l, 0:NJ * P].rearrange("(j p) n -> p j n", p=P)).then_inc(l_w2, 16)
                act.dma_start(st_w2t[0:TAIL, l, :], v["w2"][l, NJ * P:HID, :]).then_inc(l_w2, 16)
                act.dma_start(st_w2t[TAIL:TAIL + 1, l, :], v["b2"][l:l + 1, :]).then_inc(l_w2, 16)
            for s, src in enumerate((v["w_q"], v["w_k"], v["w_v"])):
                for h in range(HPC):
                    act.dma_start(w_rep[h * AD:(h + 1) * AD, s, :], src.rearrange("q d h -> q (d h)")).then_inc(l_rep, 16)
            act.dma_start(v["cos_t"][:, :, :, :], v["rope_cos"]).then_inc(l_tab, 16)
            act.dma_start(v["sin_t"][:, :, :, :], v["rope_sin"]).then_inc(l_tab, 16)
            act.wait_ge(l_qkv, 16)
            for l in range(DEPTH):
                act.activation(wqkv_p[0][:, l], st_qkv[:, l], ACT.Copy).then_inc(hi_done, 1)
            act.wait_ge(l_wo, 16)
            for l in range(DEPTH):
                act.activation(wo_p[0][:, l], st_wo[:, l], ACT.Copy).then_inc(hi_done, 1)
            act.wait_ge(l_w2, 16 * 3 * DEPTH)
            for l in range(DEPTH):
                act.activation(w2_p[0][:, l, 0:NJ, :], st_w2[:, l], ACT.Copy)
                act.activation(w2_p[0][0:GT, l, NJ, :], st_w2t[:, l, :], ACT.Copy).then_inc(hi_done, 1)
            act.wait_ge(z_tail, 1)
            for l in range(DEPTH):
                act.wait_ge(w1s, l + 1)
                for dst, src in w1_blocks(w1_p[0], st_w1, l):
                    last = act.activation(dst, src, ACT.Copy)
                last.then_inc(hi_done, 1)
            act.wait_ge(bd_b, 1)
            act.activation(bd_p[0][:, :, :, :], bd_f, ACT.Copy).then_inc(hi_done, 1)
            act.wait_ge(l_small, 16 * N_SMALL)
            act.activation(c_e, cT, ACT.Exp, scale=-1.0).then_inc(e_done, 1)
            act.wait_ge(mm_done, 1)
            act.activation(mrow, ps[0:BATCH, 4:7, :].rearrange("p a n -> p (a n)"), ACT.Copy).then_inc(row_done, 1)

        @block.vector
        def _(dve):
            dve.memset(bias1[:, :, :], 0.0).then_inc(z_bias, 1)
            dve.memset(st_w2t, 0.0).then_inc(z_w2, 1)
            for q in w1_p:
                last = dve.memset(q[:, :, :, 2 * NJ, :], 0.0)
            last.then_inc(z_tail, 1)
            dve.memset(v["neg_half"][:, :], -0.5)
            dve.memset(u_tail[0][:, :], 1.0)
            dve.memset(u_tail[1][:, :], 0.0)
            for q in ht:
                dve.memset(q[:, :, :], 0.0)
            dve.memset(XS[:, 0, :], 0.0).then_inc(z_rest, 1)
            for l in range(DEPTH):
                dve.wait_ge(hi_done, l + 1)
                dve.tensor_tensor(wqkv_p[1][:, l], st_qkv[:, l], wqkv_p[0][:, l], ALU.subtract).then_inc(lo_done, 1)
            for l in range(DEPTH):
                dve.wait_ge(hi_done, DEPTH + l + 1)
                dve.tensor_tensor(wo_p[1][:, l], st_wo[:, l], wo_p[0][:, l], ALU.subtract)
            for l in range(DEPTH):
                dve.wait_ge(hi_done, 2 * DEPTH + l + 1)
                dve.tensor_tensor(w2_p[1][:, l, 0:NJ, :], st_w2[:, l], w2_p[0][:, l, 0:NJ, :], ALU.subtract)
                dve.tensor_tensor(w2_p[1][0:GT, l, NJ, :], st_w2t[:, l, :], w2_p[0][0:GT, l, NJ, :],
                                  ALU.subtract).then_inc(lo_done, 1)
            dve.wait_ge(l_small, 16 * N_SMALL)
            dve.wait_ge(lbw, 1)
            for l in range(DEPTH):
                for c in range(NC):
                    last = dve.tensor_scalar(st_w1[l][:, c, :], st_w1[l][:, c, :], lgb[:, 0, l, c:c + 1], None, ALU.mult)
                last.then_inc(w1s, 1)
            dve.wait_ge(z_bias, 1)
            for l in range(DEPTH):
                k = l * NB1
                dve.tensor_tensor(bias1[:, l, 0:2 * NJ], ps[:, 0, k:k + 2 * NJ], bias1[:, l, 0:2 * NJ], ALU.add)
                k += 2 * NJ
                for r in (0, GT):
                    last = dve.tensor_tensor(bias1[r:r + TAIL, l, 2 * NJ:2 * NJ + 1], ps[r:r + TAIL, 0, k:k + 1],
                                             bias1[r:r + TAIL, l, 2 * NJ:2 * NJ + 1], ALU.add)
            last.then_inc(bias_done, 1)
            for l in range(DEPTH):
                dve.wait_ge(hi_done, 3 * DEPTH + l + 1)
                for (dst, src), (hi, _) in zip(w1_blocks(w1_p[1], st_w1, l), w1_blocks(w1_p[0], st_w1, l)):
                    last = dve.tensor_tensor(dst, src, hi, ALU.subtract)
                last.then_inc(lo_done, 1)
            dve.wait_ge(hi_done, 4 * DEPTH + 1)
            dve.tensor_tensor(bd_p[1][:, :, :, :], bd_f, bd_p[0][:, :, :, :], ALU.subtract).then_inc(lo_done, 1)
            dve.wait_ge(e_done, 1)
            dve.tensor_scalar(c_e, c_e, 1.0, None, ALU.add).then_inc(e1_done, 1)
            dve.wait_ge(e1_done, 1)
            dve.reciprocal(silu, c_e).then_inc(e2_done, 1)
            dve.wait_ge(e2_done, 1)
            dve.tensor_tensor(silu, silu, cT, ALU.mult).then_inc(e3_done, 1)
            dve.wait_ge(row_done, 1)
            dve.tensor_scalar(mrow[:, DIM:2 * DIM], mrow[:, DIM:2 * DIM], 1.0, None, ALU.add)
            dve.tensor_scalar(mrow[:, 4 * DIM:5 * DIM], mrow[:, 4 * DIM:5 * DIM], 1.0, None, ALU.add)
            gates = [mrow[:, k * DIM:(k + 1) * DIM] for k in (2, 5)]
            tmps = [mtmp[:, k * DIM:(k + 1) * DIM] for k in range(2)]
            for g, t in zip(gates, tmps):
                last = dve.tensor_scalar(t, g, 0.0, 2.0, ALU.is_ge, ALU.mult)
            last.then_inc(row_t, 1)
            dve.wait_ge(row_t, 1)
            for g, t in zip(gates, tmps):
                last = dve.tensor_scalar(t, t, -1.0, None, ALU.add)
            last.then_inc(row_t, 1)
            dve.wait_ge(row_t, 2)
            for g, t in zip(gates, tmps):
                last = dve.tensor_tensor(g, g, t, ALU.mult)
            last.then_inc(row_t, 1)
            dve.wait_ge(row_t, 3)
            for g, t in zip(gates, tmps):
                last = dve.scalar_tensor_tensor(out=g, in0=g, scalar=0.25, in1=t, op0=ALU.max, op1=ALU.mult)
            last.then_inc(mod_done, 1)
            dve.wait_ge(z_id2, 1)
            dve.tensor_copy(id_b[:, :], id_f[:, :])
            dve.wait_ge(z_mask2, 3)
            dve.tensor_copy(mask_t[:, :, :], m_f).then_inc(mask_used, 1)
            dve.wait_ge(l_xp, 16)
            for l in range(DEPTH):
                dve.tensor_tensor(xp_t[:, l].rearrange("p t k d -> p t (k d)"), xp_base.rearrange("p t k d -> p t (k d)"),
                                  qks[:, l].rearrange("p k d -> p (k d)").unsqueeze(1).broadcast_to((P, NT, 4 * DH)),
                                  ALU.mult).then_inc(xp_done, 1)

        @block.gpsimd
        def _(pool):
            pool.memset(id_f[:, :], 0.0).then_inc(z_id, 1)
            pool.wait_ge(z_id, 1)
            pool.affine_select(out=id_f[:, :], in_=id_f[:, :], compare_op=ALU.not_equal, fill=1.0, base=0,
                               pattern=[[-1, P]], channel_multiplier=1).then_inc(z_id2, 1)
            pool.wait_ge(l_rep, 16 * 3 * HPC)
            pool.wait_ge(lo_done, 2)
            for c in range(NC):
                for s in range(3):
                    last = pool.affine_select(out=bd_f[:, c, s, :].rearrange("p (d h) -> p d h", h=HPC),
                                              in_=w_rep[:, s, :].rearrange("p (d h) -> p d h", h=AH)[:, :, c * HPC:(c + 1) * HPC],
                                              compare_op=ALU.is_ge, fill=0.0, base=0,
                                              pattern=[[0, AD], [-AD, HPC]], channel_multiplier=1)
            last.then_inc(bd_a, 1)
            pool.wait_ge(bd_a, 1)
            for c in range(NC):
                for s in range(3):
                    t = bd_f[:, c, s, :].rearrange("p (d h) -> p d h", h=HPC)
                    last = pool.affine_select(out=t, in_=t, compare_op=ALU.is_ge, fill=0.0, base=AD - 1,
                                              pattern=[[0, AD], [AD, HPC]], channel_multiplier=-1)
            last.then_inc(bd_b, 1)
            pool.wait_ge(lo_done, 2 + DEPTH)
            pool.memset(m_f, 0.0).then_inc(z_mask, 1)
            pool.wait_ge(z_mask, 1)
            m4 = m_f.rearrange("p a (i k n) -> p a i k n", i=2, k=2)
            pool.affine_select(out=m4[:, 0, :, 0, :], in_=m4[:, 0, :, 0, :], compare_op=ALU.is_ge, fill=NEG, base=0,
                               pattern=[[0, 2], [1, P]], channel_multiplier=-1).then_inc(z_mask2, 1)
            pool.memset(m4[:, 1, :, 0, :], NEG).then_inc(z_mask2, 1)
            for a in range(2):
                last = pool.affine_select(out=m4[:, a, :, 1, :], in_=m4[:, a, :, 1, :], compare_op=ALU.is_ge, fill=NEG,
                                          base=0, pattern=[[0, 2], [-1, P]], channel_multiplier=1)
            last.then_inc(z_mask2, 1)

        @block.tensor
        def _(pe):
            pe.wait_ge(l_w1, 16 * DEPTH)
            pe.wait_ge(l_small, 16 * N_SMALL)
            for l in range(DEPTH):
                for j in range(NB1 + 1):
                    if j < 2 * NJ:
                        a, r, m = (HID, 0)[j % 2] + (j // 2) * P, 0, P
                    else:
                        a, r, m = ((0, HID)[j - 2 * NJ] + NJ * P, (0, GT)[j - 2 * NJ], TAIL)
                    k = l * NB1 + min(j, 2 * NJ)
                    for c in range(NC):
                        last = pe.matmul(ps[r:r + m, 0, k:k + 1], st_w1[l][:, c, a:a + m], lgb[:, 1, l, c:c + 1],
                                         start=(c == 0), stop=(c == NC - 1))
            last.then_inc(lbw, 1)
            pe.wait_ge(e3_done, 1)
            pe.wait_ge(l_mod, 16)
            for j in range(3):
                for c in range(NC):
                    last = pe.matmul(ps[0:BATCH, 4 + j, :], silu[:, c, :], w_mod[:, c, j * 512:(j + 1) * 512],
                                     start=(c == 0), stop=(c == NC - 1))
            last.then_inc(mm_done, 1)


def w1_blocks(dst, stage, l):
    for i, base in enumerate((HID, 0)):
        for c in range(NC):
            yield (dst[:, l, c, i:2 * NJ:2, :],
                   stage[l][:, c, base:base + NJ * P].rearrange("p (j n) -> p j n", n=P))
        r = (GT, 0)[i]
        yield dst[:, l, :, 2 * NJ, r:r + TAIL], stage[l][:, :, base + NJ * P:base + HID]


N_SMALL = 2 * DEPTH + NC + 4 * DEPTH + 6 * DEPTH


def shape_tables():
    import numpy as np

    f = np.float32
    half = DIM // 2
    inv = f(1.0) / (f(10000.0) ** (np.arange(half, dtype=f) / f(half)))
    ang = np.arange(SEQ, dtype=f)[:, None] * inv[None, :]

    def lay(a):
        return np.ascontiguousarray(a.reshape(NT, P, AD, NC, HPC // 2).transpose(1, 0, 3, 2, 4).reshape(P, NT, NC, P // 2))

    idx = np.arange(0, DH, 2, dtype=f)
    inv2 = f(1.0) / (f(10000.0) ** (idx / f(DH)))
    t = np.arange(SEQ, dtype=f)
    fr = t[:, None] * inv2[None, :]
    fr = np.concatenate([fr, fr], -1)
    base = (idx + f(0.4 * DH)) / f(1.4 * DH)
    power = (t - f(SEQ // 2)) / f(64.0)
    sc = base[None, :] ** power[:, None]
    sc = np.concatenate([sc, sc], -1)
    cos, sin = np.cos(fr), np.sin(fr)
    sin[:, :DH // 2] *= f(-1.0)
    qk_scale = f(8.0)
    tab = np.stack([cos * sc * qk_scale, cos / sc, sin * sc * qk_scale, sin / sc], 1).astype(f)
    xpos = np.ascontiguousarray(tab.reshape(NT, P, 4, DH).transpose(1, 0, 2, 3))
    return lay(np.cos(ang).astype(f)), lay(np.sin(ang).astype(f)), xpos


_INS = ['L0_attn_x', 'L0_attn_w_q', 'L0_attn_w_k', 'L0_attn_w_v', 'L0_ffn_wqkv', 'L0_ffn_q_scale', 'L0_ffn_k_scale',
        'L0_ffn_wo', 'L0_ffn_ln_g', 'L0_ffn_ln_b', 'L0_ffn_w1', 'L0_ffn_b1', 'L0_ffn_w2', 'L0_ffn_b2', 'L0_c', 'L0_wmod']


def kernel(**inputs):
    import numpy as _np
    import concourse.bacc as _bacc
    from concourse import mybir as _mybir
    from concourse.bass_utils import run_bass_kernel_spmd as _run

    nc = _bacc.Bacc("TRN2", target_bir_lowering=False, num_devices=1)
    arrays, args = {}, []
    tables = dict(zip(("rope_cos", "rope_sin", "xpos"), shape_tables()))
    for name in _INS + list(tables):
        a = _np.ascontiguousarray(inputs[name] if name in inputs else tables[name])
        arrays[f"in_{name}_dram"] = a
        args.append(nc.dram_tensor(f"in_{name}_dram", a.shape, _mybir.dt.from_np(a.dtype), kind="ExternalInput").ap())
    out = nc.dram_tensor("out_0_dram", (BATCH, SEQ, DIM), F32, kind="ExternalOutput").ap()
    adaln_kernel(nc, *args, out)
    r = _run(nc, [arrays], core_ids=[0])
    return r.results[0]["out_0_dram"]
```

```python
from contextlib import ExitStack

import concourse.bass as bass
from concourse import mybir

F32 = mybir.dt.float32
F16 = mybir.dt.float16
BF16 = mybir.dt.bfloat16
ALU = mybir.AluOpType
ACT = mybir.ActivationFunctionType
AX = mybir.AxisListType.X

P = 128
EPS = 1e-5
NEG = -1.0e30
BATCH, SEQ, DIM = 8, 1024, 256
NT = SEQ // P
NC = DIM // P
AH = 16
AD = DIM // AH
HPC = AH // NC
DEPTH = 2
HEADS, DH = 8, 64
INNER = HEADS * DH
HID = DIM * 4 * 2 // 3
NJ = HID // P
TAIL = HID - NJ * P
NB1 = 2 * NJ + 1
GT = 64
NG = 2
GW = NT // NG
GAMMA = 1.0 / DIM ** 0.5


def adaln_kernel(nc, x, w_q, w_k, w_v, wqkv, q_scale, k_scale, wo, ln_g, ln_b, w1, b1, w2, b2,
                 cond, wmod, rope_cos, rope_sin, xpos, out):
    mod_rows = nc.dram_tensor("mod_rows", [BATCH, 6 * DIM], F32, kind="Internal").ap()

    with ExitStack() as ctx:
        ctx.enter_context(nc.allow_non_contiguous_dma(reason="small vectors and shifted rows"))
        def sb(name, shape, dt=F32):
            return ctx.enter_context(nc.sbuf_tensor(name, shape, dt))

        names = []

        def sem(name):
            s = ctx.enter_context(nc.semaphore(name))
            names.append(s)
            return s

        ps = ctx.enter_context(nc.psum_tensor("ps", [P, 8, 512], F32))

        wqkv_p = [sb(f"wqkv_{s}", [P, DEPTH, NC, 3 * INNER], F16) for s in ("hi", "lo")]
        wo_p = [sb(f"wo_{s}", [P, DEPTH, INNER // P, DIM], F16) for s in ("hi", "lo")]
        w1_p = [sb(f"w1_{s}", [P, DEPTH, NC, NB1, P], F16) for s in ("hi", "lo")]
        w2_p = [sb(f"w2_{s}", [P, DEPTH, NJ + 1, DIM], F16) for s in ("hi", "lo")]
        bd_p = [sb(f"bd_{s}", [P, NC, 3, P], F16) for s in ("hi", "lo")]
        cos_t = sb("cos_t", [P, NT, NC, P // 2])
        sin_t = sb("sin_t", [P, NT, NC, P // 2])
        xp_t = sb("xp_t", [P, DEPTH, NT, 4, DH])
        mask_t = sb("mask_t", [P, 2, 512], BF16)
        id_b = sb("id_b", [P, P], BF16)
        id_f = sb("id_f", [P, P])
        bias1 = sb("bias1", [P, DEPTH, NB1])
        u_tail = [sb(f"u_tail_{s}", [GT, 512], F16) for s in ("hi", "lo")]
        neg_half = sb("neg_half", [P, 16])
        modc_all = sb("modc_all", [P, BATCH, 2 * NC])

        xu = sb("xu", [P, 2, NT, DIM])
        X, U = xu[:, 0], xu[:, 1]
        modb = sb("modb", [P, 4, DIM])
        modc = sb("modc", [P, 2 * NC])
        ht = [sb(f"ht_{s}", [P, NC, SEQ + 1], F16) for s in ("hi", "lo")]
        st = sb("st", [P, 8, 2, 6])
        mv = sb("mv", [P, NT, 2])
        rstd = sb("rstd", [P, NT])
        veps = sb("veps", [P, NT])

        ar_a = sb("ar_a", [P, 26 * 256])
        QK1 = ar_a[:, 0:4096].rearrange("p (c s n) -> p c s n", c=NC, s=2)
        V1 = ar_a[:, 4096:6144].rearrange("p (t n) -> p t n", t=NT)
        KT = ar_a[:, 0:1536].rearrange("p (r h n) -> p r h n", r=3, h=4)
        QT = ar_a[:, 1536:2560].rearrange("p (r h n) -> p r h n", r=2, h=4)
        V = ar_a[:, 2560:4608].rearrange("p (r n) -> p r n", r=4)
        RAW = ar_a[:, 4608:6656].rearrange("p (r s n) -> p r s n", r=2, s=2)
        ar_b = sb("ar_b", [P, 20 * 256])
        P1 = ar_b[:, 0:2048].rearrange("p (r n) -> p r n", r=2)
        PT1 = ar_b[:, 2048:4096].rearrange("p (r k n) -> p r k n", r=2, k=NT)
        PW = ar_b[:, 0:2048].rearrange("p (f x k n) -> p f x k n", f=2, x=2, k=2)
        PTW = ar_b[:, 2048:4096].rearrange("p (f x k n) -> p f x k n", f=2, x=2, k=4)
        GB = ar_a[:, 4608:5632].rearrange("p (r n) -> p r n", r=2)
        UB = ar_a[:, 5632:6656].rearrange("p (r n) -> p r n", r=2)
        at = [4096, 4608] + [512 * j for j in range(NJ - 2)]
        uh = [ar_b[:, a:a + 256].bitcast(F16) for a in at]
        ul = [ar_b[:, a + 256:a + 512].bitcast(F16) for a in at]
        ar_c = sb("ar_c", [P, 16 * 256])
        M1 = ar_c[:, 0:2048].rearrange("p (r n) -> p r n", r=2)
        M2 = ar_c[:, 2048:3072]
        SQ = ar_c[:, 3072:4096]
        xn1 = ar_c[:, 0:1024].rearrange("p (r t c n) -> p r t c n", r=2, t=2, c=NC)
        hf1 = ar_c[:, 1024:2048].rearrange("p (r c n) -> p r c n", r=2, c=NC)
        ra = ar_c[:, 2048:3072].rearrange("p (r c s n) -> p r c s n", r=2, c=NC, s=2)
        rb = ar_c[:, 3072:4096].rearrange("p (r c s n) -> p r c s n", r=2, c=NC, s=2)
        XN = sb("XN", [P, 2, 2, DIM])
        XS = sb("XS", [P, NT, P])
        ot = [sb(f"ot_{s}", [P, 4, P], F16) for s in ("hi", "lo")]
        small = sb("small", [P, 160])
        mx1, nm1, sm1, rs1 = (small[:, 8 * i:8 * i + 8] for i in range(4))
        ss = small[:, 32:64].rearrange("p (r n) -> p r n", r=2)
        ssm = small[:, 64:80]
        rinv = small[:, 80:112].rearrange("p (r n) -> p r n", r=2)
        mxw = small[:, 112:120]
        nbw = small[:, 120:136].rearrange("p (r n) -> p r n", r=2)
        smw = small[:, 136:152].rearrange("p (r n) -> p r n", r=2)
        rsw = small[:, 152:156]
        yt = sb("yt", [P, 2, DIM])

        def mm3(pe, o, a, b, start, stop):
            pe.matmul(o, a[0], b[0], start=start, stop=False)
            pe.matmul(o, a[0], b[1], start=False, stop=False)
            return pe.matmul(o, a[1], b[0], start=False, stop=stop)

        setup(nc, ctx, locals())

        ctx2 = ctx.enter_context(ExitStack())
        names.clear()
        s_x = [sem(f"x_loaded{p}") for p in range(NT // 2)]
        s_mod = sem("mod_loaded")
        s_bst, s_mv, s_rstd = sem("bn_done"), sem("meanvar_ready"), sem("rstd_ready")
        s_xn, s_xnT, s_hh, s_hl = sem("xn_ready"), sem("xn_transposed"), sem("h_hi_ready"), sem("h_lo_ready")
        s_proj, s_m1a, s_v1, s_rot = sem("proj_done"), sem("rope_products"), sem("v_copied"), sem("rope_done")
        s_qkt, s_qk = sem("qk_transposed"), sem("qk_copied")
        s_s, s_mx, s_nm, s_e1 = sem("scores_done"), sem("rowmax_done"), sem("negmax_ready"), sem("probs_ready")
        s_ptr, s_pte, s_y, s_rs, s_yo, s_x2 = (sem("probsT_done"), sem("probsT_copied"), sem("attn_out_done"),
                                               sem("rowsum_inverse"), sem("attn_out_scaled"), sem("x_updated"))
        s_u0a, s_u0b, s_u0 = sem("ln2_ready"), sem("ln2_scaled"), sem("ffn_input_ready")
        s_t = sem("transposes_done")
        s_tf = [sem(f"transpose_bank{i}_read") for i in range(2)]
        s_dh = sem("hT_hi_ready")
        s_qkv, s_ev = sem("qkv_bank_done"), sem("qkv_bank_copied")
        s_sq, s_ss, s_rm, s_rinv = sem("squares_ready"), sem("sumsq_ready"), sem("sumsq_clipped"), sem("inverse_norms")
        s_m, s_add, s_rope = sem("xpos_products"), sem("xpos_sum"), sem("xpos_ready")
        s_sim, s_mxw, s_nb, s_exp = sem("sim_bank_done"), sem("sim_max"), sem("sim_negmax"), sem("sim_bank_exp")
        s_rsw, s_pn, s_pv = sem("prob_inverse_sums"), sem("probs_normalised"), sem("pv_half_done")
        s_oh, s_ol, s_wo, s_res = sem("o_hi_ready"), sem("o_lo_ready"), sem("wo_done"), sem("attn_residual_done")
        s_xs = [sem(f"shifted_rows{p}") for p in range(DEPTH * NT // 2)]
        s_bn, s_lnmv, s_lnv, s_lnr, s_xnw = (sem("ln_stats"), sem("ln_meanvar"), sem("ln_var_eps"),
                                             sem("ln_rstd"), sem("ln_rows_ready"))
        s_nh = sem("ln_hi_ready")
        s_w1g, s_w1, s_g, s_ust, s_uh, s_ul = (sem("w1_gate_done"), sem("w1_done"), sem("gelu_ready"),
                                               sem("hidden_ready"), sem("hidden_hi"), sem("hidden_lo"))
        s_w2, s_u2 = sem("w2_done"), sem("mlp_residual_done")
        s_fa, s_fin, s_out = sem("final_scaled"), sem("final_ready"), sem("out_stored")
        s_v2, s_r2 = sem("var_eps_ready"), sem("pool_small")


        def window_step(l, s):
            proj, turn, att, back = (("E", s), ("F", s - 1), ("A", s - 2), ("J", s - 3))
            have = {k: 0 <= w < NT for k, w in (proj, turn, att, back)}
            e, t, a, j = (l * NT + w for _, w in (proj, turn, att, back))
            f = [("G", a, 0), ("G", a, 1), ("G", a, 2), ("n", a, 0), ("G", a, 3), ("J", j), ("E", e, 0),
                 ("H", a, 0), ("E", e, 1), ("n", a, 1), ("q", e), ("I", a, 0), ("H", a, 1), ("r", e), ("E", e, 2),
                 ("x", e, 0), ("F", t), ("x", e, 1), ("I", a, 1)]
            need = {"G": "A", "n": "A", "H": "A", "I": "A", "E": "E", "q": "E", "r": "E", "x": "E", "F": "F", "J": "J"}
            f = [q for q in f if have[need[q[0]]]]
            if s in (1, 3):
                f.append(("D", l, (s + 3) // 2))
            if s == 5:
                f.append(("L", l, 0))
            if s == 6:
                f.insert(f.index(("n", a, 1)) + 1, ("K", l, 0))
                f.append(("N", l, 0))
            if s == 7:
                f.insert(f.index(("J", j)) + 1, ("L", l, 1))
                f.append(("K", l, 1))
            if s == NT:
                f = [("G", a, 0), ("G", a, 1), ("G", a, 2), ("n", a, 0), ("G", a, 3), ("J", j), ("N", l, 1), ("F", t),
                     ("n", a, 1), ("H", a, 0), ("W", l, 0, 0), ("I", a, 0), ("H", a, 1), ("w", l, 0, 0), ("I", a, 1)]
            if s == NT + 1:
                f = [("G", a, 0), ("G", a, 1), ("G", a, 2), ("n", a, 0), ("G", a, 3), ("J", j), ("W", l, 0, 1),
                     ("n", a, 1), ("H", a, 0), ("H", a, 1), ("L", l, 2), ("w", l, 0, 1),
                     ("I", a, 0), ("I", a, 1), ("K", l, 2), ("W", l, 0, 2), ("J", a), ("w", l, 0, 2), ("N", l, 2)]
            return f

        def mlp_steps(l):

            def pair(g, j):
                return [("W", l, g, j), ("w", l, g, j)]

            f = pair(0, 3) + [("L", l, 3), ("K", l, 3)] + pair(0, 4) + [("N", l, 3)] + pair(0, 5)
            f += pair(1, 0) + pair(1, 1)
            f += [("Y", l * NT + w) for w in range(GW)]
            f += sum((pair(1, j) for j in range(2, NJ)), [])
            if l + 1 < DEPTH:
                f += [("D", l + 1, 0), ("D", l + 1, 1)]
            f += pair(1, NJ)
            if l + 1 < DEPTH:
                n = (l + 1) * NT
                f += [("E", n, 0), ("E", n, 1), ("q", n), ("E", n, 2), ("r", n)]
                f += [("Y", l * NT + GW), ("x", n, 0), ("Y", l * NT + GW + 1), ("x", n, 1)]
                f += [("Y", l * NT + w) for w in range(GW + 2, NT)]
            else:
                f += [("Y", l * NT + w) for w in range(GW, NT)]
            return f

        def schedule():
            f = [("D", 0, 0), ("D", 0, 1)]
            for l in range(DEPTH):
                for s in range(1 if l else 0, NT + 2):
                    f += window_step(l, s)
                f += mlp_steps(l)
            return f

        def plan_transposes(pieces):
            order = []
            for piece in pieces:
                if piece[0] in "DN":
                    order.append(piece)
                elif piece[0] in "FH":
                    order += [piece + (0,), piece + (1,)]
            return {key: u for u, key in enumerate(order)}

        PIECES = schedule()
        tuse = plan_transposes(PIECES)

        def w1_bank(l, g, j):
            return 0 if j % 2 or (g, j) == (0, 0) else 2

        def tbank(key):
            return 5 + tuse[key] % 2

        def t_read(key):
            return s_tf[tuse[key] % 2], tuse[key] // 2 + 1

        with nc.Fori(0, BATCH) as b:
            block = nc.Block()
            with block:

                @block.sync
                def _(sp):
                    for p in range(NT // 2):
                        sp.dma_start(X[:, 2 * p:2 * p + 2, :],
                                     x[b, 2 * p * P:(2 * p + 2) * P, :].rearrange("(t p) d -> p t d", p=P)
                                     ).then_inc(s_x[p], 16)
                    sp.dma_start(modc[:, :], modc_all[:, b, :]).then_inc(s_mod, 16)
                    sp.dma_start(modb[:, :, :],
                                 mod_rows[b, 2 * DIM:6 * DIM].rearrange("(k d) -> k d", k=4).partition_broadcast(P)
                                 ).then_inc(s_mod, 16)
                    for l in range(DEPTH):
                        for w in range(NT):
                            sp.wait_ge(s_res, l * NT + w + 1)
                            sp.dma_start(XS[1:P, w, :], U[0:P - 1, w, P:DIM]).then_inc(s_xs[l * 4 + w // 2], 16)
                            if w:
                                sp.dma_start(XS[0:1, w, :], U[P - 1:P, w - 1, P:DIM]
                                             ).then_inc(s_xs[l * 4 + w // 2], 16)
                    for w in range(NT):
                        sp.wait_ge(s_fin, w + 1)
                        sp.dma_start(out[b, w * P:(w + 1) * P, :], U[:, w, :]).then_inc(s_out, 16)
                    sp.wait_ge(s_out, 16 * NT)

                @block.tensor
                def _(pe):
                    def t_xn(p):
                        pe.wait_ge(s_xn, p + 1)
                        if p >= 1:
                            pe.wait_ge(s_hh, p)
                        for t in range(2):
                            for c in range(NC):
                                last = pe.transpose(ps[:, 5, c * 256 + t * P:c * 256 + (t + 1) * P],
                                                    xn1[:, p % 2, t, c, :], id_f[:])
                        last.then_inc(s_xnT, 1)

                    def proj(t):
                        pe.wait_ge(s_hl, t // 2 + 1)
                        if t >= 1:
                            pe.wait_ge(s_v1, t)
                        for c in range(NC):
                            h = [q[:, c, 1 + t * P:1 + (t + 1) * P] for q in ht]
                            w = [q[:, c, :, :].rearrange("p s n -> p (s n)") for q in bd_p]
                            last = mm3(pe, ps[:, c, 0:3 * P], h, w, True, True)
                        last.then_inc(s_proj, 1)

                    def t_qk(t):
                        pe.wait_ge(s_rot, t + 1)
                        if t >= 1:
                            pe.wait_ge(s_qk, t)
                        for c in range(NC):
                            for s in range(2):
                                k = (c * 2 + s) * P
                                last = pe.transpose(ps[:, 4, k:k + P], ra[:, t % 2, c, s, :], id_f[:])
                        last.then_inc(s_qkt, 1)

                    def scores(i):
                        if i >= 1:
                            pe.wait_ge(s_e1, i)
                        pe.wait_ge(s_qk, i + 1)
                        n = (i + 1) * P
                        for kb in range((n + 511) // 512):
                            w = min(512, n - kb * 512)
                            bank = 2 + kb
                            for c in range(NC):
                                pe.matmul(ps[:, bank, 0:w], QK1[:, c, 0, i * P:(i + 1) * P],
                                          QK1[:, c, 1, kb * 512:kb * 512 + w], start=(c == 0),
                                          stop=(c == 1))
                        last = pe.matmul(ps[:, 2 + i // 4, (i % 4) * P:(i % 4 + 1) * P], id_b[:],
                                         mask_t[:, 0, P:2 * P], start=False, stop=True, skip_group_check=True)
                        last.then_inc(s_s, 1)

                    def probs_t(i):
                        pe.wait_ge(s_e1, i + 1)
                        for k4 in range(i // 4 + 1):
                            if i >= 1:
                                pe.wait_ge(s_pte, ptg[i])
                            if k4:
                                pe.wait_ge(s_hh, NT // 2)
                            for kb in range(4 * k4, min(i + 1, 4 * k4 + 4)):
                                last = pe.transpose(ps[:, (7, 5)[k4], (kb % 4) * P:(kb % 4 + 1) * P],
                                                    P1[:, i % 2, kb * P:(kb + 1) * P], id_f[:])
                            last.then_inc(s_ptr, 1)

                    def attn_out(i):
                        pe.wait_ge(s_pte, ptg[i] + i // 4 + 1)
                        if i >= 1:
                            pe.wait_ge(s_yo, i)
                        for kb in range(i + 1):
                            last = pe.matmul(ps[:, 6, 0:DIM], PT1[:, i % 2, kb, :], V1[:, kb, :],
                                             start=(kb == 0), stop=(kb == i))
                        last.then_inc(s_y, 1)

                    t_xn(0)
                    for t in range(NT + 4):
                        if t % 2 == 0 and t // 2 + 1 < NT // 2:
                            t_xn(t // 2 + 1)
                        if t < NT:
                            proj(t)
                        if 0 <= t - 2 < NT:
                            scores(t - 2)
                        if 0 <= t - 1 < NT:
                            t_qk(t - 1)
                        if 0 <= t - 3 < NT:
                            probs_t(t - 3)
                        if t >= 4:
                            attn_out(t - 4)

                    def claim(key):
                        u = tuse[key]
                        if u >= 2:
                            pe.wait_ge(s_tf[u % 2], u // 2)
                        return 5 + u % 2

                    def rows_t(key, rows):
                        bank = claim(key)
                        for t in range(2):
                            for c in range(NC):
                                last = pe.transpose(ps[:, bank, c * 256 + t * P:c * 256 + (t + 1) * P],
                                                    rows(t)[:, c * P:(c + 1) * P], id_f[:])
                        last.then_inc(s_t, 1)

                    for piece in PIECES:
                        kind, n = piece[0], piece[1]
                        l, w = n // NT, n % NT
                        if kind == "D":
                            l, p = piece[1:]
                            if piece[1:] == (0, 1):
                                pe.wait_ge(s_yo, NT)
                            pe.wait_ge(s_u2 if l else s_u0, 2 * p + 2)
                            rows_t(piece, lambda t: U[:, 2 * p + t, :])
                        elif kind == "N":
                            l, p = piece[1:]
                            pe.wait_ge(s_xnw, l * 4 + p + 1)
                            rows_t(piece, lambda t: XN[:, p % 2, t, :])
                        elif kind == "E":
                            k = piece[2]
                            e = 3 * n + k
                            if k == 0 and w % 2 == 0:
                                pe.wait_ge(*t_read(("D", l, w // 2)))
                            if e >= 2:
                                pe.wait_ge(s_ev, e - 1)
                            if l and w == 0 and k < 2:
                                pe.wait_ge(s_ust, l * NG * (NJ + 1) - 1 + k)
                            for c in range(NC):
                                a = w * P + (1 - c)
                                last = mm3(pe, ps[:, (e + l) % 2, :], [q[:, c, a:a + P] for q in ht],
                                           [q[:, l, c, k * INNER:(k + 1) * INNER] for q in wqkv_p], c == 0, c == 1)
                            last.then_inc(s_qkv, 1)
                        elif kind == "F":
                            pe.wait_ge(s_rope, n + 1)
                            for s in range(2):
                                bank = claim(("F", n, s))
                                for h in range(4):
                                    k = s * INNER + h * P
                                    last = pe.transpose(ps[:, bank, h * P:(h + 1) * P], M1[:, n % 2, k:k + P], id_f[:])
                                last.then_inc(s_t, 1)
                        elif kind == "G":
                            k, m = piece[2], 4 * n + piece[2]
                            if k == 0:
                                pe.wait_ge(*t_read(("F", n, 0)))
                                pe.wait_ge(*t_read(("F", n, 1)))
                            if m >= 3:
                                pe.wait_ge(s_exp, m - 2)
                            if l and w == 0 and k == 0:
                                pe.wait_ge(s_u2, n)
                            bank, r = 2 + m % 3, 64 * (k % 2)
                            pe.matmul(ps[:, bank, :], id_b[:], mask_t[:, 0 if w else 1, :], start=True, stop=True)
                            for i in range(2):
                                hp = 2 * (k // 2) + i
                                for kb in range(0 if w else 1, 2):
                                    o = i * 256 + kb * P
                                    last = pe.matmul(ps[:, bank, o:o + P], QT[r:r + 64, n % 2, hp, :],
                                                     KT[r:r + 64, (n - 1 + kb) % 3, hp, :], start=False,
                                                     stop=True, skip_group_check=True)
                            last.then_inc(s_sim, 1)
                        elif kind == "H":
                            f = piece[2]
                            pe.wait_ge(s_pn, 2 * n + f + 1)
                            for q in range(2):
                                bank = claim(("H", n, f, q))
                                for k in range(4):
                                    last = pe.transpose(ps[:, bank, k * P:(k + 1) * P],
                                                        PW[:, f, q, k // 2, (k % 2) * P:(k % 2 + 1) * P], id_f[:])
                                last.then_inc(s_t, 1)
                        elif kind == "I":
                            f = piece[2]
                            pe.wait_ge(*t_read(("H", n, f, 0)))
                            pe.wait_ge(*t_read(("H", n, f, 1)))
                            pe.wait_ge(s_ev, 3 * n + 3)
                            if f == 0 and n >= 1:
                                pe.wait_ge(s_res, n)
                            for k in range(2):
                                for kb in range(0 if w else 1, 2):
                                    for q in range(2):
                                        h = 4 * f + q + 2 * k
                                        last = pe.matmul(ps[64 * q:64 * q + 64, 7, (h // 2) * P:(h // 2 + 1) * P],
                                                         V[:, (n - 1 + kb) % 4, h * DH:(h + 1) * DH],
                                                         PTW[:, f, q, 2 * k + kb, :], start=(kb == (0 if w else 1)),
                                                         stop=(kb == 1), skip_group_check=True)
                            last.then_inc(s_pv, 1)
                        elif kind == "J":
                            pe.wait_ge(s_ol, n + 1)
                            for c in range(4):
                                last = mm3(pe, ps[:, 7, 0:DIM], [q[:, c, :] for q in ot],
                                           [q[:, l, c, :] for q in wo_p], c == 0, c == 3)
                            last.then_inc(s_wo, 1)
                        elif kind == "W":
                            l, g, j = piece[1:]
                            v = (l * NG + g) * (NJ + 1) + j
                            if j == 0:
                                pe.wait_ge(*t_read(("N", l, 2 * g)))
                                pe.wait_ge(*t_read(("N", l, 2 * g + 1)))
                            bank = w1_bank(l, g, j)
                            if v >= 2:
                                pe.wait_ge(s_ust, v if (g, j) == (0, 1) else v - 1)
                            elif v == 1:
                                pe.wait_ge(s_ust, 1)
                            for i in range(2 if j < NJ else 1):
                                m = P if j < NJ else GT + TAIL
                                for c in range(NC):
                                    a = g * 512 + 1
                                    last = mm3(pe, ps[0:m, bank + i, :],
                                               [q[:, l, c, 2 * j + i, 0:m] for q in w1_p],
                                               [q[:, c, a:a + 512] for q in ht], c == 0, c == 1)
                                last.then_inc(s_w1g if i == 0 else s_w1, 1)
                        elif kind == "Y":
                            if w % NT >= 2:
                                pe.wait_ge(s_u2, n - 1)
                            a = (w % GW) * P
                            bank = (4, 7)[w % 2]
                            for j in range(NJ + 1):
                                if w % GW == 0:
                                    pe.wait_ge(s_ul, (n // GW) * (NJ + 1) + j + 1)
                                if j < NJ:
                                    hid = [q[j][:, a:a + P] for q in (uh, ul)]
                                    wt = [q[:, l, j, :] for q in w2_p]
                                else:
                                    hid = [q[0:GT, a:a + P] for q in u_tail]
                                    wt = [q[0:GT, l, j, :] for q in w2_p]
                                last = mm3(pe, ps[:, bank, 0:DIM], hid, wt, j == 0, j == NJ)
                            last.then_inc(s_w2, 1)

                @block.scalar
                def _(act):
                    def h_parts(p):
                        act.wait_ge(s_xnT, p + 1)
                        if p == 0:
                            act.wait_ge(s_mod, 32)
                        if p >= 2:
                            act.wait_ge(s_hl, p - 1)
                        for hi in range(2):
                            for c in range(NC):
                                dst = ht[0][:, c, 1 + p * 256:1 + (p + 1) * 256] if hi else hf1[:, p % 2, c, :]
                                last = act.activation(dst, ps[:, 5, c * 256:(c + 1) * 256], ACT.Identity,
                                                      scale=modc[:, NC + c:NC + c + 1], bias=modc[:, c:c + 1])
                        last.then_inc(s_hh, 1)

                    def v_copy(t):
                        act.wait_ge(s_m1a, t + 1)
                        src = ps[:, 0:2, 2 * P:3 * P].rearrange("p c (d h) -> p c d h", h=HPC)
                        act.activation(V1[:, t, :].rearrange("p (d c h) -> p c d h", c=NC, h=HPC), src,
                                       ACT.Copy).then_inc(s_v1, 1)

                    def qk_copy(t):
                        act.wait_ge(s_qkt, t + 1)
                        act.activation(QK1[:, :, :, t * P:(t + 1) * P],
                                       ps[:, 4, :].rearrange("p (c s n) -> p c s n", c=NC, s=2),
                                       ACT.Copy).then_inc(s_qk, 1)

                    def probs(i):
                        act.wait_ge(s_nm, i + 1)
                        n = (i + 1) * P
                        if i >= 2:
                            act.wait_ge(s_ptr, ptg[i - 1])
                        src = ps[:, 2:4, :].rearrange("p a n -> p (a n)")
                        act.activation(P1[:, i % 2, 0:n], src[:, 0:n], ACT.Exp, bias=nm1[:, i:i + 1], scale=GAMMA,
                                       accum_out=sm1[:, i:i + 1]).then_inc(s_e1, 1)

                    h_parts(0)
                    for t in range(NT + 2):
                        if t % 2 == 0 and t // 2 + 1 < NT // 2:
                            h_parts(t // 2 + 1)
                        if t < NT:
                            v_copy(t)
                        if 0 <= t - 2 < NT:
                            probs(t - 2)
                        if 0 <= t - 1 < NT:
                            qk_copy(t - 1)

                    for piece in PIECES:
                        kind, n = piece[0], piece[1]
                        if kind in "DN":
                            l, p = piece[1:]
                            act.wait_ge(s_t, tuse[piece] + 1)
                            act.activation(ht[0][:, :, 1 + p * 256:1 + (p + 1) * 256],
                                           ps[:, tbank(piece), :].rearrange("p (c n) -> p c n", c=NC),
                                           ACT.Copy).then_inc(s_dh if kind == "D" else s_nh, 1)
                        elif kind == "E":
                            k = piece[2]
                            act.wait_ge(s_qkv, 3 * n + k + 1)
                            if k == 0 and n >= 2:
                                act.wait_ge(s_m, n - 1)
                            if k == 2 and n >= 4:
                                act.wait_ge(s_pv, 2 * (n - 2))
                            if n >= NT and n % NT < 2 and k == 0:
                                act.wait_ge((s_ust, s_ul)[n % NT], (n // NT) * NG * (NJ + 1))
                            dst = RAW[:, n % 2, k, :] if k < 2 else V[:, n % 4, :]
                            act.activation(dst, ps[:, (3 * n + k + n // NT) % 2, :], ACT.Copy).then_inc(s_ev, 1)
                        elif kind == "q":
                            act.wait_ge(s_ev, 3 * n + 2)
                            if n >= 1:
                                act.wait_ge(s_ss, n)
                            act.activation(SQ, RAW[:, n % 2, :, :].rearrange("p s n -> p (s n)"),
                                           ACT.Square).then_inc(s_sq, 1)
                        elif kind == "F":
                            for s in range(2):
                                key = ("F", n, s)
                                act.wait_ge(s_t, tuse[key] + 1)
                                act.activation(KT[:, n % 3] if s else QT[:, n % 2],
                                               ps[:, tbank(key), :].rearrange("p (h n) -> p h n", h=4),
                                               ACT.Copy).then_inc(t_read(key)[0], 1)
                        elif kind == "G":
                            k, m = piece[2], 4 * n + piece[2]
                            act.wait_ge(s_nb, m + 1)
                            for i in range(2):
                                h = 4 * (k // 2) + k % 2 + 2 * i
                                last = act.activation(PW[:, k // 2, k % 2, i, :],
                                                      ps[:, 2 + m % 3, i * 256:(i + 1) * 256], ACT.Exp,
                                                      bias=nbw[:, n % 2, h:h + 1], scale=rinv[:, n % 2, h:h + 1],
                                                      accum_out=smw[:, n % 2, h:h + 1])
                            last.then_inc(s_exp, 1)
                        elif kind == "H":
                            key = ("H", n, piece[2], 1)
                            act.wait_ge(s_t, tuse[key] + 1)
                            if 2 * n + piece[2] >= 2:
                                act.wait_ge(s_pv, 2 * n + piece[2] - 1)
                            act.activation(PTW[:, piece[2], 1],
                                           ps[:, tbank(key), :].rearrange("p (k n) -> p k n", k=4),
                                           ACT.Copy).then_inc(t_read(key)[0], 1)
                        elif kind == "I" and piece[2] == 1:
                            act.wait_ge(s_pv, 2 * n + 2)
                            act.activation(ot[0][:, :, :], ps[:, 7, :].rearrange("p (h n) -> p h n", h=4),
                                           ACT.Copy).then_inc(s_oh, 1)
                        elif kind == "w":
                            l, g, j = piece[1:]
                            v = (l * NG + g) * (NJ + 1) + j
                            act.wait_ge(s_w1g, v + 1)
                            if v >= 2:
                                act.wait_ge(s_ust, v - 1)
                            if j < NJ:
                                dst, src = GB[:, v % 2, :], ps[:, w1_bank(l, g, j), :]
                                bias = bias1[:, l, 2 * j:2 * j + 1]
                            else:
                                dst, src = GB[0:TAIL, v % 2, :], ps[GT:GT + TAIL, w1_bank(l, g, j), :]
                                bias = bias1[GT:GT + TAIL, l, 2 * j:2 * j + 1]
                            act.activation(dst, src, ACT.Gelu, bias=bias).then_inc(s_g, 1)
                            todo = [v - 1] if j > 0 else []
                            if j == NJ:
                                todo.append(v)
                            for q in todo:
                                jj = q % (NJ + 1)
                                act.wait_ge(s_ust, q + 1)
                                if jj == 0 and q > 0:
                                    act.wait_ge(s_w2, (q // (NJ + 1)) * GW)
                                rows = P if jj < NJ else TAIL
                                dst = uh[jj] if jj < NJ else u_tail[0][0:TAIL, :]
                                act.activation(dst, UB[0:rows, q % 2, :], ACT.Copy).then_inc(s_uh, 1)

                @block.vector
                def _(dve):
                    def stats(p):
                        dve.wait_ge(s_x[p], 16)
                        for t in range(2 * p, 2 * p + 2):
                            last = dve.bn_stats(st[:, t, 0, :], X[:, t, :])
                        last.then_inc(s_bst, 1)
                        dve.wait_ge(s_bst, p + 1)
                        for t in range(2 * p, 2 * p + 2):
                            last = dve.bn_aggr(mv[:, t, :], st[:, t, 0, :])
                        last.then_inc(s_mv, 1)

                    def ln_rows(p):
                        dve.wait_ge(s_rstd, p + 1)
                        if p >= 2:
                            dve.wait_ge(s_xnT, p - 1)
                        for i in range(2):
                            t = 2 * p + i
                            last = dve.tensor_scalar(
                                xn1[:, p % 2, i, :, :].rearrange("p c (h q) -> p (c h) q", q=AD),
                                X[:, t, :].rearrange("p (q h) -> p h q", h=AH),
                                mv[:, t, 0:1], rstd[:, t:t + 1], ALU.subtract, ALU.mult)
                        last.then_inc(s_xn, 1)

                    def rope1(t):
                        dve.wait_ge(s_proj, t + 1)
                        if t >= 2:
                            dve.wait_ge(s_qkt, t - 1)
                        for c in range(NC):
                            src = ps[:, c, 0:2 * P].rearrange("p (s i e) -> p s i e", s=2, e=2)
                            a = ra[:, t % 2, c].rearrange("p s (i e) -> p s i e", e=2)
                            bb = rb[:, t % 2, c].rearrange("p s (i e) -> p s i e", e=2)
                            cs = cos_t[:, t, c, :].unsqueeze(1).broadcast_to((P, 2, 64))
                            sn = sin_t[:, t, c, :].unsqueeze(1).broadcast_to((P, 2, 64))
                            for e in range(2):
                                dve.tensor_tensor(a[:, :, :, e], src[:, :, :, e], cs, ALU.mult)
                            dve.scalar_tensor_tensor(out=bb[:, :, :, 0], in0=src[:, :, :, 1], scalar=-1.0, in1=sn,
                                                     op0=ALU.mult, op1=ALU.mult)
                            last = dve.tensor_tensor(bb[:, :, :, 1], src[:, :, :, 0], sn, ALU.mult)
                        last.then_inc(s_m1a, 1)

                    def row_max(i):
                        dve.wait_ge(s_s, i + 1)
                        src = ps[:, 2:4, :].rearrange("p a n -> p (a n)")
                        dve.tensor_reduce(mx1[:, i:i + 1], src[:, 0:(i + 1) * P], AX, ALU.max).then_inc(s_mx, 1)
                        dve.wait_ge(s_mx, i + 1)
                        dve.tensor_scalar(nm1[:, i:i + 1], mx1[:, i:i + 1], -GAMMA, None, ALU.mult).then_inc(s_nm, 1)

                    def probs_copy(i):
                        for k4 in range(i // 4 + 1):
                            g = ptg[i] + k4
                            dve.wait_ge(s_ptr, g + 1)
                            if i >= 2 and k4 == 0:
                                dve.wait_ge(s_y, i - 1)
                            m = min(4, i + 1 - 4 * k4)
                            dve.tensor_copy(PT1[:, i % 2, 4 * k4:4 * k4 + m, :],
                                            ps[:, (7, 5)[k4], 0:m * P].rearrange("p (k n) -> p k n", n=P)
                                            ).then_inc(s_pte, 1)

                    def y_scale(i):
                        dve.wait_ge(s_e1, i + 1)
                        dve.reciprocal(rs1[:, i:i + 1], sm1[:, i:i + 1]).then_inc(s_rs, 1)
                        dve.wait_ge(s_rs, i + 1)
                        dve.wait_ge(s_y, i + 1)
                        if i >= 2:
                            dve.wait_ge(s_x2, i - 1)
                        dve.scalar_tensor_tensor(out=yt[:, i % 2, :], in0=ps[:, 6, 0:DIM],
                                                 scalar=rs1[:, i:i + 1], in1=modb[:, 0, :], op0=ALU.mult,
                                                 op1=ALU.mult).then_inc(s_yo, 1)

                    stats(0)
                    stats(1)
                    ln_rows(0)
                    stats(2)
                    ln_rows(1)
                    stats(3)
                    dve.wait_ge(s_mod, 32)
                    for t in range(NT + 4):
                        if t % 2 == 0 and t // 2 + 2 < NT // 2:
                            ln_rows(t // 2 + 2)
                        if t < NT:
                            rope1(t)
                        if 0 <= t - 2 < NT:
                            row_max(t - 2)
                        if 0 <= t - 3 < NT:
                            probs_copy(t - 3)
                        if t >= 4:
                            y_scale(t - 4)
                        if t in (8, NT + 3):
                            g = 0 if t == 8 else 1
                            dve.wait_ge(s_x2, 4 * g + 4)
                            for t in range(4 * g, 4 * g + 4):
                                last = dve.bn_stats(st[:, t, 0, :], X[:, t, :])
                            last.then_inc(s_bst, 1)
                            dve.wait_ge(s_bst, 5 + g)
                            for t in range(4 * g, 4 * g + 4):
                                last = dve.bn_aggr(mv[:, t, :], st[:, t, 0, :])
                            last.then_inc(s_mv, 1)
                            dve.wait_ge(s_rstd, 5 + g)
                            for t in range(4 * g, 4 * g + 4):
                                dve.tensor_scalar(U[:, t, :], X[:, t, :], mv[:, t, 0:1], rstd[:, t:t + 1],
                                                  ALU.subtract, ALU.mult).then_inc(s_u0a, 1)

                    def norm(n, f):
                        dve.wait_ge(s_exp, 4 * n + 2 * f + 2)
                        dve.reciprocal(rsw, smw[:, n % 2, 4 * f:4 * f + 4]).then_inc(s_rsw, 1)
                        dve.wait_ge(s_rsw, 2 * n + f + 1)
                        for q in range(2):
                            for i in range(2):
                                k = q + 2 * i
                                pw = PW[:, f, q, i, :]
                                last = dve.tensor_scalar(pw, pw, rsw[:, k:k + 1], None, ALU.mult)
                        last.then_inc(s_pn, 1)

                    for piece in PIECES:
                        kind, n = piece[0], piece[1]
                        l, w = n // NT, n % NT
                        if kind in "DN":
                            l, p = piece[1:]
                            dve.wait_ge(s_dh if kind == "D" else s_nh, l * 4 + p + 1)
                            cols = slice(1 + p * 256, 1 + (p + 1) * 256)
                            dve.tensor_tensor(ht[1][:, :, cols],
                                              ps[:, tbank(piece), :].rearrange("p (c n) -> p c n", c=NC),
                                              ht[0][:, :, cols], ALU.subtract).then_inc(t_read(piece)[0], 1)
                        elif kind == "r":
                            dve.wait_ge(s_sq, n + 1)
                            dve.tensor_reduce(ss[:, n % 2, :], SQ.rearrange("p (h d) -> p h d", d=DH), AX,
                                              ALU.add).then_inc(s_ss, 1)
                        elif kind == "x":
                            raw = RAW[:, n % 2].rearrange("p s (h d) -> p s h d", d=DH)
                            m1 = M1[:, n % 2, :].rearrange("p (s h d) -> p s h d", s=2, d=DH)
                            m2 = M2.rearrange("p (s h d) -> p s h d", s=2, d=DH)
                            cs = xp_t[:, l, w, 0:2, :].unsqueeze(2).broadcast_to((P, 2, HEADS, DH))
                            sn = xp_t[:, l, w, 2:4, :].unsqueeze(2).broadcast_to((P, 2, HEADS, DH))
                            if piece[2] == 0:
                                if n >= 2:
                                    dve.wait_ge(s_t, tuse[("F", n - 2, 1)] + 1)
                                dve.wait_ge(s_ev, 3 * n + 2)
                                dve.tensor_tensor(m1, raw, cs, ALU.mult)
                                continue
                            if n >= 1:
                                dve.wait_ge(s_add, n)
                            for e in range(2):
                                lo, hi = slice(32 * e, 32 * e + 32), slice(32 - 32 * e, 64 - 32 * e)
                                last = dve.tensor_tensor(m2[:, :, :, lo], raw[:, :, :, hi], sn[:, :, :, lo], ALU.mult)
                            last.then_inc(s_m, 1)
                        elif kind == "G":
                            k, m = piece[2], 4 * n + piece[2]
                            h = 4 * (k // 2) + k % 2
                            dve.wait_ge(s_sim, m + 1)
                            dve.tensor_reduce(mxw[:, h:h + 3:2], ps[:, 2 + m % 3, :].rearrange("p (i n) -> p i n", i=2),
                                              AX, ALU.max).then_inc(s_mxw, 1)
                            dve.wait_ge(s_mxw, m + 1)
                            dve.wait_ge(s_rinv, n + 1)
                            dve.scalar_tensor_tensor(out=nbw[:, n % 2, h:h + 3:2], in0=mxw[:, h:h + 3:2], scalar=-1.0,
                                                     in1=rinv[:, n % 2, h:h + 3:2], op0=ALU.mult,
                                                     op1=ALU.mult).then_inc(s_nb, 1)
                        elif kind == "n":
                            norm(n, piece[2])
                        elif kind == "H":
                            key = ("H", n, piece[2], 0)
                            dve.wait_ge(s_t, tuse[key] + 1)
                            if 2 * n + piece[2] >= 2:
                                dve.wait_ge(s_pv, 2 * n + piece[2] - 1)
                            dve.tensor_copy(PTW[:, piece[2], 0],
                                            ps[:, tbank(key), :].rearrange("p (k n) -> p k n", k=4)
                                            ).then_inc(t_read(key)[0], 1)
                        elif kind == "I" and piece[2] == 1:
                            dve.wait_ge(s_oh, n + 1)
                            dve.tensor_tensor(ot[1][:, :, :], ps[:, 7, :].rearrange("p (h n) -> p h n", h=4),
                                              ot[0][:, :, :], ALU.subtract).then_inc(s_ol, 1)
                        elif kind == "J":
                            dve.wait_ge(s_wo, n + 1)
                            dve.tensor_tensor(U[:, w, :], ps[:, 7, 0:DIM], U[:, w, :], ALU.add).then_inc(s_res, 1)
                        elif kind == "L":
                            l, p = piece[1:]
                            q = l * 4 + p
                            dve.wait_ge(s_xs[q], 16 * (4 - (p == 0)))
                            dve.wait_ge(s_res, l * NT + 2 * p + 2)
                            for w in range(2 * p, 2 * p + 2):
                                dve.bn_stats(st[:, w, 0, :], U[:, w, 0:P])
                                last = dve.bn_stats(st[:, w, 1, :], XS[:, w, :])
                            last.then_inc(s_bn, 1)
                            dve.wait_ge(s_bn, q + 1)
                            for w in range(2 * p, 2 * p + 2):
                                last = dve.bn_aggr(mv[:, w, :], st[:, w, :, :].rearrange("p a b -> p (a b)"))
                            last.then_inc(s_lnmv, 1)
                        elif kind == "K":
                            l, p = piece[1:]
                            dve.wait_ge(s_lnr, l * 4 + p + 1)
                            if l * 4 + p >= 2:
                                pl, pp = divmod(l * 4 + p - 2, 4)
                                dve.wait_ge(s_t, tuse[("N", pl, pp)] + 1)
                            for i in range(2):
                                w = 2 * p + i
                                dve.tensor_scalar(XN[:, p % 2, i, 0:P], U[:, w, 0:P], mv[:, w, 0:1],
                                                  rstd[:, w:w + 1], ALU.subtract, ALU.mult)
                                last = dve.tensor_scalar(XN[:, p % 2, i, P:DIM], XS[:, w, :], mv[:, w, 0:1],
                                                         rstd[:, w:w + 1], ALU.subtract, ALU.mult)
                            last.then_inc(s_xnw, 1)
                        elif kind == "w":
                            l, g, j = piece[1:]
                            v = (l * NG + g) * (NJ + 1) + j
                            dve.wait_ge(s_g, v + 1)
                            if j < NJ:
                                dve.wait_ge(s_w1, (l * NG + g) * NJ + j + 1)
                            if v >= 2:
                                dve.wait_ge(s_ul, v - 1)
                            rows = P if j < NJ else TAIL
                            src = ps[0:rows, w1_bank(l, g, j) + (1 if j < NJ else 0), :]
                            dve.scalar_tensor_tensor(out=UB[0:rows, v % 2, :], in0=src,
                                                     scalar=bias1[0:rows, l, min(2 * j + 1, 2 * NJ):min(2 * j + 1, 2 * NJ) + 1],
                                                     in1=GB[0:rows, v % 2, :], op0=ALU.add,
                                                     op1=ALU.mult).then_inc(s_ust, 1)
                        elif kind == "Y":
                            dve.wait_ge(s_w2, n + 1)
                            dve.tensor_tensor(U[:, w, :], ps[:, (4, 7)[w % 2], 0:DIM], U[:, w, :],
                                              ALU.add).then_inc(s_u2, 1)

                @block.gpsimd
                def _(pool):
                    def root(count, lo, hi):
                        pool.tensor_scalar(veps[:, lo:hi], mv[:, lo:hi, 1], EPS, None, ALU.add).then_inc(s_v2, 1)
                        pool.wait_ge(s_v2, count)
                        return pool.tensor_tensor(rstd[:, lo:hi], veps[:, lo:hi], neg_half[:, 0:hi - lo], ALU.pow)

                    for p in range(NT // 2):
                        pool.wait_ge(s_mv, p + 1)
                        root(p + 1, 2 * p, 2 * p + 2).then_inc(s_rstd, 1)

                    def low_part(p):
                        pool.wait_ge(s_hh, p + 1)
                        pool.tensor_tensor(ht[1][:, :, 1 + p * 256:1 + (p + 1) * 256], hf1[:, p % 2],
                                           ht[0][:, :, 1 + p * 256:1 + (p + 1) * 256],
                                           ALU.subtract).then_inc(s_hl, 1)

                    low_part(0)
                    pool.wait_ge(s_mod, 32)
                    for t in range(NT + 4):
                        if t % 2 == 0 and t // 2 + 1 < NT // 2:
                            low_part(t // 2 + 1)
                        if t < NT:
                            pool.wait_ge(s_m1a, t + 1)
                            a = ra[:, t % 2].rearrange("p c s n -> p (c s n)")
                            pool.tensor_tensor(a, a, rb[:, t % 2].rearrange("p c s n -> p (c s n)"),
                                               ALU.add).then_inc(s_rot, 1)
                        if t < 4:
                            continue
                        i = t - 4
                        pool.wait_ge(s_yo, i + 1)
                        pool.tensor_tensor(X[:, i, :], X[:, i, :], yt[:, i % 2, :], ALU.add).then_inc(s_x2, 1)
                        if i in (4, NT - 1):
                            g = 0 if i == 4 else 1
                            pool.wait_ge(s_mv, 5 + g)
                            root(5 + g, 4 * g, 4 * g + 4).then_inc(s_rstd, 1)
                            for t in range(4 * g, 4 * g + 4):
                                pool.wait_ge(s_u0a, t + 1)
                                pool.tensor_tensor(U[:, t, :], U[:, t, :], modb[:, 2, :], ALU.mult).then_inc(s_u0b, 1)
                            for t in range(4 * g, 4 * g + 4):
                                pool.wait_ge(s_u0b, t + 1)
                                pool.tensor_tensor(U[:, t, :], U[:, t, :], modb[:, 1, :], ALU.add).then_inc(s_u0, 1)

                    for piece in PIECES:
                        kind, n = piece[0], piece[1]
                        l, w = n // NT, n % NT
                        if kind == "r":
                            pool.wait_ge(s_ss, n + 1)
                            pool.tensor_scalar(ssm, ss[:, n % 2, :], 1e-24, None, ALU.max).then_inc(s_rm, 1)
                            pool.wait_ge(s_rm, n + 1)
                            pool.tensor_tensor(rinv[:, n % 2, :], ssm, neg_half[:, 0:16], ALU.pow).then_inc(s_rinv, 1)
                        elif kind == "x" and piece[2] == 1:
                            pool.wait_ge(s_m, n + 1)
                            pool.tensor_tensor(M1[:, n % 2, :], M1[:, n % 2, :], M2, ALU.add).then_inc(s_add, 1)
                            pool.wait_ge(s_add, n + 1)
                            pool.wait_ge(s_rinv, n + 1)
                            kk = M1[:, n % 2, INNER:2 * INNER].rearrange("p (h d) -> p h d", d=DH)
                            pool.tensor_tensor(kk, kk, rinv[:, n % 2, 8:16].unsqueeze(2).broadcast_to((P, HEADS, DH)),
                                               ALU.mult).then_inc(s_rope, 1)
                        elif kind == "L":
                            l, p = piece[1:]
                            pool.wait_ge(s_lnmv, l * 4 + p + 1)
                            root(7 + l * 4 + p, 2 * p, 2 * p + 2).then_inc(s_lnr, 1)
                        elif kind == "w":
                            l, g, j = piece[1:]
                            v = (l * NG + g) * (NJ + 1) + j
                            pool.wait_ge(s_uh, v + 1)
                            rows = P if j < NJ else TAIL
                            hi = uh[j] if j < NJ else u_tail[0][0:TAIL, :]
                            lo = ul[j] if j < NJ else u_tail[1][0:TAIL, :]
                            pool.tensor_tensor(lo, UB[0:rows, v % 2, :], hi, ALU.subtract).then_inc(s_ul, 1)
                        elif kind == "Y" and l == DEPTH - 1:
                            pool.wait_ge(s_u2, n + 1)
                            pool.tensor_tensor(U[:, w, :], U[:, w, :], modb[:, 3, :], ALU.mult).then_inc(s_fa, 1)
                            pool.wait_ge(s_fa, w + 1)
                            pool.tensor_tensor(U[:, w, :], U[:, w, :], X[:, w, :], ALU.add).then_inc(s_fin, 1)

            for s in names:
                nc.gpsimd.sem_clear(s)
            nc.all_engine_barrier()


ptg = [sum(k // 4 + 1 for k in range(i)) for i in range(NT + 1)]


def setup(nc, ctx, v):
    ps, ar_a, ar_b, ar_c, xu = v["ps"], v["ar_a"], v["ar_b"], v["ar_c"], v["xu"]
    wqkv_p, wo_p, w1_p, w2_p, bd_p = v["wqkv_p"], v["wo_p"], v["w1_p"], v["w2_p"], v["bd_p"]
    id_f, id_b, mask_t, xp_t, bias1 = v["id_f"], v["id_b"], v["mask_t"], v["xp_t"], v["bias1"]
    u_tail, ht, XS = v["u_tail"], v["ht"], v["XS"]
    sem = v["sem"]

    xu_f = xu[:, :, :, :].rearrange("p a t d -> p (a t d)")
    st_qkv = ar_a[:, 0:6144].rearrange("p (l c n) -> p l c n", l=DEPTH, c=NC)
    st_w2 = ar_b[:, 0:2560].rearrange("p (l j n) -> p l j n", l=DEPTH, j=NJ)
    st_w2t = ar_b[0:GT, 2560:3072].rearrange("p (l n) -> p l n", l=DEPTH)
    st_wo = ar_b[:, 3072:5120].rearrange("p (l c n) -> p l c n", l=DEPTH, c=4)
    st_w1 = [xu_f[:, 0:4 * HID].rearrange("p (c n) -> p c n", c=NC),
             ar_c[:, 0:4 * HID].rearrange("p (c n) -> p c n", c=NC)]
    o = 4 * HID
    w_rep = xu_f[:, o:o + 768].rearrange("p (s n) -> p s n", s=3)
    cT = xu_f[:, o + 768:o + 784].rearrange("p (c n) -> p c n", c=NC)
    c_e = xu_f[:, o + 784:o + 800].rearrange("p (c n) -> p c n", c=NC)
    silu = xu_f[:, o + 800:o + 816].rearrange("p (c n) -> p c n", c=NC)
    lgb = xu_f[:, o + 816:o + 824].rearrange("p (k l c) -> p k l c", k=2, l=DEPTH)
    qks = xu_f[:, o + 824:o + 824 + 512].rearrange("p (l k d) -> p l k d", l=DEPTH, k=4)
    w_mod = ar_a[:, 0:3072].rearrange("p (c n) -> p c n", c=NC)
    mrow = ar_a[0:BATCH, 3072:4608]
    mtmp = ar_a[0:BATCH, 4608:5120]
    xp_base = ar_a[:, 3072:3072 + 2048].rearrange("p (t k d) -> p t k d", t=NT, k=4)
    bd_f = ar_a[:, 5120:5120 + 768].rearrange("p (c s n) -> p c s n", c=NC, s=3)
    m_f = ar_b[:, 0:1024].rearrange("p (a n) -> p a n", a=2)

    l_qkv, l_wo, l_w1, l_w2, l_rep, l_small, l_tab = (sem(f"load_{n}") for n in
                                                      ("qkv", "wo", "w1", "w2", "rep", "small", "tables"))
    z_id, z_id2, z_w2, z_mask, z_mask2, z_rest = (sem(n) for n in ("id_zero", "id_ready", "w2_tail_zero", "mask_zero",
                                                                   "mask_ready", "rest_filled"))
    z_bias, z_tail = sem("bias_zero"), sem("w1_tail_zero")
    hi_done, lo_done = sem("setup_hi"), sem("setup_lo")
    lbw, w1s, bias_done = sem("lb_w1_done"), sem("w1_scaled"), sem("bias_done")
    bd_a, bd_b = sem("bd_first"), sem("bd_ready")
    e_done, e1_done, e2_done, e3_done = sem("silu_exp"), sem("silu_plus1"), sem("silu_recip"), sem("silu_ready")
    l_mod, l_xp, mm_done, row_done, row_t, mod_done, mod_out, xp_done = (sem(n) for n in (
        "load_wmod", "load_xpos", "mod_product", "mod_row", "mod_tmp", "mod_changed", "mod_stored", "xpos_scaled"))
    mask_used, mod_in = sem("masks_cast"), sem("mod_columns_loaded")

    block = nc.Block()
    with block:
        @block.sync
        def _(sp):
            for l in range(DEPTH):
                sp.dma_start(st_w1[l], v["w1"][l].rearrange("(c p) n -> p c n", p=P)).then_inc(l_w1, 16)
            for k, src in enumerate((v["ln_g"], v["ln_b"])):
                for l in range(DEPTH):
                    sp.dma_start(lgb[:, k, l, :], src[l].rearrange("(c p) -> p c", p=P)).then_inc(l_small, 16)
            for c in range(NC):
                sp.dma_start(cT[:, c, :], v["cond"][:, c * P:(c + 1) * P].rearrange("b p -> p b")).then_inc(l_small, 16)
            sp.wait_ge(z_bias, 1)
            for l in range(DEPTH):
                for i, base in enumerate((HID, 0)):
                    sp.dma_start(bias1[:, l, i:2 * NJ:2],
                                 v["b1"][l, base:base + NJ * P].rearrange("(j p) -> p j", p=P)).then_inc(l_small, 16)
                    r = (GT, 0)[i]
                    sp.dma_start(bias1[r:r + TAIL, l, 2 * NJ:2 * NJ + 1],
                                 v["b1"][l, base + NJ * P:base + HID].unsqueeze(1)).then_inc(l_small, 16)
            for l in range(DEPTH):
                for k, src in enumerate((v["q_scale"], v["k_scale"])):
                    sp.dma_start(qks[:, l, k, :], src[l].partition_broadcast(P)).then_inc(l_small, 16)
                    for e in range(2):
                        sp.dma_start(qks[:, l, 2 + k, 32 * e:32 * e + 32],
                                     src[l, 32 - 32 * e:64 - 32 * e].partition_broadcast(P)).then_inc(l_small, 16)
            sp.wait_ge(hi_done, 2)
            sp.wait_ge(lo_done, 2)
            sp.dma_start(w_mod, v["wmod"].rearrange("(c p) n -> p c n", p=P)).then_inc(l_mod, 16)
            sp.wait_ge(mod_done, 1)
            sp.dma_start(v["mod_rows"], mrow).then_inc(mod_out, 16)
            sp.wait_ge(mod_out, 16)
            sp.dma_start(xp_base, v["xpos"]).then_inc(l_xp, 16)
            for k in range(2):
                for c in range(NC):
                    for h in range(HPC):
                        a = k * DIM + c * HPC + h
                        src = v["mod_rows"][:, a:(k + 1) * DIM:AH].rearrange("b q -> q b")
                        sp.dma_start(v["modc_all"][h * AD:(h + 1) * AD, :, k * NC + c], src).then_inc(mod_in, 16)
            sp.wait_ge(mod_in, 16 * 2 * NC * HPC)
            sp.wait_ge(l_tab, 32)

        @block.scalar
        def _(act):
            act.dma_start(st_qkv, v["wqkv"].rearrange("l (c p) n -> p l c n", p=P)).then_inc(l_qkv, 16)
            act.dma_start(st_wo, v["wo"].rearrange("l (c p) n -> p l c n", p=P)).then_inc(l_wo, 16)
            act.wait_ge(z_w2, 1)
            for l in range(DEPTH):
                act.dma_start(st_w2[:, l], v["w2"][l, 0:NJ * P].rearrange("(j p) n -> p j n", p=P)).then_inc(l_w2, 16)
                act.dma_start(st_w2t[0:TAIL, l, :], v["w2"][l, NJ * P:HID, :]).then_inc(l_w2, 16)
                act.dma_start(st_w2t[TAIL:TAIL + 1, l, :], v["b2"][l:l + 1, :]).then_inc(l_w2, 16)
            for s, src in enumerate((v["w_q"], v["w_k"], v["w_v"])):
                for h in range(HPC):
                    act.dma_start(w_rep[h * AD:(h + 1) * AD, s, :], src.rearrange("q d h -> q (d h)")).then_inc(l_rep, 16)
            act.dma_start(v["cos_t"][:, :, :, :], v["rope_cos"]).then_inc(l_tab, 16)
            act.dma_start(v["sin_t"][:, :, :, :], v["rope_sin"]).then_inc(l_tab, 16)
            act.wait_ge(l_qkv, 16)
            for l in range(DEPTH):
                act.activation(wqkv_p[0][:, l], st_qkv[:, l], ACT.Copy).then_inc(hi_done, 1)
            act.wait_ge(l_wo, 16)
            for l in range(DEPTH):
                act.activation(wo_p[0][:, l], st_wo[:, l], ACT.Copy).then_inc(hi_done, 1)
            act.wait_ge(l_w2, 16 * 3 * DEPTH)
            for l in range(DEPTH):
                act.activation(w2_p[0][:, l, 0:NJ, :], st_w2[:, l], ACT.Copy)
                act.activation(w2_p[0][0:GT, l, NJ, :], st_w2t[:, l, :], ACT.Copy).then_inc(hi_done, 1)
            act.wait_ge(z_tail, 1)
            for l in range(DEPTH):
                act.wait_ge(w1s, l + 1)
                for dst, src in w1_blocks(w1_p[0], st_w1, l):
                    last = act.activation(dst, src, ACT.Copy)
                last.then_inc(hi_done, 1)
            act.wait_ge(bd_b, 1)
            act.activation(bd_p[0][:, :, :, :], bd_f, ACT.Copy).then_inc(hi_done, 1)
            act.wait_ge(l_small, 16 * N_SMALL)
            act.activation(c_e, cT, ACT.Exp, scale=-1.0).then_inc(e_done, 1)
            act.wait_ge(mm_done, 1)
            act.activation(mrow, ps[0:BATCH, 4:7, :].rearrange("p a n -> p (a n)"), ACT.Copy).then_inc(row_done, 1)

        @block.vector
        def _(dve):
            dve.memset(bias1[:, :, :], 0.0).then_inc(z_bias, 1)
            dve.memset(st_w2t, 0.0).then_inc(z_w2, 1)
            for q in w1_p:
                last = dve.memset(q[:, :, :, 2 * NJ, :], 0.0)
            last.then_inc(z_tail, 1)
            dve.memset(v["neg_half"][:, :], -0.5)
            dve.memset(u_tail[0][:, :], 1.0)
            dve.memset(u_tail[1][:, :], 0.0)
            for q in ht:
                dve.memset(q[:, :, :], 0.0)
            dve.memset(XS[:, 0, :], 0.0).then_inc(z_rest, 1)
            for l in range(DEPTH):
                dve.wait_ge(hi_done, l + 1)
                dve.tensor_tensor(wqkv_p[1][:, l], st_qkv[:, l], wqkv_p[0][:, l], ALU.subtract).then_inc(lo_done, 1)
            for l in range(DEPTH):
                dve.wait_ge(hi_done, DEPTH + l + 1)
                dve.tensor_tensor(wo_p[1][:, l], st_wo[:, l], wo_p[0][:, l], ALU.subtract)
            for l in range(DEPTH):
                dve.wait_ge(hi_done, 2 * DEPTH + l + 1)
                dve.tensor_tensor(w2_p[1][:, l, 0:NJ, :], st_w2[:, l], w2_p[0][:, l, 0:NJ, :], ALU.subtract)
                dve.tensor_tensor(w2_p[1][0:GT, l, NJ, :], st_w2t[:, l, :], w2_p[0][0:GT, l, NJ, :],
                                  ALU.subtract).then_inc(lo_done, 1)
            dve.wait_ge(l_small, 16 * N_SMALL)
            dve.wait_ge(lbw, 1)
            for l in range(DEPTH):
                for c in range(NC):
                    last = dve.tensor_scalar(st_w1[l][:, c, :], st_w1[l][:, c, :], lgb[:, 0, l, c:c + 1], None, ALU.mult)
                last.then_inc(w1s, 1)
            dve.wait_ge(z_bias, 1)
            for l in range(DEPTH):
                k = l * NB1
                dve.tensor_tensor(bias1[:, l, 0:2 * NJ], ps[:, 0, k:k + 2 * NJ], bias1[:, l, 0:2 * NJ], ALU.add)
                k += 2 * NJ
                for r in (0, GT):
                    last = dve.tensor_tensor(bias1[r:r + TAIL, l, 2 * NJ:2 * NJ + 1], ps[r:r + TAIL, 0, k:k + 1],
                                             bias1[r:r + TAIL, l, 2 * NJ:2 * NJ + 1], ALU.add)
            last.then_inc(bias_done, 1)
            for l in range(DEPTH):
                dve.wait_ge(hi_done, 3 * DEPTH + l + 1)
                for (dst, src), (hi, _) in zip(w1_blocks(w1_p[1], st_w1, l), w1_blocks(w1_p[0], st_w1, l)):
                    last = dve.tensor_tensor(dst, src, hi, ALU.subtract)
                last.then_inc(lo_done, 1)
            dve.wait_ge(hi_done, 4 * DEPTH + 1)
            dve.tensor_tensor(bd_p[1][:, :, :, :], bd_f, bd_p[0][:, :, :, :], ALU.subtract).then_inc(lo_done, 1)
            dve.wait_ge(e_done, 1)
            dve.tensor_scalar(c_e, c_e, 1.0, None, ALU.add).then_inc(e1_done, 1)
            dve.wait_ge(e1_done, 1)
            dve.reciprocal(silu, c_e).then_inc(e2_done, 1)
            dve.wait_ge(e2_done, 1)
            dve.tensor_tensor(silu, silu, cT, ALU.mult).then_inc(e3_done, 1)
            dve.wait_ge(row_done, 1)
            dve.tensor_scalar(mrow[:, DIM:2 * DIM], mrow[:, DIM:2 * DIM], 1.0, None, ALU.add)
            dve.tensor_scalar(mrow[:, 4 * DIM:5 * DIM], mrow[:, 4 * DIM:5 * DIM], 1.0, None, ALU.add)
            gates = [mrow[:, k * DIM:(k + 1) * DIM] for k in (2, 5)]
            tmps = [mtmp[:, k * DIM:(k + 1) * DIM] for k in range(2)]
            for g, t in zip(gates, tmps):
                last = dve.tensor_scalar(t, g, 0.0, 2.0, ALU.is_ge, ALU.mult)
            last.then_inc(row_t, 1)
            dve.wait_ge(row_t, 1)
            for g, t in zip(gates, tmps):
                last = dve.tensor_scalar(t, t, -1.0, None, ALU.add)
            last.then_inc(row_t, 1)
            dve.wait_ge(row_t, 2)
            for g, t in zip(gates, tmps):
                last = dve.tensor_tensor(g, g, t, ALU.mult)
            last.then_inc(row_t, 1)
            dve.wait_ge(row_t, 3)
            for g, t in zip(gates, tmps):
                last = dve.scalar_tensor_tensor(out=g, in0=g, scalar=0.25, in1=t, op0=ALU.max, op1=ALU.mult)
            last.then_inc(mod_done, 1)
            dve.wait_ge(z_id2, 1)
            dve.tensor_copy(id_b[:, :], id_f[:, :])
            dve.wait_ge(z_mask2, 3)
            dve.tensor_copy(mask_t[:, :, :], m_f).then_inc(mask_used, 1)
            dve.wait_ge(l_xp, 16)
            for l in range(DEPTH):
                dve.tensor_tensor(xp_t[:, l].rearrange("p t k d -> p t (k d)"), xp_base.rearrange("p t k d -> p t (k d)"),
                                  qks[:, l].rearrange("p k d -> p (k d)").unsqueeze(1).broadcast_to((P, NT, 4 * DH)),
                                  ALU.mult).then_inc(xp_done, 1)

        @block.gpsimd
        def _(pool):
            pool.memset(id_f[:, :], 0.0).then_inc(z_id, 1)
            pool.wait_ge(z_id, 1)
            pool.affine_select(out=id_f[:, :], in_=id_f[:, :], compare_op=ALU.not_equal, fill=1.0, base=0,
                               pattern=[[-1, P]], channel_multiplier=1).then_inc(z_id2, 1)
            pool.wait_ge(l_rep, 16 * 3 * HPC)
            pool.wait_ge(lo_done, 2)
            for c in range(NC):
                for s in range(3):
                    last = pool.affine_select(out=bd_f[:, c, s, :].rearrange("p (d h) -> p d h", h=HPC),
                                              in_=w_rep[:, s, :].rearrange("p (d h) -> p d h", h=AH)[:, :, c * HPC:(c + 1) * HPC],
                                              compare_op=ALU.is_ge, fill=0.0, base=0,
                                              pattern=[[0, AD], [-AD, HPC]], channel_multiplier=1)
            last.then_inc(bd_a, 1)
            pool.wait_ge(bd_a, 1)
            for c in range(NC):
                for s in range(3):
                    t = bd_f[:, c, s, :].rearrange("p (d h) -> p d h", h=HPC)
                    last = pool.affine_select(out=t, in_=t, compare_op=ALU.is_ge, fill=0.0, base=AD - 1,
                                              pattern=[[0, AD], [AD, HPC]], channel_multiplier=-1)
            last.then_inc(bd_b, 1)
            pool.wait_ge(lo_done, 2 + DEPTH)
            pool.memset(m_f, 0.0).then_inc(z_mask, 1)
            pool.wait_ge(z_mask, 1)
            m4 = m_f.rearrange("p a (i k n) -> p a i k n", i=2, k=2)
            pool.affine_select(out=m4[:, 0, :, 0, :], in_=m4[:, 0, :, 0, :], compare_op=ALU.is_ge, fill=NEG, base=0,
                               pattern=[[0, 2], [1, P]], channel_multiplier=-1).then_inc(z_mask2, 1)
            pool.memset(m4[:, 1, :, 0, :], NEG).then_inc(z_mask2, 1)
            for a in range(2):
                last = pool.affine_select(out=m4[:, a, :, 1, :], in_=m4[:, a, :, 1, :], compare_op=ALU.is_ge, fill=NEG,
                                          base=0, pattern=[[0, 2], [-1, P]], channel_multiplier=1)
            last.then_inc(z_mask2, 1)

        @block.tensor
        def _(pe):
            pe.wait_ge(l_w1, 16 * DEPTH)
            pe.wait_ge(l_small, 16 * N_SMALL)
            for l in range(DEPTH):
                for j in range(NB1 + 1):
                    if j < 2 * NJ:
                        a, r, m = (HID, 0)[j % 2] + (j // 2) * P, 0, P
                    else:
                        a, r, m = ((0, HID)[j - 2 * NJ] + NJ * P, (0, GT)[j - 2 * NJ], TAIL)
                    k = l * NB1 + min(j, 2 * NJ)
                    for c in range(NC):
                        last = pe.matmul(ps[r:r + m, 0, k:k + 1], st_w1[l][:, c, a:a + m], lgb[:, 1, l, c:c + 1],
                                         start=(c == 0), stop=(c == NC - 1))
            last.then_inc(lbw, 1)
            pe.wait_ge(e3_done, 1)
            pe.wait_ge(l_mod, 16)
            for j in range(3):
                for c in range(NC):
                    last = pe.matmul(ps[0:BATCH, 4 + j, :], silu[:, c, :], w_mod[:, c, j * 512:(j + 1) * 512],
                                     start=(c == 0), stop=(c == NC - 1))
            last.then_inc(mm_done, 1)


def w1_blocks(dst, stage, l):
    for i, base in enumerate((HID, 0)):
        for c in range(NC):
            yield (dst[:, l, c, i:2 * NJ:2, :],
                   stage[l][:, c, base:base + NJ * P].rearrange("p (j n) -> p j n", n=P))
        r = (GT, 0)[i]
        yield dst[:, l, :, 2 * NJ, r:r + TAIL], stage[l][:, :, base + NJ * P:base + HID]


N_SMALL = 2 * DEPTH + NC + 4 * DEPTH + 6 * DEPTH


def shape_tables():
    import numpy as np

    f = np.float32
    half = DIM // 2
    inv = f(1.0) / (f(10000.0) ** (np.arange(half, dtype=f) / f(half)))
    ang = np.arange(SEQ, dtype=f)[:, None] * inv[None, :]

    def lay(a):
        return np.ascontiguousarray(a.reshape(NT, P, AD, NC, HPC // 2).transpose(1, 0, 3, 2, 4).reshape(P, NT, NC, P // 2))

    idx = np.arange(0, DH, 2, dtype=f)
    inv2 = f(1.0) / (f(10000.0) ** (idx / f(DH)))
    t = np.arange(SEQ, dtype=f)
    fr = t[:, None] * inv2[None, :]
    fr = np.concatenate([fr, fr], -1)
    base = (idx + f(0.4 * DH)) / f(1.4 * DH)
    power = (t - f(SEQ // 2)) / f(64.0)
    sc = base[None, :] ** power[:, None]
    sc = np.concatenate([sc, sc], -1)
    cos, sin = np.cos(fr), np.sin(fr)
    sin[:, :DH // 2] *= f(-1.0)
    qk_scale = f(8.0)
    tab = np.stack([cos * sc * qk_scale, cos / sc, sin * sc * qk_scale, sin / sc], 1).astype(f)
    xpos = np.ascontiguousarray(tab.reshape(NT, P, 4, DH).transpose(1, 0, 2, 3))
    return lay(np.cos(ang).astype(f)), lay(np.sin(ang).astype(f)), xpos


_INS = ['L0_attn_x', 'L0_attn_w_q', 'L0_attn_w_k', 'L0_attn_w_v', 'L0_ffn_wqkv', 'L0_ffn_q_scale', 'L0_ffn_k_scale',
        'L0_ffn_wo', 'L0_ffn_ln_g', 'L0_ffn_ln_b', 'L0_ffn_w1', 'L0_ffn_b1', 'L0_ffn_w2', 'L0_ffn_b2', 'L0_c', 'L0_wmod']


def kernel(**inputs):
    import numpy as _np
    import concourse.bacc as _bacc
    from concourse import mybir as _mybir
    from concourse.bass_utils import run_bass_kernel_spmd as _run

    nc = _bacc.Bacc("TRN2", target_bir_lowering=False, num_devices=1)
    arrays, args = {}, []
    tables = dict(zip(("rope_cos", "rope_sin", "xpos"), shape_tables()))
    for name in _INS + list(tables):
        a = _np.ascontiguousarray(inputs[name] if name in inputs else tables[name])
        arrays[f"in_{name}_dram"] = a
        args.append(nc.dram_tensor(f"in_{name}_dram", a.shape, _mybir.dt.from_np(a.dtype), kind="ExternalInput").ap())
    out = nc.dram_tensor("out_0_dram", (BATCH, SEQ, DIM), F32, kind="ExternalOutput").ap()
    adaln_kernel(nc, *args, out)
    r = _run(nc, [arrays], core_ids=[0])
    return r.results[0]["out_0_dram"]
```

```python
from contextlib import ExitStack

import concourse.bass as bass
from concourse import mybir

F32 = mybir.dt.float32
F16 = mybir.dt.float16
BF16 = mybir.dt.bfloat16
ALU = mybir.AluOpType
ACT = mybir.ActivationFunctionType
AX = mybir.AxisListType.X

P = 128
EPS = 1e-5
NEG = -1.0e30
BATCH, SEQ, DIM = 8, 1024, 256
NT = SEQ // P
NC = DIM // P
AH = 16
AD = DIM // AH
HPC = AH // NC
DEPTH = 2
HEADS, DH = 8, 64
INNER = HEADS * DH
HID = DIM * 4 * 2 // 3
NJ = HID // P
TAIL = HID - NJ * P
NB1 = 2 * NJ + 1
GT = 64
NG = 2
GW = NT // NG
GAMMA = 1.0 / DIM ** 0.5


def adaln_kernel(nc, x, w_q, w_k, w_v, wqkv, q_scale, k_scale, wo, ln_g, ln_b, w1, b1, w2, b2,
                 cond, wmod, rope_cos, rope_sin, xpos, out):
    mod_rows = nc.dram_tensor("mod_rows", [BATCH, 6 * DIM], F32, kind="Internal").ap()

    with ExitStack() as ctx:
        ctx.enter_context(nc.allow_non_contiguous_dma(reason="small vectors and shifted rows"))
        def sb(name, shape, dt=F32):
            return ctx.enter_context(nc.sbuf_tensor(name, shape, dt))

        names = []

        def sem(name):
            s = ctx.enter_context(nc.semaphore(name))
            names.append(s)
            return s

        ps = ctx.enter_context(nc.psum_tensor("ps", [P, 8, 512], F32))

        wqkv_p = [sb(f"wqkv_{s}", [P, DEPTH, NC, 3 * INNER], F16) for s in ("hi", "lo")]
        wo_p = [sb(f"wo_{s}", [P, DEPTH, INNER // P, DIM], F16) for s in ("hi", "lo")]
        w1_p = [sb(f"w1_{s}", [P, DEPTH, NC, NB1, P], F16) for s in ("hi", "lo")]
        w2_p = [sb(f"w2_{s}", [P, DEPTH, NJ + 1, DIM], F16) for s in ("hi", "lo")]
        bd_p = [sb(f"bd_{s}", [P, NC, 3, P], F16) for s in ("hi", "lo")]
        cos_t = sb("cos_t", [P, NT, NC, P // 2])
        sin_t = sb("sin_t", [P, NT, NC, P // 2])
        xp_t = sb("xp_t", [P, DEPTH, NT, 4, DH])
        mask_t = sb("mask_t", [P, 2, 512], BF16)
        id_b = sb("id_b", [P, P], BF16)
        id_f = sb("id_f", [P, P])
        bias1 = sb("bias1", [P, DEPTH, NB1])
        u_tail = [sb(f"u_tail_{s}", [GT, 512], F16) for s in ("hi", "lo")]
        neg_half = sb("neg_half", [P, 16])
        modc_all = sb("modc_all", [P, BATCH, 2 * NC])

        xu = sb("xu", [P, 2, NT, DIM])
        X, U = xu[:, 0], xu[:, 1]
        modb = sb("modb", [P, 4, DIM])
        modc = sb("modc", [P, 2 * NC])
        ht = [sb(f"ht_{s}", [P, NC, SEQ + 1], F16) for s in ("hi", "lo")]
        st = sb("st", [P, 8, 2, 6])
        mv = sb("mv", [P, NT, 2])
        rstd = sb("rstd", [P, NT])
        veps = sb("veps", [P, NT])

        ar_a = sb("ar_a", [P, 26 * 256])
        QK1 = ar_a[:, 0:4096].rearrange("p (c s n) -> p c s n", c=NC, s=2)
        V1 = ar_a[:, 4096:6144].rearrange("p (t n) -> p t n", t=NT)
        V = ar_a[:, 0:2048].rearrange("p (r n) -> p r n", r=4)
        QT = ar_a[:, 3072:4096].rearrange("p (r h n) -> p r h n", r=2, h=4)
        KT = ar_a[:, 4096:5632].rearrange("p (r h n) -> p r h n", r=3, h=4)
        ar_b = sb("ar_b", [P, 20 * 256])
        P1 = ar_b[:, 0:2048].rearrange("p (r n) -> p r n", r=2)
        PT1 = ar_b[:, 2048:4096].rearrange("p (r k n) -> p r k n", r=2, k=NT)
        PW = ar_b[:, 0:2048].rearrange("p (f x k n) -> p f x k n", f=2, x=2, k=2)
        PTW = ar_b[:, 2048:4096].rearrange("p (f x k n) -> p f x k n", f=2, x=2, k=4)
        UB = ar_a[:, 5632:6656].rearrange("p (r n) -> p r n", r=2)
        GB = ar_a[:, 2048:3072].rearrange("p (r n) -> p r n", r=2)
        RAW_SLOTS = [a.rearrange("p (s n) -> p s n", s=2) for a in (ar_b[:, 4096:5120], ar_a[:, 2048:3072])]
        at = [4096, 4608] + [512 * j for j in range(NJ - 2)]
        uh = [ar_b[:, a:a + 256].bitcast(F16) for a in at]
        ul = [ar_b[:, a + 256:a + 512].bitcast(F16) for a in at]
        ar_c = sb("ar_c", [P, 16 * 256])
        M1 = ar_c[:, 0:2048].rearrange("p (r n) -> p r n", r=2)
        M2 = ar_c[:, 2048:3072]
        SQ = ar_c[:, 3072:4096]
        xn1 = ar_c[:, 0:1024].rearrange("p (r t c n) -> p r t c n", r=2, t=2, c=NC)
        hf1 = ar_c[:, 1024:2048].rearrange("p (r c n) -> p r c n", r=2, c=NC)
        ra = ar_c[:, 2048:3072].rearrange("p (r c s n) -> p r c s n", r=2, c=NC, s=2)
        rb = ar_c[:, 3072:4096].rearrange("p (r c s n) -> p r c s n", r=2, c=NC, s=2)
        XN = sb("XN", [P, 2, 2, DIM])
        XS = sb("XS", [P, NT, P])
        ot = [sb(f"ot_{s}", [P, 4, P], F16) for s in ("hi", "lo")]
        small = sb("small", [P, 160])
        mx1, nm1, sm1, rs1 = (small[:, 8 * i:8 * i + 8] for i in range(4))
        ss = small[:, 32:64].rearrange("p (r n) -> p r n", r=2)
        ssm = small[:, 64:80]
        rinv = small[:, 80:112].rearrange("p (r n) -> p r n", r=2)
        mxw = small[:, 112:120]
        nbw = small[:, 120:136].rearrange("p (r n) -> p r n", r=2)
        smw = small[:, 136:152].rearrange("p (r n) -> p r n", r=2)
        rsw = small[:, 152:156]
        yt = sb("yt", [P, 2, DIM])

        def mm3(pe, o, a, b, start, stop):
            pe.matmul(o, a[0], b[0], start=start, stop=False)
            pe.matmul(o, a[0], b[1], start=False, stop=False)
            return pe.matmul(o, a[1], b[0], start=False, stop=stop)

        def raw_slot(n):
            return RAW_SLOTS[(n + n // NT) % 2]

        setup(nc, ctx, locals())

        ctx2 = ctx.enter_context(ExitStack())
        names.clear()
        s_x = [sem(f"x_loaded{p}") for p in range(NT // 2)]
        s_mod, s_modc = sem("mod_loaded"), sem("next_mod_columns_loaded")
        s_bst, s_mv, s_rstd = sem("bn_done"), sem("meanvar_ready"), sem("rstd_ready")
        s_xn, s_xnT, s_hf = sem("xn_ready"), sem("xn_transposed"), sem("h_ready")
        s_hh, s_hl = sem("h_hi_ready"), sem("h_lo_ready")
        s_proj, s_m1a, s_v1, s_rot = sem("proj_done"), sem("rope_products"), sem("v_copied"), sem("rope_done")
        s_qkt, s_qk = sem("qk_transposed"), sem("qk_copied")
        s_s, s_mx, s_nm, s_e1 = sem("scores_done"), sem("rowmax_done"), sem("negmax_ready"), sem("probs_ready")
        s_ptr, s_pte, s_y, s_rs, s_yo, s_x2 = (sem("probsT_done"), sem("probsT_copied"), sem("attn_out_done"),
                                               sem("rowsum_inverse"), sem("attn_out_scaled"), sem("x_updated"))
        s_u0a, s_u0b, s_u0 = sem("ln2_ready"), sem("ln2_scaled"), sem("ffn_input_ready")
        s_t, s_t0, s_t0f = sem("transposes_done"), sem("first_transposes_done"), sem("first_transposes_read")
        s_tf = [sem(f"transpose_bank{i}_read") for i in range(2)]
        s_dh = sem("hT_hi_ready")
        s_qkv, s_ev = sem("qkv_bank_done"), sem("qkv_bank_copied")
        s_sq, s_ss, s_rm, s_rinv = sem("squares_ready"), sem("sumsq_ready"), sem("sumsq_clipped"), sem("inverse_norms")
        s_m, s_add, s_rope = sem("xpos_products"), sem("xpos_sum"), sem("xpos_ready")
        s_sim, s_mxw, s_nb, s_exp = sem("sim_bank_done"), sem("sim_max"), sem("sim_negmax"), sem("sim_bank_exp")
        s_rsw, s_pn, s_pv = sem("prob_inverse_sums"), sem("probs_normalised"), sem("pv_half_done")
        s_oh, s_ol, s_wo, s_res = sem("o_hi_ready"), sem("o_lo_ready"), sem("wo_done"), sem("attn_residual_done")
        s_xs = [sem(f"shifted_rows{p}") for p in range(DEPTH * NT // 2)]
        s_bn, s_lnmv, s_lnv, s_lnr, s_xnw = (sem("ln_stats"), sem("ln_meanvar"), sem("ln_var_eps"),
                                             sem("ln_rstd"), sem("ln_rows_ready"))
        s_nh = sem("ln_hi_ready")
        s_w1g, s_w1, s_g, s_ust, s_uh, s_ul = (sem("w1_gate_done"), sem("w1_done"), sem("gelu_ready"),
                                               sem("hidden_ready"), sem("hidden_hi"), sem("hidden_lo"))
        s_w2, s_u2 = sem("w2_done"), sem("mlp_residual_done")
        s_fa, s_fin, s_out = sem("final_scaled"), sem("final_ready"), sem("out_stored")
        s_v2, s_r2 = sem("var_eps_ready"), sem("pool_small")


        def window_step(l, s):
            proj, turn, att, back = (("E", s), ("F", s - 1), ("A", s - 2), ("J", s - 3))
            have = {k: 0 <= w < NT for k, w in (proj, turn, att, back)}
            e, t, a, j = (l * NT + w for _, w in (proj, turn, att, back))
            f = [("G", a, 0), ("G", a, 1), ("G", a, 2), ("n", a, 0), ("G", a, 3), ("J", j), ("E", e, 0),
                 ("H", a, 0), ("E", e, 1), ("n", a, 1), ("q", e), ("I", a, 0), ("H", a, 1), ("r", e), ("E", e, 2),
                 ("x", e, 0), ("F", t), ("x", e, 1), ("I", a, 1)]
            need = {"G": "A", "n": "A", "H": "A", "I": "A", "E": "E", "q": "E", "r": "E", "x": "E", "F": "F", "J": "J"}
            f = [q for q in f if have[need[q[0]]]]
            if s in (3, 4):
                f.append(("D", l, s - 1))
            if (l, s) == (0, 2):
                f.insert(f.index(("G", a, 3)) + 1, ("a", 0))
                f.append(("b", 4))
            if (l, s) == (0, 3):
                f.insert(f.index(("n", a, 1)) + 1, ("b", 6))
            if s == 5:
                f.append(("L", l, 0))
            if s == 6:
                f.insert(f.index(("n", a, 1)) + 1, ("K", l, 0))
                f.append(("N", l, 0))
            if s == 7:
                f.insert(f.index(("J", j)) + 1, ("L", l, 1))
                f.append(("K", l, 1))
            if s == NT:
                f = [("G", a, 0), ("G", a, 1), ("G", a, 2), ("n", a, 0), ("G", a, 3), ("J", j), ("N", l, 1), ("F", t),
                     ("n", a, 1), ("H", a, 0), ("W", l, 0, 0), ("I", a, 0), ("H", a, 1), ("w", l, 0, 0), ("I", a, 1)]
            if s == NT + 1:
                f = [("G", a, 0), ("G", a, 1), ("G", a, 2), ("n", a, 0), ("G", a, 3), ("J", j), ("W", l, 0, 1),
                     ("n", a, 1), ("H", a, 0), ("H", a, 1), ("L", l, 2), ("w", l, 0, 1),
                     ("I", a, 0), ("I", a, 1), ("K", l, 2), ("W", l, 0, 2), ("J", a), ("w", l, 0, 2), ("N", l, 2)]
            return f

        def mlp_steps(l):

            def pair(g, j):
                return [("W", l, g, j), ("w", l, g, j)]

            f = pair(0, 3) + [("L", l, 3), ("K", l, 3)] + pair(0, 4) + [("N", l, 3)] + pair(0, 5)
            f += pair(1, 0) + pair(1, 1)
            f += [("Y", l * NT + w) for w in range(GW)]
            if l + 1 < DEPTH:
                f += sum((pair(1, j) for j in range(2, NJ)), []) + [("D", l + 1, 0), ("D", l + 1, 1)] + pair(1, NJ)
            else:
                f += pair(1, 2) + pair(1, 3) + [("s", 0)] + pair(1, 4) + pair(1, 5) + [("t", 0)]
            if l + 1 < DEPTH:
                n = (l + 1) * NT
                f += [("E", n, 0), ("E", n, 1), ("q", n), ("E", n, 2), ("r", n)]
                f += [("Y", l * NT + GW), ("x", n, 0), ("Y", l * NT + GW + 1), ("x", n, 1)]
                f += [("Y", l * NT + w) for w in range(GW + 2, NT)]
            else:
                f += [("u", 0), ("Y", l * NT + GW), ("t", 1), ("u", 1)]
                f += [("Y", l * NT + w) for w in range(GW + 1, NT)]
            return f

        def schedule():
            f = []
            for l in range(DEPTH):
                for s in range(1, NT + 2):
                    f += window_step(l, s)
                f += mlp_steps(l)
            return f

        def plan_transposes(pieces):
            order = []
            for piece in pieces:
                if piece[0] in "DN":
                    order.append(piece)
                elif piece[0] in "FH":
                    order += [piece + (0,), piece + (1,)]
            return {key: u for u, key in enumerate(order)}

        FIRST = window_step(0, 1)[:5]
        BESIDE = {NT + 1: [("D", 0, 0), ("D", 0, 1)],
                  NT + 2: [("E", 0, 0), ("E", 0, 1), ("q", 0), ("E", 0, 2), ("r", 0), ("x", 0, 0), ("x", 0, 1)],
                  NT + 3: FIRST}
        PIECES = [q for q in schedule() if q not in FIRST]
        tuse = plan_transposes(PIECES)

        def w1_bank(l, g, j):
            return 0 if j % 2 or (g, j) == (0, 0) else 2

        def tbank(key):
            return 5 + tuse[key] % 2 if key in tuse else (4, 1)[key[2]]

        def t_done(key):
            return (s_t, tuse[key] + 1) if key in tuse else (s_t0, key[2] + 1)

        def t_read(key):
            return (s_tf[tuse[key] % 2], tuse[key] // 2 + 1) if key in tuse else (s_t0f, key[2] + 1)

        def pair_stats(dve, p, o, m):
            dve.wait_ge(s_x[p], 16)
            for t in range(2 * p, 2 * p + 2):
                last = dve.bn_stats(st[:, t, 0, :], X[:, t, :])
            last.then_inc(s_bst, 1)
            dve.wait_ge(s_bst, m + 1)
            for t in range(2 * p, 2 * p + 2):
                last = dve.bn_aggr(mv[:, t, :], st[:, t, 0, :])
            last.then_inc(s_mv, 1)

        def root(pool, count, lo, hi):
            pool.tensor_scalar(veps[:, lo:hi], mv[:, lo:hi, 1], EPS, None, ALU.add).then_inc(s_v2, 1)
            pool.wait_ge(s_v2, count)
            return pool.tensor_tensor(rstd[:, lo:hi], veps[:, lo:hi], neg_half[:, 0:hi - lo], ALU.pow)

        def pair_root(pool, p, m, count):
            pool.wait_ge(s_mv, m + 1)
            root(pool, count, 2 * p, 2 * p + 2).then_inc(s_rstd, 1)

        def pair_rows(dve, p, o, m):
            dve.wait_ge(s_rstd, m + 1)
            if o >= 2:
                dve.wait_ge(s_xnT, o - 1)
            for i in range(2):
                t = 2 * p + i
                last = dve.tensor_scalar(
                    xn1[:, p % 2, i, :, :].rearrange("p c (h q) -> p (c h) q", q=AD),
                    X[:, t, :].rearrange("p (q h) -> p h q", h=AH),
                    mv[:, t, 0:1], rstd[:, t:t + 1], ALU.subtract, ALU.mult)
            last.then_inc(s_xn, 1)

        def pair_transpose(pe, p, o):
            pe.wait_ge(s_xn, o + 1)
            if o >= 1:
                pe.wait_ge(s_hf, o)
            for t in range(2):
                for c in range(NC):
                    last = pe.transpose(ps[:, 5, c * 256 + t * P:c * 256 + (t + 1) * P],
                                        xn1[:, p % 2, t, c, :], id_f[:])
            last.then_inc(s_xnT, 1)

        def pair_affine(dve, p, o):
            dve.wait_ge(s_xnT, o + 1)
            if o >= 2:
                dve.wait_ge(s_hl, o - 1)
            for c in range(NC):
                last = dve.tensor_scalar(hf1[:, p % 2, c, :], ps[:, 5, c * 256:(c + 1) * 256],
                                         modc[:, NC + c:NC + c + 1], modc[:, c:c + 1], ALU.mult, ALU.add)
            last.then_inc(s_hf, 1)

        def pair_high(act, p, o):
            act.wait_ge(s_hf, o + 1)
            act.activation(ht[0][:, :, 1 + p * 256:1 + (p + 1) * 256], hf1[:, p % 2], ACT.Copy).then_inc(s_hh, 1)

        def pair_low(pool, p, o):
            pool.wait_ge(s_hh, o + 1)
            cols = slice(1 + p * 256, 1 + (p + 1) * 256)
            pool.tensor_tensor(ht[1][:, :, cols], hf1[:, p % 2], ht[0][:, :, cols], ALU.subtract).then_inc(s_hl, 1)

        def load_pair(sp, b, p):
            sp.dma_start(X[:, 2 * p:2 * p + 2, :],
                         x[b, 2 * p * P:(2 * p + 2) * P, :].rearrange("(t p) d -> p t d", p=P)).then_inc(s_x[p], 16)

        def clear_counts():
            engines = (nc.gpsimd, nc.vector, nc.scalar, nc.tensor, nc.sync)
            for i, s in enumerate(names):
                engines[i % len(engines)].sem_clear(s)
            nc.all_engine_barrier()

        block = nc.Block()
        with block:

            @block.sync
            def _(sp):
                sp.dma_start(modc[:, :], modc_all[:, 0, :]).then_inc(s_modc, 16)
                for p in range(2):
                    load_pair(sp, 0, p)

            @block.vector
            def _(dve):
                for p in range(2):
                    pair_stats(dve, p, p, p)
                for p in range(2):
                    pair_rows(dve, p, p, p)
                dve.wait_ge(s_modc, 16)
                for p in range(2):
                    pair_affine(dve, p, p)

            @block.gpsimd
            def _(pool):
                for p in range(2):
                    pair_root(pool, p, p, p + 1)
                for p in range(2):
                    pair_low(pool, p, p)

            @block.tensor
            def _(pe):
                for p in range(2):
                    pair_transpose(pe, p, p)

            @block.scalar
            def _(act):
                for p in range(2):
                    pair_high(act, p, p)

        clear_counts()

        with nc.Fori(0, BATCH) as b:
            block = nc.Block()
            with block:

                @block.sync
                def _(sp):
                    for p in range(2, NT // 2):
                        load_pair(sp, b, p)
                    sp.dma_start(modb[:, :, :],
                                 mod_rows[b, 2 * DIM:6 * DIM].rearrange("(k d) -> k d", k=4).partition_broadcast(P)
                                 ).then_inc(s_mod, 16)
                    sp.wait_ge(s_hf, 2)
                    sp.dma_start(modc[:, :], modc_all[:, (b + 1) % BATCH, :]).then_inc(s_modc, 16)
                    for l in range(DEPTH):
                        for w in range(NT):
                            sp.wait_ge(s_res, l * NT + w + 1)
                            sp.dma_start(XS[1:P, w, :], U[0:P - 1, w, P:DIM]).then_inc(s_xs[l * 4 + w // 2], 16)
                            if w:
                                sp.dma_start(XS[0:1, w, :], U[P - 1:P, w - 1, P:DIM]
                                             ).then_inc(s_xs[l * 4 + w // 2], 16)
                    for w in range(NT):
                        sp.wait_ge(s_fin, w + 1)
                        sp.dma_start(out[b, w * P:(w + 1) * P, :], U[:, w, :]).then_inc(s_out, 16)
                        if w == GW - 1:
                            for p in range(2):
                                load_pair(sp, (b + 1) % BATCH, p)
                    sp.wait_ge(s_out, 16 * NT)

                @block.tensor
                def _(pe):
                    def proj(t):
                        if t >= 4:
                            pe.wait_ge(s_hl, t // 2 - 1)
                        if t >= 1:
                            pe.wait_ge(s_v1, t)
                        for c in range(NC):
                            h = [q[:, c, 1 + t * P:1 + (t + 1) * P] for q in ht]
                            w = [q[:, c, :, :].rearrange("p s n -> p (s n)") for q in bd_p]
                            last = mm3(pe, ps[:, c, 0:3 * P], h, w, True, True)
                        last.then_inc(s_proj, 1)

                    def t_qk(t):
                        pe.wait_ge(s_rot, t + 1)
                        if t >= 1:
                            pe.wait_ge(s_qk, t)
                        for c in range(NC):
                            for s in range(2):
                                k = (c * 2 + s) * P
                                last = pe.transpose(ps[:, 4, k:k + P], ra[:, t % 2, c, s, :], id_f[:])
                        last.then_inc(s_qkt, 1)

                    def scores(i):
                        if i >= 1:
                            pe.wait_ge(s_e1, i)
                        pe.wait_ge(s_qk, i + 1)
                        n = (i + 1) * P
                        for kb in range((n + 511) // 512):
                            w = min(512, n - kb * 512)
                            bank = 2 + kb
                            for c in range(NC):
                                pe.matmul(ps[:, bank, 0:w], QK1[:, c, 0, i * P:(i + 1) * P],
                                          QK1[:, c, 1, kb * 512:kb * 512 + w], start=(c == 0),
                                          stop=(c == 1))
                        last = pe.matmul(ps[:, 2 + i // 4, (i % 4) * P:(i % 4 + 1) * P], id_b[:],
                                         mask_t[:, 0, P:2 * P], start=False, stop=True, skip_group_check=True)
                        last.then_inc(s_s, 1)

                    def probs_t(i):
                        pe.wait_ge(s_e1, i + 1)
                        for k4 in range(i // 4 + 1):
                            if i >= 1:
                                pe.wait_ge(s_pte, ptg[i])
                            if k4:
                                pe.wait_ge(s_hf, 2)
                            for kb in range(4 * k4, min(i + 1, 4 * k4 + 4)):
                                last = pe.transpose(ps[:, (7, 5)[k4], (kb % 4) * P:(kb % 4 + 1) * P],
                                                    P1[:, i % 2, kb * P:(kb + 1) * P], id_f[:])
                            last.then_inc(s_ptr, 1)

                    def attn_out(i):
                        pe.wait_ge(s_pte, ptg[i] + i // 4 + 1)
                        if i >= 1:
                            pe.wait_ge(s_yo, i)
                        for kb in range(i + 1):
                            last = pe.matmul(ps[:, 6, 0:DIM], PT1[:, i % 2, kb, :], V1[:, kb, :],
                                             start=(kb == 0), stop=(kb == i))
                        last.then_inc(s_y, 1)

                    def claim(key):
                        if key not in tuse:
                            pe.wait_ge((s_qk, s_v1)[key[2]], NT)
                        elif tuse[key] == 0:
                            pe.wait_ge(s_pte, ptg[NT])
                        elif tuse[key] == 1:
                            pe.wait_ge(s_yo, NT)
                        else:
                            pe.wait_ge(s_tf[tuse[key] % 2], tuse[key] // 2)
                        return tbank(key)

                    def rows_t(key, rows):
                        bank = claim(key)
                        for t in range(2):
                            for c in range(NC):
                                last = pe.transpose(ps[:, bank, c * 256 + t * P:c * 256 + (t + 1) * P],
                                                    rows(t)[:, c * P:(c + 1) * P], id_f[:])
                        last.then_inc(t_done(key)[0], 1)

                    def ffn(pieces):
                        for piece in pieces:
                            kind, n = piece[0], piece[1]
                            l, w = n // NT, n % NT
                            if kind == "t":
                                if n == 0:
                                    pe.wait_ge(s_tf[0], (len(tuse) + 1) // 2)
                                pair_transpose(pe, n, n + 2)
                            elif kind == "D":
                                l, p = piece[1:]
                                pe.wait_ge(s_u2 if l else s_u0, 2 * p + 2)
                                rows_t(piece, lambda t: U[:, 2 * p + t, :])
                            elif kind == "N":
                                l, p = piece[1:]
                                pe.wait_ge(s_xnw, l * 4 + p + 1)
                                rows_t(piece, lambda t: XN[:, p % 2, t, :])
                            elif kind == "E":
                                k = piece[2]
                                e = 3 * n + k
                                if k == 0 and w % 2 == 0:
                                    pe.wait_ge(*t_read(("D", l, w // 2)))
                                if e >= 2:
                                    pe.wait_ge(s_ev, e - 1)
                                elif e == 0:
                                    pe.wait_ge(s_v1, NT)
                                else:
                                    pe.wait_ge(*t_read(("D", 0, 1)))
                                if l and w == 0 and k < 2:
                                    pe.wait_ge(s_ust, l * NG * (NJ + 1) - 1 + k)
                                for c in range(NC):
                                    a = w * P + (1 - c)
                                    last = mm3(pe, ps[:, (e + l) % 2, :], [q[:, c, a:a + P] for q in ht],
                                               [q[:, l, c, k * INNER:(k + 1) * INNER] for q in wqkv_p], c == 0, c == 1)
                                last.then_inc(s_qkv, 1)
                            elif kind == "F":
                                pe.wait_ge(s_rope, n + 1)
                                for s in range(2):
                                    bank = claim(("F", n, s))
                                    for h in range(4):
                                        k = s * INNER + h * P
                                        last = pe.transpose(ps[:, bank, h * P:(h + 1) * P], M1[:, n % 2, k:k + P], id_f[:])
                                    last.then_inc(s_t, 1)
                            elif kind == "G":
                                k, m = piece[2], 4 * n + piece[2]
                                if k == 0:
                                    pe.wait_ge(*t_read(("F", n, 0)))
                                    pe.wait_ge(*t_read(("F", n, 1)))
                                if m >= 3:
                                    pe.wait_ge(s_exp, m - 2)
                                if l and w == 0 and k == 0:
                                    pe.wait_ge(s_u2, n)
                                bank, r = 2 + m % 3, 64 * (k % 2)
                                pe.matmul(ps[:, bank, :], id_b[:], mask_t[:, 0 if w else 1, :], start=True, stop=True)
                                for i in range(2):
                                    hp = 2 * (k // 2) + i
                                    for kb in range(0 if w else 1, 2):
                                        o = i * 256 + kb * P
                                        last = pe.matmul(ps[:, bank, o:o + P], QT[r:r + 64, n % 2, hp, :],
                                                         KT[r:r + 64, (n - 1 + kb) % 3, hp, :], start=False,
                                                         stop=True, skip_group_check=True)
                                last.then_inc(s_sim, 1)
                            elif kind == "H":
                                f = piece[2]
                                pe.wait_ge(s_pn, 2 * n + f + 1)
                                for q in range(2):
                                    bank = claim(("H", n, f, q))
                                    for k in range(4):
                                        last = pe.transpose(ps[:, bank, k * P:(k + 1) * P],
                                                            PW[:, f, q, k // 2, (k % 2) * P:(k % 2 + 1) * P], id_f[:])
                                    last.then_inc(s_t, 1)
                            elif kind == "I":
                                f = piece[2]
                                pe.wait_ge(*t_read(("H", n, f, 0)))
                                pe.wait_ge(*t_read(("H", n, f, 1)))
                                pe.wait_ge(s_ev, 3 * n + 3)
                                if f == 0 and n >= 1:
                                    pe.wait_ge(s_res, n)
                                for k in range(2):
                                    for kb in range(0 if w else 1, 2):
                                        for q in range(2):
                                            h = 4 * f + q + 2 * k
                                            last = pe.matmul(ps[64 * q:64 * q + 64, 7, (h // 2) * P:(h // 2 + 1) * P],
                                                             V[:, (n - 1 + kb) % 4, h * DH:(h + 1) * DH],
                                                             PTW[:, f, q, 2 * k + kb, :], start=(kb == (0 if w else 1)),
                                                             stop=(kb == 1), skip_group_check=True)
                                last.then_inc(s_pv, 1)
                            elif kind == "J":
                                pe.wait_ge(s_ol, n + 1)
                                for c in range(4):
                                    last = mm3(pe, ps[:, 7, 0:DIM], [q[:, c, :] for q in ot],
                                               [q[:, l, c, :] for q in wo_p], c == 0, c == 3)
                                last.then_inc(s_wo, 1)
                            elif kind == "W":
                                l, g, j = piece[1:]
                                v = (l * NG + g) * (NJ + 1) + j
                                if j == 0:
                                    pe.wait_ge(*t_read(("N", l, 2 * g)))
                                    pe.wait_ge(*t_read(("N", l, 2 * g + 1)))
                                bank = w1_bank(l, g, j)
                                if v >= 2:
                                    pe.wait_ge(s_ust, v if (g, j) == (0, 1) else v - 1)
                                elif v == 1:
                                    pe.wait_ge(s_ust, 1)
                                for i in range(2 if j < NJ else 1):
                                    m = P if j < NJ else GT + TAIL
                                    for c in range(NC):
                                        a = g * 512 + 1
                                        last = mm3(pe, ps[0:m, bank + i, :],
                                                   [q[:, l, c, 2 * j + i, 0:m] for q in w1_p],
                                                   [q[:, c, a:a + 512] for q in ht], c == 0, c == 1)
                                    last.then_inc(s_w1g if i == 0 else s_w1, 1)
                            elif kind == "Y":
                                if w % NT >= 2:
                                    pe.wait_ge(s_u2, n - 1)
                                a = (w % GW) * P
                                bank = (4, 7)[w % 2]
                                for j in range(NJ + 1):
                                    if w % GW == 0:
                                        pe.wait_ge(s_ul, (n // GW) * (NJ + 1) + j + 1)
                                    if j < NJ:
                                        hid = [q[j][:, a:a + P] for q in (uh, ul)]
                                        wt = [q[:, l, j, :] for q in w2_p]
                                    else:
                                        hid = [q[0:GT, a:a + P] for q in u_tail]
                                        wt = [q[0:GT, l, j, :] for q in w2_p]
                                    last = mm3(pe, ps[:, bank, 0:DIM], hid, wt, j == 0, j == NJ)
                                last.then_inc(s_w2, 1)

                    for t in range(NT + 4):
                        if t in (2, 4):
                            pair_transpose(pe, t // 2 + 1, t // 2 - 1)
                        if t < NT:
                            proj(t)
                        if 0 <= t - 2 < NT:
                            scores(t - 2)
                        if 0 <= t - 1 < NT:
                            t_qk(t - 1)
                        if 0 <= t - 3 < NT:
                            probs_t(t - 3)
                        ffn(BESIDE.get(t, []))
                        if t >= 4:
                            attn_out(t - 4)
                    ffn(PIECES)

                @block.scalar
                def _(act):
                    def v_copy(t):
                        act.wait_ge(s_m1a, t + 1)
                        src = ps[:, 0:2, 2 * P:3 * P].rearrange("p c (d h) -> p c d h", h=HPC)
                        act.activation(V1[:, t, :].rearrange("p (d c h) -> p c d h", c=NC, h=HPC), src,
                                       ACT.Copy).then_inc(s_v1, 1)

                    def qk_copy(t):
                        act.wait_ge(s_qkt, t + 1)
                        act.activation(QK1[:, :, :, t * P:(t + 1) * P],
                                       ps[:, 4, :].rearrange("p (c s n) -> p c s n", c=NC, s=2),
                                       ACT.Copy).then_inc(s_qk, 1)

                    def probs(i):
                        act.wait_ge(s_nm, i + 1)
                        n = (i + 1) * P
                        if i >= 2:
                            act.wait_ge(s_ptr, ptg[i - 1])
                        src = ps[:, 2:4, :].rearrange("p a n -> p (a n)")
                        act.activation(P1[:, i % 2, 0:n], src[:, 0:n], ACT.Exp, bias=nm1[:, i:i + 1], scale=GAMMA,
                                       accum_out=sm1[:, i:i + 1]).then_inc(s_e1, 1)

                    def ffn(pieces):
                        for piece in pieces:
                            kind, n = piece[0], piece[1]
                            if kind == "u":
                                pair_high(act, n, n + 2)
                            elif kind in "DN":
                                l, p = piece[1:]
                                act.wait_ge(*t_done(piece))
                                act.activation(ht[0][:, :, 1 + p * 256:1 + (p + 1) * 256],
                                               ps[:, tbank(piece), :].rearrange("p (c n) -> p c n", c=NC),
                                               ACT.Copy).then_inc(s_dh if kind == "D" else s_nh, 1)
                            elif kind == "E":
                                k = piece[2]
                                act.wait_ge(s_qkv, 3 * n + k + 1)
                                if k == 0 and n >= 2:
                                    act.wait_ge(s_m, n - 1)
                                if k == 2 and n >= 4:
                                    act.wait_ge(s_pv, 2 * (n - 2))
                                if n >= NT and n % NT < 2 and k == 0:
                                    act.wait_ge((s_ust, s_ul)[n % NT], (n // NT) * NG * (NJ + 1))
                                dst = raw_slot(n)[:, k, :] if k < 2 else V[:, n % 4, :]
                                act.activation(dst, ps[:, (3 * n + k + n // NT) % 2, :], ACT.Copy).then_inc(s_ev, 1)
                            elif kind == "q":
                                act.wait_ge(s_ev, 3 * n + 2)
                                if n >= 1:
                                    act.wait_ge(s_ss, n)
                                act.activation(SQ, raw_slot(n).rearrange("p s n -> p (s n)"),
                                               ACT.Square).then_inc(s_sq, 1)
                            elif kind == "F":
                                for s in range(2):
                                    key = ("F", n, s)
                                    act.wait_ge(*t_done(key))
                                    act.activation(KT[:, n % 3] if s else QT[:, n % 2],
                                                   ps[:, tbank(key), :].rearrange("p (h n) -> p h n", h=4),
                                                   ACT.Copy).then_inc(t_read(key)[0], 1)
                            elif kind == "G":
                                k, m = piece[2], 4 * n + piece[2]
                                act.wait_ge(s_nb, m + 1)
                                for i in range(2):
                                    h = 4 * (k // 2) + k % 2 + 2 * i
                                    last = act.activation(PW[:, k // 2, k % 2, i, :],
                                                          ps[:, 2 + m % 3, i * 256:(i + 1) * 256], ACT.Exp,
                                                          bias=nbw[:, n % 2, h:h + 1], scale=rinv[:, n % 2, h:h + 1],
                                                          accum_out=smw[:, n % 2, h:h + 1])
                                last.then_inc(s_exp, 1)
                            elif kind == "H":
                                key = ("H", n, piece[2], 1)
                                act.wait_ge(*t_done(key))
                                if 2 * n + piece[2] >= 2:
                                    act.wait_ge(s_pv, 2 * n + piece[2] - 1)
                                act.activation(PTW[:, piece[2], 1],
                                               ps[:, tbank(key), :].rearrange("p (k n) -> p k n", k=4),
                                               ACT.Copy).then_inc(t_read(key)[0], 1)
                            elif kind == "I" and piece[2] == 1:
                                act.wait_ge(s_pv, 2 * n + 2)
                                act.activation(ot[0][:, :, :], ps[:, 7, :].rearrange("p (h n) -> p h n", h=4),
                                               ACT.Copy).then_inc(s_oh, 1)
                            elif kind == "w":
                                l, g, j = piece[1:]
                                v = (l * NG + g) * (NJ + 1) + j
                                act.wait_ge(s_w1g, v + 1)
                                if v >= 2:
                                    act.wait_ge(s_ust, v - 1)
                                if j < NJ:
                                    dst, src = GB[:, v % 2, :], ps[:, w1_bank(l, g, j), :]
                                    bias = bias1[:, l, 2 * j:2 * j + 1]
                                else:
                                    dst, src = GB[0:TAIL, v % 2, :], ps[GT:GT + TAIL, w1_bank(l, g, j), :]
                                    bias = bias1[GT:GT + TAIL, l, 2 * j:2 * j + 1]
                                act.activation(dst, src, ACT.Gelu, bias=bias).then_inc(s_g, 1)
                                todo = [v - 1] if j > 0 else []
                                if j == NJ:
                                    todo.append(v)
                                for q in todo:
                                    jj = q % (NJ + 1)
                                    act.wait_ge(s_ust, q + 1)
                                    if jj == 0 and q > 0:
                                        act.wait_ge(s_w2, (q // (NJ + 1)) * GW)
                                    rows = P if jj < NJ else TAIL
                                    dst = uh[jj] if jj < NJ else u_tail[0][0:TAIL, :]
                                    act.activation(dst, UB[0:rows, q % 2, :], ACT.Copy).then_inc(s_uh, 1)

                    for t in range(NT + 4):
                        if t in (2, 4):
                            pair_high(act, t // 2 + 1, t // 2 - 1)
                        if t < NT:
                            v_copy(t)
                        if 0 <= t - 2 < NT:
                            probs(t - 2)
                        if 0 <= t - 1 < NT:
                            qk_copy(t - 1)
                        ffn(BESIDE.get(t, []))
                    ffn(PIECES)

                @block.vector
                def _(dve):
                    def rope1(t):
                        dve.wait_ge(s_proj, t + 1)
                        if t >= 2:
                            dve.wait_ge(s_qkt, t - 1)
                        for c in range(NC):
                            src = ps[:, c, 0:2 * P].rearrange("p (s i e) -> p s i e", s=2, e=2)
                            a = ra[:, t % 2, c].rearrange("p s (i e) -> p s i e", e=2)
                            bb = rb[:, t % 2, c].rearrange("p s (i e) -> p s i e", e=2)
                            cs = cos_t[:, t, c, :].unsqueeze(1).broadcast_to((P, 2, 64))
                            sn = sin_t[:, t, c, :].unsqueeze(1).broadcast_to((P, 2, 64))
                            for e in range(2):
                                dve.tensor_tensor(a[:, :, :, e], src[:, :, :, e], cs, ALU.mult)
                            dve.scalar_tensor_tensor(out=bb[:, :, :, 0], in0=src[:, :, :, 1], scalar=-1.0, in1=sn,
                                                     op0=ALU.mult, op1=ALU.mult)
                            last = dve.tensor_tensor(bb[:, :, :, 1], src[:, :, :, 0], sn, ALU.mult)
                        last.then_inc(s_m1a, 1)

                    def row_max(i):
                        dve.wait_ge(s_s, i + 1)
                        src = ps[:, 2:4, :].rearrange("p a n -> p (a n)")
                        dve.tensor_reduce(mx1[:, i:i + 1], src[:, 0:(i + 1) * P], AX, ALU.max).then_inc(s_mx, 1)
                        dve.wait_ge(s_mx, i + 1)
                        dve.tensor_scalar(nm1[:, i:i + 1], mx1[:, i:i + 1], -GAMMA, None, ALU.mult).then_inc(s_nm, 1)

                    def probs_copy(i):
                        for k4 in range(i // 4 + 1):
                            g = ptg[i] + k4
                            dve.wait_ge(s_ptr, g + 1)
                            if i >= 2 and k4 == 0:
                                dve.wait_ge(s_y, i - 1)
                            m = min(4, i + 1 - 4 * k4)
                            dve.tensor_copy(PT1[:, i % 2, 4 * k4:4 * k4 + m, :],
                                            ps[:, (7, 5)[k4], 0:m * P].rearrange("p (k n) -> p k n", n=P)
                                            ).then_inc(s_pte, 1)

                    def y_scale(i):
                        if i == 0:
                            dve.wait_ge(s_mod, 16)
                        dve.wait_ge(s_e1, i + 1)
                        dve.reciprocal(rs1[:, i:i + 1], sm1[:, i:i + 1]).then_inc(s_rs, 1)
                        dve.wait_ge(s_rs, i + 1)
                        dve.wait_ge(s_y, i + 1)
                        dve.scalar_tensor_tensor(out=yt[:, i % 2, :], in0=ps[:, 6, 0:DIM],
                                                 scalar=rs1[:, i:i + 1], in1=modb[:, 0, :], op0=ALU.mult,
                                                 op1=ALU.mult).then_inc(s_yo, 1)
                        dve.wait_ge(s_yo, i + 1)
                        dve.tensor_tensor(X[:, i, :], X[:, i, :], yt[:, i % 2, :], ALU.add).then_inc(s_x2, 1)

                    def ln2_stats(g):
                        dve.wait_ge(s_x2, 4 * g + 4)
                        for t in range(4 * g, 4 * g + 4):
                            last = dve.bn_stats(st[:, t, 0, :], X[:, t, :])
                        last.then_inc(s_bst, 1)
                        dve.wait_ge(s_bst, 3 + g)
                        for t in range(4 * g, 4 * g + 4):
                            last = dve.bn_aggr(mv[:, t, :], st[:, t, 0, :])
                        last.then_inc(s_mv, 1)

                    def ln2_rows(lo, hi):
                        dve.wait_ge(s_mv, 3 + lo // 4)
                        for t in range(lo, hi):
                            dve.scalar_tensor_tensor(out=U[:, t, :], in0=X[:, t, :], scalar=mv[:, t, 0:1],
                                                     in1=modb[:, 2, :], op0=ALU.subtract, op1=ALU.mult).then_inc(s_u0b, 1)
                        dve.wait_ge(s_rstd, 3 + lo // 4)
                        for t in range(lo, hi):
                            dve.wait_ge(s_u0b, t + 1)
                            dve.scalar_tensor_tensor(out=U[:, t, :], in0=U[:, t, :], scalar=rstd[:, t:t + 1],
                                                     in1=modb[:, 1, :], op0=ALU.mult, op1=ALU.add).then_inc(s_u0, 1)

                    def norm(n, f):
                        dve.wait_ge(s_exp, 4 * n + 2 * f + 2)
                        dve.reciprocal(rsw, smw[:, n % 2, 4 * f:4 * f + 4]).then_inc(s_rsw, 1)
                        dve.wait_ge(s_rsw, 2 * n + f + 1)
                        for q in range(2):
                            for i in range(2):
                                k = q + 2 * i
                                pw = PW[:, f, q, i, :]
                                last = dve.tensor_scalar(pw, pw, rsw[:, k:k + 1], None, ALU.mult)
                        last.then_inc(s_pn, 1)

                    def ffn(pieces):
                        for piece in pieces:
                            kind, n = piece[0], piece[1]
                            l, w = n // NT, n % NT
                            if kind == "s":
                                pair_stats(dve, 0, 2, 4)
                                pair_stats(dve, 1, 3, 5)
                            elif kind == "t":
                                if n == 0:
                                    for p in range(2):
                                        pair_rows(dve, p, p + 2, p + 4)
                            elif kind == "u":
                                if n == 0:
                                    dve.wait_ge(s_modc, 16)
                                pair_affine(dve, n, n + 2)
                            elif kind == "a":
                                ln2_stats(1)
                            elif kind == "b":
                                ln2_rows(n, n + 2)
                            elif kind in "DN":
                                l, p = piece[1:]
                                dve.wait_ge(s_dh if kind == "D" else s_nh, l * 4 + p + 1)
                                cols = slice(1 + p * 256, 1 + (p + 1) * 256)
                                dve.tensor_tensor(ht[1][:, :, cols],
                                                  ps[:, tbank(piece), :].rearrange("p (c n) -> p c n", c=NC),
                                                  ht[0][:, :, cols], ALU.subtract).then_inc(t_read(piece)[0], 1)
                            elif kind == "r":
                                dve.wait_ge(s_sq, n + 1)
                                dve.tensor_reduce(ss[:, n % 2, :], SQ.rearrange("p (h d) -> p h d", d=DH), AX,
                                                  ALU.add).then_inc(s_ss, 1)
                            elif kind == "x":
                                raw = raw_slot(n).rearrange("p s (h d) -> p s h d", d=DH)
                                m1 = M1[:, n % 2, :].rearrange("p (s h d) -> p s h d", s=2, d=DH)
                                m2 = M2.rearrange("p (s h d) -> p s h d", s=2, d=DH)
                                cs = xp_t[:, l, w, 0:2, :].unsqueeze(2).broadcast_to((P, 2, HEADS, DH))
                                sn = xp_t[:, l, w, 2:4, :].unsqueeze(2).broadcast_to((P, 2, HEADS, DH))
                                if piece[2] == 0:
                                    if n >= 2:
                                        dve.wait_ge(*t_done(("F", n - 2, 1)))
                                    dve.wait_ge(s_ev, 3 * n + 2)
                                    dve.tensor_tensor(m1, raw, cs, ALU.mult)
                                    continue
                                if n >= 1:
                                    dve.wait_ge(s_add, n)
                                for e in range(2):
                                    lo, hi = slice(32 * e, 32 * e + 32), slice(32 - 32 * e, 64 - 32 * e)
                                    last = dve.tensor_tensor(m2[:, :, :, lo], raw[:, :, :, hi], sn[:, :, :, lo], ALU.mult)
                                last.then_inc(s_m, 1)
                            elif kind == "G":
                                k, m = piece[2], 4 * n + piece[2]
                                h = 4 * (k // 2) + k % 2
                                dve.wait_ge(s_sim, m + 1)
                                dve.tensor_reduce(mxw[:, h:h + 3:2], ps[:, 2 + m % 3, :].rearrange("p (i n) -> p i n", i=2),
                                                  AX, ALU.max).then_inc(s_mxw, 1)
                                dve.wait_ge(s_mxw, m + 1)
                                dve.wait_ge(s_rinv, n + 1)
                                dve.scalar_tensor_tensor(out=nbw[:, n % 2, h:h + 3:2], in0=mxw[:, h:h + 3:2], scalar=-1.0,
                                                         in1=rinv[:, n % 2, h:h + 3:2], op0=ALU.mult,
                                                         op1=ALU.mult).then_inc(s_nb, 1)
                            elif kind == "n":
                                norm(n, piece[2])
                            elif kind == "H":
                                key = ("H", n, piece[2], 0)
                                dve.wait_ge(*t_done(key))
                                if 2 * n + piece[2] >= 2:
                                    dve.wait_ge(s_pv, 2 * n + piece[2] - 1)
                                dve.tensor_copy(PTW[:, piece[2], 0],
                                                ps[:, tbank(key), :].rearrange("p (k n) -> p k n", k=4)
                                                ).then_inc(t_read(key)[0], 1)
                            elif kind == "I" and piece[2] == 1:
                                dve.wait_ge(s_oh, n + 1)
                                dve.tensor_tensor(ot[1][:, :, :], ps[:, 7, :].rearrange("p (h n) -> p h n", h=4),
                                                  ot[0][:, :, :], ALU.subtract).then_inc(s_ol, 1)
                            elif kind == "J":
                                dve.wait_ge(s_wo, n + 1)
                                dve.tensor_tensor(U[:, w, :], ps[:, 7, 0:DIM], U[:, w, :], ALU.add).then_inc(s_res, 1)
                            elif kind == "L":
                                l, p = piece[1:]
                                q = l * 4 + p
                                dve.wait_ge(s_xs[q], 16 * (4 - (p == 0)))
                                dve.wait_ge(s_res, l * NT + 2 * p + 2)
                                for w in range(2 * p, 2 * p + 2):
                                    dve.bn_stats(st[:, w, 0, :], U[:, w, 0:P])
                                    last = dve.bn_stats(st[:, w, 1, :], XS[:, w, :])
                                last.then_inc(s_bn, 1)
                                dve.wait_ge(s_bn, q + 1)
                                for w in range(2 * p, 2 * p + 2):
                                    last = dve.bn_aggr(mv[:, w, :], st[:, w, :, :].rearrange("p a b -> p (a b)"))
                                last.then_inc(s_lnmv, 1)
                            elif kind == "K":
                                l, p = piece[1:]
                                dve.wait_ge(s_lnr, l * 4 + p + 1)
                                if l * 4 + p >= 2:
                                    pl, pp = divmod(l * 4 + p - 2, 4)
                                    dve.wait_ge(*t_done(("N", pl, pp)))
                                for i in range(2):
                                    w = 2 * p + i
                                    dve.tensor_scalar(XN[:, p % 2, i, 0:P], U[:, w, 0:P], mv[:, w, 0:1],
                                                      rstd[:, w:w + 1], ALU.subtract, ALU.mult)
                                    last = dve.tensor_scalar(XN[:, p % 2, i, P:DIM], XS[:, w, :], mv[:, w, 0:1],
                                                             rstd[:, w:w + 1], ALU.subtract, ALU.mult)
                                last.then_inc(s_xnw, 1)
                            elif kind == "w":
                                l, g, j = piece[1:]
                                v = (l * NG + g) * (NJ + 1) + j
                                dve.wait_ge(s_g, v + 1)
                                if j < NJ:
                                    dve.wait_ge(s_w1, (l * NG + g) * NJ + j + 1)
                                if v >= 2:
                                    dve.wait_ge(s_ul, v - 1)
                                rows = P if j < NJ else TAIL
                                src = ps[0:rows, w1_bank(l, g, j) + (1 if j < NJ else 0), :]
                                dve.scalar_tensor_tensor(out=UB[0:rows, v % 2, :], in0=src,
                                                         scalar=bias1[0:rows, l, min(2 * j + 1, 2 * NJ):min(2 * j + 1, 2 * NJ) + 1],
                                                         in1=GB[0:rows, v % 2, :], op0=ALU.add,
                                                         op1=ALU.mult).then_inc(s_ust, 1)
                            elif kind == "Y":
                                dve.wait_ge(s_w2, n + 1)
                                dve.tensor_tensor(U[:, w, :], ps[:, (4, 7)[w % 2], 0:DIM], U[:, w, :],
                                                  ALU.add).then_inc(s_u2, 1)
                                if l == DEPTH - 1:
                                    dve.wait_ge(s_u2, n + 1)
                                    dve.tensor_tensor(U[:, w, :], U[:, w, :], modb[:, 3, :], ALU.mult).then_inc(s_fa, 1)
                                    dve.wait_ge(s_fa, w + 1)
                                    dve.tensor_tensor(U[:, w, :], U[:, w, :], X[:, w, :], ALU.add).then_inc(s_fin, 1)

                    for t in range(NT + 4):
                        if t < NT:
                            rope1(t)
                        if t == 0:
                            pair_stats(dve, 2, 0, 0)
                            pair_stats(dve, 3, 1, 1)
                        elif t <= 2:
                            pair_rows(dve, t + 1, t - 1, t - 1)
                        if t in (2, 4):
                            pair_affine(dve, t // 2 + 1, t // 2 - 1)
                        if t == NT:
                            ln2_stats(0)
                        if 0 <= t - 2 < NT:
                            row_max(t - 2)
                        if 0 <= t - 3 < NT:
                            probs_copy(t - 3)
                        if t == NT:
                            ln2_rows(0, 4)
                        ffn(BESIDE.get(t, []))
                        if t >= 4:
                            y_scale(t - 4)
                    ffn(PIECES)

                @block.gpsimd
                def _(pool):
                    def ffn(pieces):
                        for piece in pieces:
                            kind, n = piece[0], piece[1]
                            l, w = n // NT, n % NT
                            if kind == "s":
                                for p in range(2):
                                    pair_root(pool, p, p + 4, 5 + DEPTH * 4 + p)
                            elif kind == "u":
                                pair_low(pool, n, n + 2)
                            elif kind == "a":
                                pool.wait_ge(s_mv, 4)
                                root(pool, 4, 4, 8).then_inc(s_rstd, 1)
                            elif kind == "r":
                                pool.wait_ge(s_ss, n + 1)
                                pool.tensor_scalar(ssm, ss[:, n % 2, :], 1e-24, None, ALU.max).then_inc(s_rm, 1)
                                pool.wait_ge(s_rm, n + 1)
                                pool.tensor_tensor(rinv[:, n % 2, :], ssm, neg_half[:, 0:16], ALU.pow).then_inc(s_rinv, 1)
                            elif kind == "x" and piece[2] == 1:
                                pool.wait_ge(s_m, n + 1)
                                pool.tensor_tensor(M1[:, n % 2, :], M1[:, n % 2, :], M2, ALU.add).then_inc(s_add, 1)
                                pool.wait_ge(s_add, n + 1)
                                pool.wait_ge(s_rinv, n + 1)
                                kk = M1[:, n % 2, INNER:2 * INNER].rearrange("p (h d) -> p h d", d=DH)
                                pool.tensor_tensor(kk, kk, rinv[:, n % 2, 8:16].unsqueeze(2).broadcast_to((P, HEADS, DH)),
                                                   ALU.mult).then_inc(s_rope, 1)
                            elif kind == "L":
                                l, p = piece[1:]
                                pool.wait_ge(s_lnmv, l * 4 + p + 1)
                                root(pool, 5 + l * 4 + p, 2 * p, 2 * p + 2).then_inc(s_lnr, 1)
                            elif kind == "w":
                                l, g, j = piece[1:]
                                v = (l * NG + g) * (NJ + 1) + j
                                pool.wait_ge(s_uh, v + 1)
                                rows = P if j < NJ else TAIL
                                hi = uh[j] if j < NJ else u_tail[0][0:TAIL, :]
                                lo = ul[j] if j < NJ else u_tail[1][0:TAIL, :]
                                pool.tensor_tensor(lo, UB[0:rows, v % 2, :], hi, ALU.subtract).then_inc(s_ul, 1)

                    for p in (2, 3):
                        pair_root(pool, p, p - 2, p - 1)
                    for t in range(NT + 4):
                        if t in (2, 4):
                            pair_low(pool, t // 2 + 1, t // 2 - 1)
                        if t < NT:
                            pool.wait_ge(s_m1a, t + 1)
                            a = ra[:, t % 2].rearrange("p c s n -> p (c s n)")
                            pool.tensor_tensor(a, a, rb[:, t % 2].rearrange("p c s n -> p (c s n)"),
                                               ALU.add).then_inc(s_rot, 1)
                        if t == NT:
                            pool.wait_ge(s_mv, 3)
                            root(pool, 3, 0, 4).then_inc(s_rstd, 1)
                        ffn(BESIDE.get(t, []))
                    ffn(PIECES)

            clear_counts()


ptg = [sum(k // 4 + 1 for k in range(i)) for i in range(NT + 1)]


def setup(nc, ctx, v):
    ps, ar_a, ar_b, ar_c, xu = v["ps"], v["ar_a"], v["ar_b"], v["ar_c"], v["xu"]
    wqkv_p, wo_p, w1_p, w2_p, bd_p = v["wqkv_p"], v["wo_p"], v["w1_p"], v["w2_p"], v["bd_p"]
    id_f, id_b, mask_t, xp_t, bias1 = v["id_f"], v["id_b"], v["mask_t"], v["xp_t"], v["bias1"]
    u_tail, ht, XS = v["u_tail"], v["ht"], v["XS"]
    sem = v["sem"]

    xu_f = xu[:, :, :, :].rearrange("p a t d -> p (a t d)")
    st_qkv = ar_a[:, 0:6144].rearrange("p (l c n) -> p l c n", l=DEPTH, c=NC)
    st_w2 = ar_b[:, 0:2560].rearrange("p (l j n) -> p l j n", l=DEPTH, j=NJ)
    st_w2t = ar_b[0:GT, 2560:3072].rearrange("p (l n) -> p l n", l=DEPTH)
    st_wo = ar_b[:, 3072:5120].rearrange("p (l c n) -> p l c n", l=DEPTH, c=4)
    st_w1 = [xu_f[:, 0:4 * HID].rearrange("p (c n) -> p c n", c=NC),
             ar_c[:, 0:4 * HID].rearrange("p (c n) -> p c n", c=NC)]
    o = 4 * HID
    w_rep = xu_f[:, o:o + 768].rearrange("p (s n) -> p s n", s=3)
    cT = xu_f[:, o + 768:o + 784].rearrange("p (c n) -> p c n", c=NC)
    c_e = xu_f[:, o + 784:o + 800].rearrange("p (c n) -> p c n", c=NC)
    silu = xu_f[:, o + 800:o + 816].rearrange("p (c n) -> p c n", c=NC)
    lgb = xu_f[:, o + 816:o + 824].rearrange("p (k l c) -> p k l c", k=2, l=DEPTH)
    qks = xu_f[:, o + 824:o + 824 + 512].rearrange("p (l k d) -> p l k d", l=DEPTH, k=4)
    w_mod = ar_a[:, 0:3072].rearrange("p (c n) -> p c n", c=NC)
    mrow = ar_a[0:BATCH, 3072:4608]
    mtmp = ar_a[0:BATCH, 4608:5120]
    xp_base = ar_a[:, 3072:3072 + 2048].rearrange("p (t k d) -> p t k d", t=NT, k=4)
    bd_f = ar_a[:, 5120:5120 + 768].rearrange("p (c s n) -> p c s n", c=NC, s=3)
    m_f = ar_b[:, 0:1024].rearrange("p (a n) -> p a n", a=2)

    l_qkv, l_wo, l_w1, l_w2, l_rep, l_small, l_tab = (sem(f"load_{n}") for n in
                                                      ("qkv", "wo", "w1", "w2", "rep", "small", "tables"))
    z_id, z_id2, z_w2, z_mask, z_mask2, z_rest = (sem(n) for n in ("id_zero", "id_ready", "w2_tail_zero", "mask_zero",
                                                                   "mask_ready", "rest_filled"))
    z_bias, z_tail = sem("bias_zero"), sem("w1_tail_zero")
    hi_done, lo_done = sem("setup_hi"), sem("setup_lo")
    lbw, w1s, bias_done = sem("lb_w1_done"), sem("w1_scaled"), sem("bias_done")
    bd_a, bd_b = sem("bd_first"), sem("bd_ready")
    e_done, e1_done, e2_done, e3_done = sem("silu_exp"), sem("silu_plus1"), sem("silu_recip"), sem("silu_ready")
    l_mod, l_xp, mm_done, row_done, row_t, mod_done, mod_out, xp_done = (sem(n) for n in (
        "load_wmod", "load_xpos", "mod_product", "mod_row", "mod_tmp", "mod_changed", "mod_stored", "xpos_scaled"))
    mask_used, mod_in = sem("masks_cast"), sem("mod_columns_loaded")

    block = nc.Block()
    with block:
        @block.sync
        def _(sp):
            for l in range(DEPTH):
                sp.dma_start(st_w1[l], v["w1"][l].rearrange("(c p) n -> p c n", p=P)).then_inc(l_w1, 16)
            for k, src in enumerate((v["ln_g"], v["ln_b"])):
                for l in range(DEPTH):
                    sp.dma_start(lgb[:, k, l, :], src[l].rearrange("(c p) -> p c", p=P)).then_inc(l_small, 16)
            for c in range(NC):
                sp.dma_start(cT[:, c, :], v["cond"][:, c * P:(c + 1) * P].rearrange("b p -> p b")).then_inc(l_small, 16)
            sp.wait_ge(z_bias, 1)
            for l in range(DEPTH):
                for i, base in enumerate((HID, 0)):
                    sp.dma_start(bias1[:, l, i:2 * NJ:2],
                                 v["b1"][l, base:base + NJ * P].rearrange("(j p) -> p j", p=P)).then_inc(l_small, 16)
                    r = (GT, 0)[i]
                    sp.dma_start(bias1[r:r + TAIL, l, 2 * NJ:2 * NJ + 1],
                                 v["b1"][l, base + NJ * P:base + HID].unsqueeze(1)).then_inc(l_small, 16)
            for l in range(DEPTH):
                for k, src in enumerate((v["q_scale"], v["k_scale"])):
                    sp.dma_start(qks[:, l, k, :], src[l].partition_broadcast(P)).then_inc(l_small, 16)
                    for e in range(2):
                        sp.dma_start(qks[:, l, 2 + k, 32 * e:32 * e + 32],
                                     src[l, 32 - 32 * e:64 - 32 * e].partition_broadcast(P)).then_inc(l_small, 16)
            sp.wait_ge(hi_done, 2)
            sp.wait_ge(lo_done, 2)
            sp.dma_start(w_mod, v["wmod"].rearrange("(c p) n -> p c n", p=P)).then_inc(l_mod, 16)
            sp.wait_ge(mod_done, 1)
            sp.dma_start(v["mod_rows"], mrow).then_inc(mod_out, 16)
            sp.wait_ge(mod_out, 16)
            sp.dma_start(xp_base, v["xpos"]).then_inc(l_xp, 16)
            for k in range(2):
                for c in range(NC):
                    for h in range(HPC):
                        a = k * DIM + c * HPC + h
                        src = v["mod_rows"][:, a:(k + 1) * DIM:AH].rearrange("b q -> q b")
                        sp.dma_start(v["modc_all"][h * AD:(h + 1) * AD, :, k * NC + c], src).then_inc(mod_in, 16)
            sp.wait_ge(mod_in, 16 * 2 * NC * HPC)
            sp.wait_ge(l_tab, 32)

        @block.scalar
        def _(act):
            act.dma_start(st_qkv, v["wqkv"].rearrange("l (c p) n -> p l c n", p=P)).then_inc(l_qkv, 16)
            act.dma_start(st_wo, v["wo"].rearrange("l (c p) n -> p l c n", p=P)).then_inc(l_wo, 16)
            act.wait_ge(z_w2, 1)
            for l in range(DEPTH):
                act.dma_start(st_w2[:, l], v["w2"][l, 0:NJ * P].rearrange("(j p) n -> p j n", p=P)).then_inc(l_w2, 16)
                act.dma_start(st_w2t[0:TAIL, l, :], v["w2"][l, NJ * P:HID, :]).then_inc(l_w2, 16)
                act.dma_start(st_w2t[TAIL:TAIL + 1, l, :], v["b2"][l:l + 1, :]).then_inc(l_w2, 16)
            for s, src in enumerate((v["w_q"], v["w_k"], v["w_v"])):
                for h in range(HPC):
                    act.dma_start(w_rep[h * AD:(h + 1) * AD, s, :], src.rearrange("q d h -> q (d h)")).then_inc(l_rep, 16)
            act.dma_start(v["cos_t"][:, :, :, :], v["rope_cos"]).then_inc(l_tab, 16)
            act.dma_start(v["sin_t"][:, :, :, :], v["rope_sin"]).then_inc(l_tab, 16)
            act.wait_ge(l_qkv, 16)
            for l in range(DEPTH):
                act.activation(wqkv_p[0][:, l], st_qkv[:, l], ACT.Copy).then_inc(hi_done, 1)
            act.wait_ge(l_wo, 16)
            for l in range(DEPTH):
                act.activation(wo_p[0][:, l], st_wo[:, l], ACT.Copy).then_inc(hi_done, 1)
            act.wait_ge(l_w2, 16 * 3 * DEPTH)
            for l in range(DEPTH):
                act.activation(w2_p[0][:, l, 0:NJ, :], st_w2[:, l], ACT.Copy)
                act.activation(w2_p[0][0:GT, l, NJ, :], st_w2t[:, l, :], ACT.Copy).then_inc(hi_done, 1)
            act.wait_ge(z_tail, 1)
            for l in range(DEPTH):
                act.wait_ge(w1s, l + 1)
                for dst, src in w1_blocks(w1_p[0], st_w1, l):
                    last = act.activation(dst, src, ACT.Copy)
                last.then_inc(hi_done, 1)
            act.wait_ge(bd_b, 1)
            act.activation(bd_p[0][:, :, :, :], bd_f, ACT.Copy).then_inc(hi_done, 1)
            act.wait_ge(l_small, 16 * N_SMALL)
            act.activation(c_e, cT, ACT.Exp, scale=-1.0).then_inc(e_done, 1)
            act.wait_ge(mm_done, 1)
            act.activation(mrow, ps[0:BATCH, 4:7, :].rearrange("p a n -> p (a n)"), ACT.Copy).then_inc(row_done, 1)

        @block.vector
        def _(dve):
            dve.memset(bias1[:, :, :], 0.0).then_inc(z_bias, 1)
            dve.memset(st_w2t, 0.0).then_inc(z_w2, 1)
            for q in w1_p:
                last = dve.memset(q[:, :, :, 2 * NJ, :], 0.0)
            last.then_inc(z_tail, 1)
            dve.memset(v["neg_half"][:, :], -0.5)
            dve.memset(u_tail[0][:, :], 1.0)
            dve.memset(u_tail[1][:, :], 0.0)
            for q in ht:
                dve.memset(q[:, :, :], 0.0)
            dve.memset(XS[:, 0, :], 0.0).then_inc(z_rest, 1)
            for l in range(DEPTH):
                dve.wait_ge(hi_done, l + 1)
                dve.tensor_tensor(wqkv_p[1][:, l], st_qkv[:, l], wqkv_p[0][:, l], ALU.subtract).then_inc(lo_done, 1)
            for l in range(DEPTH):
                dve.wait_ge(hi_done, DEPTH + l + 1)
                dve.tensor_tensor(wo_p[1][:, l], st_wo[:, l], wo_p[0][:, l], ALU.subtract)
            for l in range(DEPTH):
                dve.wait_ge(hi_done, 2 * DEPTH + l + 1)
                dve.tensor_tensor(w2_p[1][:, l, 0:NJ, :], st_w2[:, l], w2_p[0][:, l, 0:NJ, :], ALU.subtract)
                dve.tensor_tensor(w2_p[1][0:GT, l, NJ, :], st_w2t[:, l, :], w2_p[0][0:GT, l, NJ, :],
                                  ALU.subtract).then_inc(lo_done, 1)
            dve.wait_ge(l_small, 16 * N_SMALL)
            dve.wait_ge(lbw, 1)
            for l in range(DEPTH):
                for c in range(NC):
                    last = dve.tensor_scalar(st_w1[l][:, c, :], st_w1[l][:, c, :], lgb[:, 0, l, c:c + 1], None, ALU.mult)
                last.then_inc(w1s, 1)
            dve.wait_ge(z_bias, 1)
            for l in range(DEPTH):
                k = l * NB1
                dve.tensor_tensor(bias1[:, l, 0:2 * NJ], ps[:, 0, k:k + 2 * NJ], bias1[:, l, 0:2 * NJ], ALU.add)
                k += 2 * NJ
                for r in (0, GT):
                    last = dve.tensor_tensor(bias1[r:r + TAIL, l, 2 * NJ:2 * NJ + 1], ps[r:r + TAIL, 0, k:k + 1],
                                             bias1[r:r + TAIL, l, 2 * NJ:2 * NJ + 1], ALU.add)
            last.then_inc(bias_done, 1)
            for l in range(DEPTH):
                dve.wait_ge(hi_done, 3 * DEPTH + l + 1)
                for (dst, src), (hi, _) in zip(w1_blocks(w1_p[1], st_w1, l), w1_blocks(w1_p[0], st_w1, l)):
                    last = dve.tensor_tensor(dst, src, hi, ALU.subtract)
                last.then_inc(lo_done, 1)
            dve.wait_ge(hi_done, 4 * DEPTH + 1)
            dve.tensor_tensor(bd_p[1][:, :, :, :], bd_f, bd_p[0][:, :, :, :], ALU.subtract).then_inc(lo_done, 1)
            dve.wait_ge(e_done, 1)
            dve.tensor_scalar(c_e, c_e, 1.0, None, ALU.add).then_inc(e1_done, 1)
            dve.wait_ge(e1_done, 1)
            dve.reciprocal(silu, c_e).then_inc(e2_done, 1)
            dve.wait_ge(e2_done, 1)
            dve.tensor_tensor(silu, silu, cT, ALU.mult).then_inc(e3_done, 1)
            dve.wait_ge(row_done, 1)
            dve.tensor_scalar(mrow[:, DIM:2 * DIM], mrow[:, DIM:2 * DIM], 1.0, None, ALU.add)
            dve.tensor_scalar(mrow[:, 4 * DIM:5 * DIM], mrow[:, 4 * DIM:5 * DIM], 1.0, None, ALU.add)
            gates = [mrow[:, k * DIM:(k + 1) * DIM] for k in (2, 5)]
            tmps = [mtmp[:, k * DIM:(k + 1) * DIM] for k in range(2)]
            for g, t in zip(gates, tmps):
                last = dve.tensor_scalar(t, g, 0.0, 2.0, ALU.is_ge, ALU.mult)
            last.then_inc(row_t, 1)
            dve.wait_ge(row_t, 1)
            for g, t in zip(gates, tmps):
                last = dve.tensor_scalar(t, t, -1.0, None, ALU.add)
            last.then_inc(row_t, 1)
            dve.wait_ge(row_t, 2)
            for g, t in zip(gates, tmps):
                last = dve.tensor_tensor(g, g, t, ALU.mult)
            last.then_inc(row_t, 1)
            dve.wait_ge(row_t, 3)
            for g, t in zip(gates, tmps):
                last = dve.scalar_tensor_tensor(out=g, in0=g, scalar=0.25, in1=t, op0=ALU.max, op1=ALU.mult)
            last.then_inc(mod_done, 1)
            dve.wait_ge(z_id2, 1)
            dve.tensor_copy(id_b[:, :], id_f[:, :])
            dve.wait_ge(z_mask2, 3)
            dve.tensor_copy(mask_t[:, :, :], m_f).then_inc(mask_used, 1)
            dve.wait_ge(l_xp, 16)
            for l in range(DEPTH):
                dve.tensor_tensor(xp_t[:, l].rearrange("p t k d -> p t (k d)"), xp_base.rearrange("p t k d -> p t (k d)"),
                                  qks[:, l].rearrange("p k d -> p (k d)").unsqueeze(1).broadcast_to((P, NT, 4 * DH)),
                                  ALU.mult).then_inc(xp_done, 1)

        @block.gpsimd
        def _(pool):
            pool.memset(id_f[:, :], 0.0).then_inc(z_id, 1)
            pool.wait_ge(z_id, 1)
            pool.affine_select(out=id_f[:, :], in_=id_f[:, :], compare_op=ALU.not_equal, fill=1.0, base=0,
                               pattern=[[-1, P]], channel_multiplier=1).then_inc(z_id2, 1)
            pool.wait_ge(l_rep, 16 * 3 * HPC)
            pool.wait_ge(lo_done, 2)
            for c in range(NC):
                for s in range(3):
                    last = pool.affine_select(out=bd_f[:, c, s, :].rearrange("p (d h) -> p d h", h=HPC),
                                              in_=w_rep[:, s, :].rearrange("p (d h) -> p d h", h=AH)[:, :, c * HPC:(c + 1) * HPC],
                                              compare_op=ALU.is_ge, fill=0.0, base=0,
                                              pattern=[[0, AD], [-AD, HPC]], channel_multiplier=1)
            last.then_inc(bd_a, 1)
            pool.wait_ge(bd_a, 1)
            for c in range(NC):
                for s in range(3):
                    t = bd_f[:, c, s, :].rearrange("p (d h) -> p d h", h=HPC)
                    last = pool.affine_select(out=t, in_=t, compare_op=ALU.is_ge, fill=0.0, base=AD - 1,
                                              pattern=[[0, AD], [AD, HPC]], channel_multiplier=-1)
            last.then_inc(bd_b, 1)
            pool.wait_ge(lo_done, 2 + DEPTH)
            pool.memset(m_f, 0.0).then_inc(z_mask, 1)
            pool.wait_ge(z_mask, 1)
            m4 = m_f.rearrange("p a (i k n) -> p a i k n", i=2, k=2)
            pool.affine_select(out=m4[:, 0, :, 0, :], in_=m4[:, 0, :, 0, :], compare_op=ALU.is_ge, fill=NEG, base=0,
                               pattern=[[0, 2], [1, P]], channel_multiplier=-1).then_inc(z_mask2, 1)
            pool.memset(m4[:, 1, :, 0, :], NEG).then_inc(z_mask2, 1)
            for a in range(2):
                last = pool.affine_select(out=m4[:, a, :, 1, :], in_=m4[:, a, :, 1, :], compare_op=ALU.is_ge, fill=NEG,
                                          base=0, pattern=[[0, 2], [-1, P]], channel_multiplier=1)
            last.then_inc(z_mask2, 1)

        @block.tensor
        def _(pe):
            pe.wait_ge(l_w1, 16 * DEPTH)
            pe.wait_ge(l_small, 16 * N_SMALL)
            for l in range(DEPTH):
                for j in range(NB1 + 1):
                    if j < 2 * NJ:
                        a, r, m = (HID, 0)[j % 2] + (j // 2) * P, 0, P
                    else:
                        a, r, m = ((0, HID)[j - 2 * NJ] + NJ * P, (0, GT)[j - 2 * NJ], TAIL)
                    k = l * NB1 + min(j, 2 * NJ)
                    for c in range(NC):
                        last = pe.matmul(ps[r:r + m, 0, k:k + 1], st_w1[l][:, c, a:a + m], lgb[:, 1, l, c:c + 1],
                                         start=(c == 0), stop=(c == NC - 1))
            last.then_inc(lbw, 1)
            pe.wait_ge(e3_done, 1)
            pe.wait_ge(l_mod, 16)
            for j in range(3):
                for c in range(NC):
                    last = pe.matmul(ps[0:BATCH, 4 + j, :], silu[:, c, :], w_mod[:, c, j * 512:(j + 1) * 512],
                                     start=(c == 0), stop=(c == NC - 1))
            last.then_inc(mm_done, 1)


def w1_blocks(dst, stage, l):
    for i, base in enumerate((HID, 0)):
        for c in range(NC):
            yield (dst[:, l, c, i:2 * NJ:2, :],
                   stage[l][:, c, base:base + NJ * P].rearrange("p (j n) -> p j n", n=P))
        r = (GT, 0)[i]
        yield dst[:, l, :, 2 * NJ, r:r + TAIL], stage[l][:, :, base + NJ * P:base + HID]


N_SMALL = 2 * DEPTH + NC + 4 * DEPTH + 6 * DEPTH


def shape_tables():
    import numpy as np

    f = np.float32
    half = DIM // 2
    inv = f(1.0) / (f(10000.0) ** (np.arange(half, dtype=f) / f(half)))
    ang = np.arange(SEQ, dtype=f)[:, None] * inv[None, :]

    def lay(a):
        return np.ascontiguousarray(a.reshape(NT, P, AD, NC, HPC // 2).transpose(1, 0, 3, 2, 4).reshape(P, NT, NC, P // 2))

    idx = np.arange(0, DH, 2, dtype=f)
    inv2 = f(1.0) / (f(10000.0) ** (idx / f(DH)))
    t = np.arange(SEQ, dtype=f)
    fr = t[:, None] * inv2[None, :]
    fr = np.concatenate([fr, fr], -1)
    base = (idx + f(0.4 * DH)) / f(1.4 * DH)
    power = (t - f(SEQ // 2)) / f(64.0)
    sc = base[None, :] ** power[:, None]
    sc = np.concatenate([sc, sc], -1)
    cos, sin = np.cos(fr), np.sin(fr)
    sin[:, :DH // 2] *= f(-1.0)
    qk_scale = f(8.0)
    tab = np.stack([cos * sc * qk_scale, cos / sc, sin * sc * qk_scale, sin / sc], 1).astype(f)
    xpos = np.ascontiguousarray(tab.reshape(NT, P, 4, DH).transpose(1, 0, 2, 3))
    return lay(np.cos(ang).astype(f)), lay(np.sin(ang).astype(f)), xpos


_INS = ['L0_attn_x', 'L0_attn_w_q', 'L0_attn_w_k', 'L0_attn_w_v', 'L0_ffn_wqkv', 'L0_ffn_q_scale', 'L0_ffn_k_scale',
        'L0_ffn_wo', 'L0_ffn_ln_g', 'L0_ffn_ln_b', 'L0_ffn_w1', 'L0_ffn_b1', 'L0_ffn_w2', 'L0_ffn_b2', 'L0_c', 'L0_wmod']


def kernel(**inputs):
    import numpy as _np
    import concourse.bacc as _bacc
    from concourse import mybir as _mybir
    from concourse.bass_utils import run_bass_kernel_spmd as _run

    nc = _bacc.Bacc("TRN2", target_bir_lowering=False, num_devices=1)
    arrays, args = {}, []
    tables = dict(zip(("rope_cos", "rope_sin", "xpos"), shape_tables()))
    for name in _INS + list(tables):
        a = _np.ascontiguousarray(inputs[name] if name in inputs else tables[name])
        arrays[f"in_{name}_dram"] = a
        args.append(nc.dram_tensor(f"in_{name}_dram", a.shape, _mybir.dt.from_np(a.dtype), kind="ExternalInput").ap())
    out = nc.dram_tensor("out_0_dram", (BATCH, SEQ, DIM), F32, kind="ExternalOutput").ap()
    adaln_kernel(nc, *args, out)
    r = _run(nc, [arrays], core_ids=[0])
    return r.results[0]["out_0_dram"]
```
